# Optimizing a Trainium2 kernel written in Bass

```python
import numpy as np
import jax
import jax.numpy as jnp

def _softmax(x, axis=-1):
    return jax.nn.softmax(x, axis=axis)

def _gelu(x):
    return jax.nn.gelu(x, approximate=True)

def _silu(x):
    return jax.nn.silu(x)

def _sigmoid(x):
    return jax.nn.sigmoid(x)

def _layernorm(x, axis=-1, eps=1e-05):
    m = jnp.mean(x, axis=axis, keepdims=True)
    v = jnp.var(x, axis=axis, keepdims=True)
    return (x - m) / jnp.sqrt(v + eps)

def _scatter_add(tgt, idx, src, axis=0):
    return tgt.at[idx].add(src)

def _segment_sum(src, seg, n):
    return jax.ops.segment_sum(src, seg, n)
kernel_name = 'mk_sandwich_d1_jaxref_r8_a1d1c3'

def setup_inputs(seed: int=0):
    np.random.seed(seed)
    _w = jnp.asarray

    def _L0_attn_setup():
        import jax, jax.numpy as jnp
        import numpy as np
        D_MODEL = 128
        N_HEADS = 16
        N_GROUPS = 4
        D_HEAD = D_MODEL // N_HEADS
        HPG = N_HEADS // N_GROUPS
        B, T = (2, 256)

        def _rope(x):
            t, d = (x.shape[2], x.shape[3])
            pos = jnp.arange(t, dtype=jnp.float32)[:, None]
            freq = jnp.exp(-(jnp.arange(0, d, 2, dtype=jnp.float32) / d) * jnp.log(jnp.float32(10000.0)))
            angle = pos * freq
            cos, sin = (jnp.cos(angle), jnp.sin(angle))
            xe, xo = (x[..., ::2], x[..., 1::2])
            re = xe * cos - xo * sin
            ro = xe * sin + xo * cos
            return jnp.stack([re, ro], axis=-1).reshape(x.shape)
        key = jax.random.key(seed)
        ks = jax.random.split(key, 10)
        s = 0.02
        return {'x': jax.random.normal(ks[0], (B, T, D_MODEL), dtype=jnp.float32), 'Wq': jax.random.normal(ks[1], (D_MODEL, D_MODEL), dtype=jnp.float32) * s, 'bq': jax.random.normal(ks[2], (D_MODEL,), dtype=jnp.float32) * s, 'Wk': jax.random.normal(ks[3], (D_MODEL, N_GROUPS * D_HEAD), dtype=jnp.float32) * s, 'bk': jax.random.normal(ks[4], (N_GROUPS * D_HEAD,), dtype=jnp.float32) * s, 'Wv': jax.random.normal(ks[5], (D_MODEL, N_GROUPS * D_HEAD), dtype=jnp.float32) * s, 'bv': jax.random.normal(ks[6], (N_GROUPS * D_HEAD,), dtype=jnp.float32) * s, 'Wo': jax.random.normal(ks[7], (D_MODEL, D_MODEL), dtype=jnp.float32) * s, 'bo': jax.random.normal(ks[8], (D_MODEL,), dtype=jnp.float32) * s}
    _L0_attn_in = _L0_attn_setup()

    def _L0_ffn_setup():
        import jax, jax.numpy as jnp
        import numpy as np
        DIM = 128
        DEPTH = 2
        HEADS = 8
        DIM_HEAD = 64
        WINDOW = 64
        INNER = HEADS * DIM_HEAD
        HID = int(DIM * 4 * 2 / 3)
        B, N = (2, 1024)
        QK_SCALE = 8.0

        def shift_token(t):
            t1, t2 = jnp.split(t, 2, axis=-1)
            t2 = jnp.pad(t2, ((0, 0), (1, 0), (0, 0)))[:, :-1]
            return jnp.concatenate([t1, t2], axis=-1)

        def l2norm(t):
            return t / jnp.clip(jnp.linalg.norm(t, axis=-1, keepdims=True), 1e-12)

        def rotate_half(x):
            x1, x2 = jnp.split(x, 2, axis=-1)
            return jnp.concatenate([-x2, x1], axis=-1)

        def rotary_xpos(q, k):
            n = q.shape[-2]
            half_idx = jnp.arange(0, DIM_HEAD, 2, dtype=jnp.float32)
            inv_freq = 1.0 / 10000.0 ** (half_idx / DIM_HEAD)
            t = jnp.arange(n, dtype=jnp.float32)
            freqs = t[:, None] * inv_freq[None, :]
            freqs = jnp.concatenate([freqs, freqs], axis=-1)
            base = (half_idx + 0.4 * DIM_HEAD) / (1.4 * DIM_HEAD)
            power = (t - n // 2) / float(WINDOW // 2)
            scale = base[None, :] ** power[:, None]
            scale = jnp.concatenate([scale, scale], axis=-1)
            cos, sin = (jnp.cos(freqs), jnp.sin(freqs))
            q = q * cos * scale + rotate_half(q) * sin * scale
            k = k * cos / scale + rotate_half(k) * sin / scale
            return (q, k)

        def local_attention(q, k, v):
            b, h, n, d = q.shape
            w = n // WINDOW
            bq = q.reshape(b, h, w, WINDOW, d) * QK_SCALE
            bk = k.reshape(b, h, w, WINDOW, d)
            bv = v.reshape(b, h, w, WINDOW, d)

            def look_around(t):
                p = jnp.pad(t, ((0, 0), (0, 0), (1, 0), (0, 0), (0, 0)))
                return jnp.concatenate([p[:, :, :w], p[:, :, 1:]], axis=3)
            bk, bv = (look_around(bk), look_around(bv))
            bt = jnp.arange(n).reshape(w, WINDOW)
            btp = jnp.pad(bt, ((1, 0), (0, 0)), constant_values=-1)
            btk = jnp.concatenate([btp[:w], btp[1:]], axis=1)
            sim = jnp.einsum('bhwid,bhwjd->bhwij', bq, bk)
            i = bt[:, :, None]
            j = btk[:, None, :]
            mask = (i < j) | (i > j + WINDOW) | (j == -1)
            sim = jnp.where(mask, -jnp.finfo(sim.dtype).max, sim)
            attn = jax.nn.softmax(sim, axis=-1)
            out = jnp.einsum('bhwij,bhwjd->bhwid', attn, bv)
            return out.reshape(b, h, n, d)

        def _layer(x, wqkv, qs, ksc, wo, lg, lb, w1, b1, w2, b2):
            b, n, _ = x.shape
            h = shift_token(x)
            qkv = h @ wqkv
            q, k, v = jnp.split(qkv, 3, axis=-1)
            to_heads = lambda t: t.reshape(b, n, HEADS, DIM_HEAD).transpose(0, 2, 1, 3)
            q, k, v = (to_heads(q), to_heads(k), to_heads(v))
            q = l2norm(q) * qs
            k = l2norm(k) * ksc
            q, k = rotary_xpos(q, k)
            o = local_attention(q, k, v)
            o = o.transpose(0, 2, 1, 3).reshape(b, n, INNER)
            x = x + o @ wo
            h = shift_token(x)
            mu = h.mean(-1, keepdims=True)
            var = h.var(-1, keepdims=True)
            h = (h - mu) / jnp.sqrt(var + 1e-05) * lg + lb
            h = h @ w1 + b1
            a, g = jnp.split(h, 2, axis=-1)
            h = a * jax.nn.gelu(g, approximate=False)
            x = x + h @ w2 + b2
            return x
        key = jax.random.key(seed)
        ks = jax.random.split(key, 6)
        return {'x': jax.random.normal(ks[0], (B, N, DIM), jnp.float32), 'wqkv': jax.random.normal(ks[1], (DEPTH, DIM, 3 * INNER), jnp.float32) * 0.02, 'q_scale': jnp.ones((DEPTH, DIM_HEAD), jnp.float32), 'k_scale': jnp.ones((DEPTH, DIM_HEAD), jnp.float32), 'wo': jax.random.normal(ks[2], (DEPTH, INNER, DIM), jnp.float32) * 0.02, 'ln_g': jnp.ones((DEPTH, DIM), jnp.float32), 'ln_b': jnp.zeros((DEPTH, DIM), jnp.float32), 'w1': jax.random.normal(ks[3], (DEPTH, DIM, 2 * HID), jnp.float32) * 0.02, 'b1': jnp.zeros((DEPTH, 2 * HID), jnp.float32), 'w2': jax.random.normal(ks[4], (DEPTH, HID, DIM), jnp.float32) * 0.02, 'b2': jnp.zeros((DEPTH, DIM), jnp.float32)}
    _L0_ffn_in = _L0_ffn_setup()
    _d = {'L0_attn_x': _L0_attn_in['x'], 'L0_attn_Wq': _L0_attn_in['Wq'], 'L0_attn_bq': _L0_attn_in['bq'], 'L0_attn_Wk': _L0_attn_in['Wk'], 'L0_attn_bk': _L0_attn_in['bk'], 'L0_attn_Wv': _L0_attn_in['Wv'], 'L0_attn_bv': _L0_attn_in['bv'], 'L0_attn_Wo': _L0_attn_in['Wo'], 'L0_attn_bo': _L0_attn_in['bo'], 'L0_ffn_wqkv': _L0_ffn_in['wqkv'], 'L0_ffn_q_scale': _L0_ffn_in['q_scale'], 'L0_ffn_k_scale': _L0_ffn_in['k_scale'], 'L0_ffn_wo': _L0_ffn_in['wo'], 'L0_ffn_ln_g': _L0_ffn_in['ln_g'], 'L0_ffn_ln_b': _L0_ffn_in['ln_b'], 'L0_ffn_w1': _L0_ffn_in['w1'], 'L0_ffn_b1': _L0_ffn_in['b1'], 'L0_ffn_w2': _L0_ffn_in['w2'], 'L0_ffn_b2': _L0_ffn_in['b2']}
    _x0 = _d['L0_attn_x']
    _d['L0_attn_x'] = jax.random.normal(jax.random.fold_in(jax.random.key(seed), 1), (16, 512, 128), dtype=_x0.dtype)
    del _x0
    return _d

def reference(L0_attn_x, L0_attn_Wq, L0_attn_bq, L0_attn_Wk, L0_attn_bk, L0_attn_Wv, L0_attn_bv, L0_attn_Wo, L0_attn_bo, L0_ffn_wqkv, L0_ffn_q_scale, L0_ffn_k_scale, L0_ffn_wo, L0_ffn_ln_g, L0_ffn_ln_b, L0_ffn_w1, L0_ffn_b1, L0_ffn_w2, L0_ffn_b2):

    def _L0_attn_ref(x, Wq, bq, Wk, bk, Wv, bv, Wo, bo):
        import jax, jax.numpy as jnp
        import numpy as np
        D_MODEL = 128
        N_HEADS = 16
        N_GROUPS = 4
        D_HEAD = D_MODEL // N_HEADS
        HPG = N_HEADS // N_GROUPS
        B, T = (2, 256)

        def _rope(x):
            t, d = (x.shape[2], x.shape[3])
            pos = jnp.arange(t, dtype=jnp.float32)[:, None]
            freq = jnp.exp(-(jnp.arange(0, d, 2, dtype=jnp.float32) / d) * jnp.log(jnp.float32(10000.0)))
            angle = pos * freq
            cos, sin = (jnp.cos(angle), jnp.sin(angle))
            xe, xo = (x[..., ::2], x[..., 1::2])
            re = xe * cos - xo * sin
            ro = xe * sin + xo * cos
            return jnp.stack([re, ro], axis=-1).reshape(x.shape)
        b, t, _ = x.shape
        q = (x @ Wq + bq).reshape(b, t, N_HEADS, D_HEAD).transpose(0, 2, 1, 3)
        k = (x @ Wk + bk).reshape(b, t, N_GROUPS, D_HEAD).transpose(0, 2, 1, 3)
        v = (x @ Wv + bv).reshape(b, t, N_GROUPS, D_HEAD).transpose(0, 2, 1, 3)
        k = jnp.repeat(k, HPG, axis=1)
        v = jnp.repeat(v, HPG, axis=1)
        q = _rope(q)
        k = _rope(k)
        scale = jnp.float32(np.sqrt(D_HEAD))
        scores = jnp.einsum('bhtd,bhsd->bhts', q, k) / scale
        causal = jnp.tril(jnp.ones((t, t), dtype=bool))
        scores = jnp.where(causal, scores, -jnp.inf)
        probs = jax.nn.softmax(scores, axis=-1)
        attn = jnp.einsum('bhts,bhsd->bhtd', probs, v)
        out = attn.transpose(0, 2, 1, 3).reshape(b, t, N_HEADS * D_HEAD)
        return out @ Wo + bo

    def _L0_ffn_ref(x, wqkv, q_scale, k_scale, wo, ln_g, ln_b, w1, b1, w2, b2):
        import jax, jax.numpy as jnp
        import numpy as np
        DIM = 128
        DEPTH = 2
        HEADS = 8
        DIM_HEAD = 64
        WINDOW = 64
        INNER = HEADS * DIM_HEAD
        HID = int(DIM * 4 * 2 / 3)
        B, N = (2, 1024)
        QK_SCALE = 8.0

        def shift_token(t):
            t1, t2 = jnp.split(t, 2, axis=-1)
            t2 = jnp.pad(t2, ((0, 0), (1, 0), (0, 0)))[:, :-1]
            return jnp.concatenate([t1, t2], axis=-1)

        def l2norm(t):
            return t / jnp.clip(jnp.linalg.norm(t, axis=-1, keepdims=True), 1e-12)

        def rotate_half(x):
            x1, x2 = jnp.split(x, 2, axis=-1)
            return jnp.concatenate([-x2, x1], axis=-1)

        def rotary_xpos(q, k):
            n = q.shape[-2]
            half_idx = jnp.arange(0, DIM_HEAD, 2, dtype=jnp.float32)
            inv_freq = 1.0 / 10000.0 ** (half_idx / DIM_HEAD)
            t = jnp.arange(n, dtype=jnp.float32)
            freqs = t[:, None] * inv_freq[None, :]
            freqs = jnp.concatenate([freqs, freqs], axis=-1)
            base = (half_idx + 0.4 * DIM_HEAD) / (1.4 * DIM_HEAD)
            power = (t - n // 2) / float(WINDOW // 2)
            scale = base[None, :] ** power[:, None]
            scale = jnp.concatenate([scale, scale], axis=-1)
            cos, sin = (jnp.cos(freqs), jnp.sin(freqs))
            q = q * cos * scale + rotate_half(q) * sin * scale
            k = k * cos / scale + rotate_half(k) * sin / scale
            return (q, k)

        def local_attention(q, k, v):
            b, h, n, d = q.shape
            w = n // WINDOW
            bq = q.reshape(b, h, w, WINDOW, d) * QK_SCALE
            bk = k.reshape(b, h, w, WINDOW, d)
            bv = v.reshape(b, h, w, WINDOW, d)

            def look_around(t):
                p = jnp.pad(t, ((0, 0), (0, 0), (1, 0), (0, 0), (0, 0)))
                return jnp.concatenate([p[:, :, :w], p[:, :, 1:]], axis=3)
            bk, bv = (look_around(bk), look_around(bv))
            bt = jnp.arange(n).reshape(w, WINDOW)
            btp = jnp.pad(bt, ((1, 0), (0, 0)), constant_values=-1)
            btk = jnp.concatenate([btp[:w], btp[1:]], axis=1)
            sim = jnp.einsum('bhwid,bhwjd->bhwij', bq, bk)
            i = bt[:, :, None]
            j = btk[:, None, :]
            mask = (i < j) | (i > j + WINDOW) | (j == -1)
            sim = jnp.where(mask, -jnp.finfo(sim.dtype).max, sim)
            attn = jax.nn.softmax(sim, axis=-1)
            out = jnp.einsum('bhwij,bhwjd->bhwid', attn, bv)
            return out.reshape(b, h, n, d)

        def _layer(x, wqkv, qs, ksc, wo, lg, lb, w1, b1, w2, b2):
            b, n, _ = x.shape
            h = shift_token(x)
            qkv = h @ wqkv
            q, k, v = jnp.split(qkv, 3, axis=-1)
            to_heads = lambda t: t.reshape(b, n, HEADS, DIM_HEAD).transpose(0, 2, 1, 3)
            q, k, v = (to_heads(q), to_heads(k), to_heads(v))
            q = l2norm(q) * qs
            k = l2norm(k) * ksc
            q, k = rotary_xpos(q, k)
            o = local_attention(q, k, v)
            o = o.transpose(0, 2, 1, 3).reshape(b, n, INNER)
            x = x + o @ wo
            h = shift_token(x)
            mu = h.mean(-1, keepdims=True)
            var = h.var(-1, keepdims=True)
            h = (h - mu) / jnp.sqrt(var + 1e-05) * lg + lb
            h = h @ w1 + b1
            a, g = jnp.split(h, 2, axis=-1)
            h = a * jax.nn.gelu(g, approximate=False)
            x = x + h @ w2 + b2
            return x
        for l in range(DEPTH):
            x = _layer(x, wqkv[l], q_scale[l], k_scale[l], wo[l], ln_g[l], ln_b[l], w1[l], b1[l], w2[l], b2[l])
        return x
    x = L0_attn_x
    x = x + _layernorm(_L0_attn_ref(_layernorm(x, axis=-1), L0_attn_Wq, L0_attn_bq, L0_attn_Wk, L0_attn_bk, L0_attn_Wv, L0_attn_bv, L0_attn_Wo, L0_attn_bo), axis=-1)
    x = x + _layernorm(_L0_ffn_ref(_layernorm(x, axis=-1), L0_ffn_wqkv, L0_ffn_q_scale, L0_ffn_k_scale, L0_ffn_wo, L0_ffn_ln_g, L0_ffn_ln_b, L0_ffn_w1, L0_ffn_b1, L0_ffn_w2, L0_ffn_b2), axis=-1)
    return x

_drawn_inputs = setup_inputs


def setup_inputs(seed=0):
    import zlib

    import numpy as np

    out = dict(_drawn_inputs(seed))
    spreads = {'L0_ffn_q_scale': (1.0, 0.6),
     'L0_ffn_k_scale': (1.0, 0.6),
     'L0_ffn_ln_g': (1.0, 0.6),
     'L0_ffn_ln_b': (0.0, 0.8),
     'L0_ffn_b1': (0.0, 0.8),
     'L0_ffn_b2': (0.0, 0.8)}
    factors = {'L0_attn_Wq': 6.059,
     'L0_attn_bq': 8.0,
     'L0_attn_Wk': 5.969,
     'L0_attn_bk': 8.0,
     'L0_ffn_w1': 7.44,
     'L0_ffn_w2': 7.247}
    for name, (base, spread) in spreads.items():
        noise = np.random.default_rng([zlib.crc32(name.encode()), seed]).standard_normal(out[name].shape)
        drawn = base * np.exp(spread * noise) if base else spread * noise
        out[name] = jnp.asarray(drawn.astype(out[name].dtype))
    for name, factor in factors.items():
        out[name] = (out[name] * factor).astype(out[name].dtype)
    return out
```

```python
from contextlib import ExitStack

import numpy as np
import concourse.bass as bass
from concourse import mybir

F32 = mybir.dt.float32
F32R = mybir.dt.float32r
BF16 = mybir.dt.bfloat16
I32 = mybir.dt.int32
ALU = mybir.AluOpType
ACT = mybir.ActivationFunctionType
AX = mybir.AxisListType.X

P = 128
B, T, D = 16, 512, 128
TT = T // P
EPS = 1e-5
MASKED = -1e30
RSQRT_SEED = 0x5F3759DF

H1, G1, DH1 = 16, 4, 8
J1 = H1 // G1
QK1 = H1 * DH1 + G1 * DH1
QKV1 = QK1 + G1 * DH1
ROWS = P // G1
NEG_MAX = 3 * DH1
SCALE1 = 1.0 / float(np.sqrt(np.float32(DH1)))

CHUNKS = [(3, [g]) for g in range(G1)] + [(2, [g]) for g in range(G1)] + [(1, [0, 1]), (1, [2, 3]), (0, [0, 1, 2, 3])]
NCH = len(CHUNKS)
UNITS = []
for _gp in range(G1 // 2):
    for _g in (2 * _gp, 2 * _gp + 1):
        UNITS += [[(_g, 0, 0)], [(_g, 1, 0), (_g, 3, 384)]]
    UNITS += [[(2 * _gp, 2, 0), (2 * _gp + 1, 2, 256)]]
NU = len(UNITS)
PLACE = {(g, s): (n, c) for n, un in enumerate(UNITS) for g, s, c in un}
UNIT_BANK = [0, 1, 2, 0, 1, 2, 0, 1, 2, 1]
UNIT_BACK = [next(d for d in range(1, NU + 1) if UNIT_BANK[(n - d) % NU] == UNIT_BANK[n]) for n in range(NU)]


def rope_tables():
    d = np.arange(0, DH1, 2, dtype=np.float32) / np.float32(DH1)
    freq = np.exp(-d * np.log(np.float32(10000.0))).astype(np.float32)
    angle = (np.arange(T, dtype=np.float32)[:, None] * freq).astype(np.float32).astype(np.float64)
    cos = np.repeat(np.cos(angle), 2, axis=1)
    sin = np.repeat(np.sin(angle), 2, axis=1) * np.tile([-1.0, 1.0], DH1 // 2)
    lay = lambda a: np.tile(a, (1, QK1 // DH1)).reshape(TT, P, QK1).transpose(1, 0, 2).astype(np.float32)
    return np.ascontiguousarray(lay(cos)), np.ascontiguousarray(lay(sin))


class Tally:

    def __init__(self, parts):
        self.parts = parts
        self.base, self.k = 0, 0

    def body(self, b):
        p1, p2, p3 = self.parts
        self.base = p1 if isinstance(b, int) and b == 0 else b * (p1 + p2 + p3) + (p1 - p3)
        self.k = 0

    def epilogue(self):
        p1, p2, p3 = self.parts
        self.base, self.k = B * (p1 + p2 + p3) - p3, 0

    def check(self, want):
        assert self.k == want, (self.k, want, self.parts)

    def next(self):
        self.k += 1
        return self.base + (self.k - 1)


def skewed(eng, tallies, prologue, body, epilogue):
    prologue()
    for t in tallies:
        t.check(t.parts[0])

    def one(b, slot, first=False, last=False):
        for t in tallies:
            t.body(b)
        body(b, slot, first, last)
        for t in tallies:
            t.check(sum(t.parts) - (t.parts[2] if first else 0) - (t.parts[0] if last else 0))

    one(0, 0, first=True)
    with eng.Fori(1, B - 2, 2) as b:
        one(b, 1)
        one(b + 1, 0)
    one(B - 1, 1, last=True)
    for t in tallies:
        t.epilogue()
    epilogue()


def sandwich_kernel(nc, x, Wq, bq, Wk, bk, Wv, bv, Wo, bo, wqkv, q_scale, k_scale, wo, ln_g, ln_b, w1, b1, w2, b2,
                    cos1, sin1, tab2, out):
    x_v = x.rearrange("b (i p) d -> p b i d", p=P)
    out_v = out.rearrange("b (i p) d -> p b i d", p=P)

    with ExitStack() as whole:
        def sem(name):
            return whole.enter_context(nc.semaphore(name))

        def resident(name, shape, dt=F32):
            return whole.enter_context(nc.sbuf_tensor(name, shape, dt))

        ident = resident("ident", [P, P])
        ident_bf = resident("ident_bf", [P, P], BF16)
        u = resident("u", [P, B, T])

        x1_dram = nc.dram_tensor("x1_scratch", (B, T, D), F32, kind="Internal").ap()
        x1_v = x1_dram.rearrange("b (i p) d -> p b i d", p=P)

        causal_attention(nc, sem, ident, ident_bf, x1_v, u, x_v, Wq, bq, Wk, bk, Wv, bv, Wo, bo, cos1, sin1)
        local_layers(nc, sem, ident, ident_bf, u, wqkv, q_scale, k_scale, wo, ln_g, ln_b, w1, b1, w2, b2, tab2)
        last_norm(nc, sem, ident, u, x1_v, out_v)


def rsqrt(dve, step, y, v, t):
    step(dve.tensor_scalar(y.bitcast(I32), v.bitcast(I32), 1, None, ALU.logical_shift_right))
    step(dve.tensor_scalar(y.bitcast(I32), y.bitcast(I32), -1.0, float(RSQRT_SEED), ALU.mult, ALU.add))
    for _ in range(3):
        step(dve.tensor_tensor(t, y, y, ALU.mult))
        step(dve.scalar_tensor_tensor(t, t, -0.5, v, ALU.mult, ALU.mult))
        step(dve.scalar_tensor_tensor(y, t, 1.5, y, ALU.add, ALU.mult))


def causal_attention(nc, sem, ident, ident_bf, x1_v, u, x_v, Wq, bq, Wk, bk, Wv, bv, Wo, bo, cos1, sin1):
    with ExitStack() as ctx:
        def sb(name, shape, dt=F32):
            return ctx.enter_context(nc.sbuf_tensor("a_" + name, shape, dt))

        def banks(name, n):
            return ctx.enter_context(nc.psum_tensor("a_" + name, [P, n, 512], F32))

        x1 = sb("x1", [P, B, TT, D])
        wqkv = sb("wqkv", [D, QKV1])
        wo = sb("wo", [D, D])
        bqkv = sb("bqkv", [P, QKV1])
        bo_b = sb("bo", [P, D])
        cos = sb("cos", [P, TT, QK1])
        sin = sb("sin", [P, TT, QK1])
        mask_ts = sb("mask_ts", [P, P], BF16)
        mask_st = sb("mask_st", [P, P], BF16)
        xn = sb("xn", [P, TT, D])
        xT = sb("xT", [D, T])
        qkv = sb("qkv", [P, TT, QKV1])
        turned = sb("turned", [P, TT, QK1])
        crossed = sb("crossed", [P, TT, QK1])
        qpack = sb("qpack", [P, 2, TT, J1, G1, ROWS])
        kpack = sb("kpack", [P, TT, G1, ROWS])
        qT = sb("qT", [P, 2, J1, T], F32R)
        qmT = sb("qmT", [P, 2, T], F32R)
        kT = sb("kT", [P, 2, G1, T], F32R)
        v = sb("v", [P, 2, TT, G1, ROWS])
        probs = sb("probs", [P, 2, NU, 512])
        oT = sb("oT", [P, 2, T])
        rden = sb("rden", [P, TT, G1])
        attn = sb("attn", [P, 2, TT, G1, J1, DH1])
        aT = sb("aT", [D, T])
        z = sb("z", [P, TT, D])
        stats = sb("stats", [P, TT, 6])
        mv = sb("mv", [P, TT, 2])
        var, rstd, tmp = (sb(n, [P, TT]) for n in ("var", "rstd", "tmp"))
        pause = sb("pause", [P, 1])

        s_bank = banks("s", 2)
        st_bank = banks("st", 3)
        o_bank = banks("o", 1)[:, 0]
        act_bank = banks("for_act", 1)[:, 0]
        dve_bank = banks("for_dve", 1)[:, 0]

        (consts_loaded, first_loaded, rest_loaded, consts_made, xn_made, act_bank_filled, act_bank_copied,
         dve_bank_filled, dve_bank_copied, rope_step, high_made, packed, scores_filled, maxed, units_filled,
         probs_made, pv_done, o_copied, attn_made, dve_step, x1_made, x1_stored) = (
            sem("a_" + n) for n in """consts_loaded first_loaded rest_loaded consts_made xn_made act_bank_filled act_bank_copied
            dve_bank_filled dve_bank_copied rope_step high_made packed scores_filled maxed units_filled
            probs_made pv_done o_copied attn_made dve_step x1_made x1_stored""".split())

        LOADS, CONSTS_MADE = 10, 13
        def act_uses():
            return Tally((1 + 1 + 2, J1, 2))
        def dve_uses():
            return Tally((2 + 2, J1 - 1, 2))

        def quads(b, slot, first, last, scores, units, tasks):
            def task(name, *args):
                if name in tasks:
                    tasks[name](*args)

            for j in range(J1):
                after = (b, slot, j + 1) if j < J1 - 1 else (b + 1, 1 - slot, 0)
                before = (b, slot, j - 1) if j else (b - 1, 1 - slot, J1 - 1)
                task("max_turn", b, slot, j)
                for k in range(NCH):
                    if j < J1 - 1 or not last:
                        scores(*after, k)
                    if k < NU:
                        units(b, slot, j, k)
                    if (j or not first) and 1 <= k <= TT:
                        task("pv", *before, k - 1)
                    if (j or not first) and k == 6:
                        task("o_turn", *before)
                    if not last:
                        for at, name, *args in PART1:
                            if at == (j, k):
                                task(name, b + 1, 1 - slot, *args)
                    if not first:
                        for at, name, *args in PART3:
                            if at == (j, k):
                                task(name, b - 1, 1 - slot, *args)

        PART1 = [((0, 0), "norm"), ((0, 3), "x_turn"), ((0, 4), "project", 0), ((0, 6), "project", 1), ((0, 7), "rope"), ((1, 9), "high"),
                 ((2, 4), "k_turn"), ((2, 5), "q_turn", 0), ((2, 6), "q_turn", 1), ((2, 7), "q_turn", 2), ((2, 8), "q_turn", 3)]
        PART3 = [((0, 9), "attn_turn"), ((1, 0), "out_project"), ((1, 8), "u_turn")]

        def prologue(scores, tasks):
            for _, name, *args in PART1:
                if name in tasks:
                    tasks[name](0, 0, *args)
            for c in range(NCH):
                scores(0, 0, 0, c)

        def epilogue(tasks):
            for k in range(TT):
                if "pv" in tasks:
                    tasks["pv"](B - 1, 1, J1 - 1, k)
            if "o_turn" in tasks:
                tasks["o_turn"](B - 1, 1, J1 - 1)
            for _, name, *args in PART3:
                if name in tasks:
                    tasks[name](B - 1, 1, *args)

        def program(eng, tallies, scores, units, tasks):
            skewed(eng, tallies, lambda: prologue(scores, tasks),
                   lambda b, slot, first, last: quads(b, slot, first, last, scores, units, tasks),
                   lambda: epilogue(tasks))

        nothing = lambda *a: None
        block = ctx.enter_context(nc.Block())

        @block.sync
        def _(sp):
            row = lambda a: a.rearrange("(a n) -> a n", a=1)
            sp.dma_start(x1[:, 0], x_v[:, 0]).then_inc(first_loaded, 16)
            for dst, src in [
                    (wqkv[:, 0:128], Wq), (wqkv[:, 128:160], Wk), (wqkv[:, 160:192], Wv), (wo[:], Wo),
                    (bqkv[:, 0:128], row(bq).to_broadcast([P, 128])), (bqkv[:, 128:160], row(bk).to_broadcast([P, 32])),
                    (bqkv[:, 160:192], row(bv).to_broadcast([P, 32])), (bo_b[:], row(bo).to_broadcast([P, D])),
                    (cos[:], cos1), (sin[:], sin1)]:
                sp.dma_start(dst, src).then_inc(consts_loaded, 16)
            sp.dma_start(x1[:, 1:B], x_v[:, 1:B]).then_inc(rest_loaded, 16)
            with sp.Fori(0, B) as b:
                sp.wait_ge(x1_made, b + 1)
                sp.dma_start(x1_v[:, bass.ds(b, 1)], x1[:, bass.ds(b, 1)]).then_inc(x1_stored, 16)
            sp.wait_ge(x1_stored, 16 * B)

        @block.gpsimd
        def _(pool):
            for t, val in [(ident, 0.0), (ident_bf, 0.0), (mask_ts, 0.0), (mask_st, 0.0), (qpack, 0.0), (kpack, 0.0), (v, 1.0)]:
                pool.memset(t[:], val).then_inc(consts_made, 1)
            pool.memset(kT[:].bitcast(F32), 0.0).then_inc(consts_made, 1)
            pool.wait_ge(consts_made, 8)
            for t in (ident, ident_bf):
                pool.affine_select(out=t[:], in_=t[:], compare_op=ALU.not_equal, fill=1.0, base=0,
                                   pattern=[[-1, P]], channel_multiplier=1).then_inc(consts_made, 1)
            pool.affine_select(out=mask_ts[:], in_=mask_ts[:], compare_op=ALU.is_ge, fill=MASKED, base=0,
                               pattern=[[-1, P]], channel_multiplier=1).then_inc(consts_made, 1)
            pool.affine_select(out=mask_st[:], in_=mask_st[:], compare_op=ALU.is_ge, fill=MASKED, base=0,
                               pattern=[[1, P]], channel_multiplier=-1).then_inc(consts_made, 1)
            pool.memset(kpack[:, :, :, NEG_MAX:NEG_MAX + 1], 1.0).then_inc(consts_made, 1)
            pool.wait_ge(consts_loaded, 16 * LOADS)
            dve = dve_uses()

            def project(b, slot, half):
                dve.next()

            def rope(b, slot):
                pool.wait_ge(dve_bank_copied, dve.base + dve.k)
                pool.tensor_tensor(turned[:], qkv[:, :, 0:QK1], cos[:], ALU.mult).then_inc(rope_step, 1)
                pick = lambda a, e: a.rearrange("p i (n e) -> p i n e", e=2)[:, :, :, e]
                for e in range(2):
                    pool.tensor_tensor(pick(crossed[:], e), pick(qkv[:, :, 0:QK1], 1 - e), pick(sin[:], e),
                                       ALU.mult).then_inc(rope_step, 1)
                pool.wait_ge(rope_step, b * 4 + 3)
                pool.tensor_tensor(turned[:], turned[:], crossed[:], ALU.add).then_inc(rope_step, 1)
                for t in range(TT):
                    last = pool.tensor_copy(v[:, slot, t, :, 0:DH1], qkv[:, t, QK1:QKV1].rearrange("p (g d) -> p g d", g=G1))

            def high(b, slot):
                pool.wait_ge(high_made, (b + 1) * 5)
                for t in range(TT):
                    q = turned[:, t, 0:128].rearrange("p (g j d) -> p j g d", g=G1, j=J1)
                    pool.tensor_tensor(qpack[:, slot, t, :, :, 8:16], q, qpack[:, slot, t, :, :, 0:8], ALU.subtract)
                    pool.tensor_copy(qpack[:, slot, t, :, :, 16:24], qpack[:, slot, t, :, :, 0:8])
                k = turned[:, :, 128:160].rearrange("p i (g d) -> p i g d", g=G1)
                pool.tensor_copy(kpack[:, :, :, 8:16], kpack[:, :, :, 0:8])
                pool.tensor_tensor(kpack[:, :, :, 16:24], k, kpack[:, :, :, 0:8], ALU.subtract).then_inc(packed, 1)

            program(pool, [dve], nothing, nothing, dict(
                project=project, rope=rope, high=high, q_turn=lambda b, s, j: j % 2 and dve.next(),
                o_turn=lambda *a: dve.next(), out_project=lambda *a: dve.next()))

        @block.scalar
        def _(act):
            uses = act_uses()

            def copy_out(dst, src):
                n = uses.next()
                act.wait_ge(act_bank_filled, n + 1)
                act.copy(dst, src).then_inc(act_bank_copied, 1)

            def k_turn(b, slot):
                n = uses.next()
                act.wait_ge(act_bank_filled, n + 1)
                for g in range(G1):
                    r = slice(ROWS * g, ROWS * g + ROWS)
                    last = act.copy(kT[r, slot, g, :], act_bank[r, :])
                last.then_inc(act_bank_copied, 1)

            def units(b, slot, j, k):
                n = (b * J1 + j) * NU + k
                act.wait_ge(units_filled, n + 1)
                act.activation(probs[:, j % 2, k, :], st_bank[:, UNIT_BANK[k], :], ACT.Exp, scale=SCALE1).then_inc(probs_made, 1)

            def o_turn(b, slot, j):
                act.wait_ge(pv_done, b * J1 + j + 1)
                act.copy(oT[:, j % 2, :], o_bank).then_inc(o_copied, 1)

            def u_turn(b, slot):
                n = uses.next()
                act.wait_ge(act_bank_filled, n + 1)
                act.copy(u[:, bass.ds(b, 1), :].rearrange("p a t -> p (a t)"), act_bank).then_inc(act_bank_copied, 1)

            act.wait_ge(consts_made, CONSTS_MADE)
            program(act, [uses], nothing, units, dict(
                max_turn=lambda b, slot, j: copy_out(qmT[:, j % 2, :], act_bank),
                x_turn=lambda b, slot: copy_out(xT[:], act_bank), k_turn=k_turn,
                q_turn=lambda b, slot, j: j % 2 or copy_out(qT[:, slot, j, :], act_bank),
                o_turn=o_turn, attn_turn=lambda b, slot: copy_out(aT[:], act_bank), u_turn=u_turn))

        @block.vector
        def _(dve):
            uses, steps = dve_uses(), Tally((NORM, J1 - 1, 2 * NORM + 4))

            def step(instruction, then_stats=False):
                n = steps.next()
                instruction.then_inc(dve_step, 1)
                dve.wait_ge(dve_step, n + 1)
                if then_stats:
                    dve.memset(pause[:], 0.0)

            def norm_stats(src):
                for t in range(TT):
                    last = dve.bn_stats(stats[:, t, :], src(t))
                step(last, then_stats=True)
                for t in range(TT):
                    last = dve.bn_aggr(mv[:, t, :], stats[:, t, :])
                step(last)
                step(dve.tensor_scalar(var[:], mv[:, :, 1], EPS, None, ALU.add))
                rsqrt(dve, step, rstd[:], var[:], tmp[:])

            def normed(dst, src, whole=None):
                for t in range(TT):
                    last = dve.tensor_scalar(dst(t), src(t), mv[:, t, 0:1], rstd[:, t:t + 1], ALU.subtract, ALU.mult)
                    if whole and not t:
                        last.then_inc(whole, 1)
                return last

            def tokens(b):
                return lambda t: x1[:, bass.ds(b, 1), t, :].rearrange("p a d -> p (a d)")

            def norm(b, slot):
                if isinstance(b, int):
                    dve.wait_ge(first_loaded if b == 0 else rest_loaded, 16)
                norm_stats(tokens(b))
                normed(lambda t: xn[:, t, :], tokens(b)).then_inc(xn_made, 1)

            def project(b, slot, half):
                n = uses.next()
                dve.wait_ge(dve_bank_filled, n + 1)
                for t in range(2):
                    last = dve.tensor_tensor(qkv[:, 2 * half + t, :], dve_bank[:, t * QKV1:(t + 1) * QKV1], bqkv[:], ALU.add)
                last.then_inc(dve_bank_copied, 1)

            def high(b, slot):
                dve.wait_ge(rope_step, b * 4 + 4)
                for t in range(TT):
                    dve.tensor_copy(qpack[:, slot, t, :, :, 0:8].bitcast(F32R),
                                    turned[:, t, 0:128].rearrange("p (g j d) -> p j g d", g=G1, j=J1)).then_inc(high_made, 1)
                dve.tensor_copy(kpack[:, :, :, 0:8].bitcast(F32R),
                                turned[:, :, 128:160].rearrange("p i (g d) -> p i g d", g=G1)).then_inc(high_made, 1)

            def q_turn(b, slot, j):
                if j % 2:
                    n = uses.next()
                    dve.wait_ge(dve_bank_filled, n + 1)
                    dve.tensor_copy(qT[:, slot, j, :], dve_bank).then_inc(dve_bank_copied, 1)

            def scores(b, slot, j, c):
                i, gs = CHUNKS[c]
                n = (b * J1 + j) * NCH + c
                dve.wait_ge(scores_filled, n + 1)
                w = (i + 1) * P
                dve.tensor_reduce(qpack[:, slot, i, j, gs[0]:gs[-1] + 1, NEG_MAX],
                                  s_bank[:, (j * NCH + c) % 2, 0:w * len(gs)].rearrange("p (g s) -> p g s", g=len(gs)),
                                  AX, ALU.max, negate=True).then_inc(maxed, 1)

            def o_turn(b, slot, j):
                n = uses.next()
                dve.wait_ge(dve_bank_filled, n + 1)
                o = dve_bank.rearrange("p (i g d) -> p i g d", i=TT, g=G1)
                step(dve.reciprocal(rden[:], o[:, :, :, DH1]))
                for t in range(TT):
                    last = dve.tensor_tensor(attn[:, slot, t, :, j, :], o[:, t, :, 0:DH1],
                                             rden[:, t, :].rearrange("p (g a) -> p g a", a=1).to_broadcast([P, G1, DH1]), ALU.mult)
                last.then_inc(dve_bank_copied, 1)

            def out_project(b, slot):
                n = uses.next()
                dve.wait_ge(dve_bank_filled, n + 1)
                last = dve.tensor_tensor(z[:], dve_bank.rearrange("p (i d) -> p i d", i=TT),
                                         bo_b[:].rearrange("p (a d) -> p a d", a=1).to_broadcast([P, TT, D]), ALU.add)
                last.then_inc(dve_bank_copied, 1)
                dve.wait_ge(dve_bank_copied, n + 1)
                dve.memset(pause[:], 0.0)
                norm_stats(lambda t: z[:, t, :])
                step(normed(lambda t: z[:, t, :], lambda t: z[:, t, :]))
                row = x1[:, bass.ds(b, 1), :, :].rearrange("p a i d -> p (a i) d")
                step(dve.tensor_tensor(row, row, z[:], ALU.add), then_stats=True)
                norm_stats(tokens(b))
                step(normed(lambda t: z[:, t, :], tokens(b), x1_made))

            dve.wait_ge(consts_loaded, 16 * LOADS)
            dve.wait_ge(consts_made, CONSTS_MADE)
            program(dve, [uses, steps], scores, nothing, dict(
                norm=norm, project=project, high=high, q_turn=q_turn, o_turn=o_turn, out_project=out_project))

        @block.tensor
        def _(pe):
            for_act, for_dve, steps = act_uses(), dve_uses(), Tally((NORM, J1 - 1, 2 * NORM + 4))
            pe.wait_ge(consts_made, CONSTS_MADE)
            pe.wait_ge(consts_loaded, 16 * LOADS)

            def act_turn(src):
                n = for_act.next()
                pe.wait_ge(act_bank_copied, n)
                for t in range(TT):
                    last = pe.transpose(act_bank[:, t * P:(t + 1) * P], src(t), ident[:])
                last.then_inc(act_bank_filled, 1)
                return last

            def x_turn(b, slot):
                pe.wait_ge(xn_made, b + 1)
                act_turn(lambda t: xn[:, t, :])

            def project(b, slot, half):
                pe.wait_ge(act_bank_copied, for_act.base + for_act.k)
                n = for_dve.next()
                pe.wait_ge(dve_bank_copied, n)
                for t in range(2):
                    i = 2 * half + t
                    last = pe.matmul(dve_bank[:, t * QKV1:(t + 1) * QKV1], xT[:, i * P:(i + 1) * P], wqkv[:], start=True, stop=True)
                last.then_inc(dve_bank_filled, 1)

            def k_turn(b, slot):
                pe.wait_ge(packed, b + 1)
                act_turn(lambda t: kpack[:, t, :, :].rearrange("p g r -> p (g r)"))

            def q_turn(b, slot, j):
                src = lambda t: qpack[:, slot, t, j, :, :].rearrange("p g r -> p (g r)")
                if j % 2 == 0:
                    act_turn(src)
                    return
                n = for_dve.next()
                pe.wait_ge(dve_bank_copied, n)
                for t in range(TT):
                    last = pe.transpose(dve_bank[:, t * P:(t + 1) * P], src(t), ident[:])
                last.then_inc(dve_bank_filled, 1)

            def max_turn(b, slot, j):
                pe.wait_ge(maxed, (b * J1 + j + 1) * NCH)
                act_turn(lambda t: qpack[:, slot, t, j, :, :].rearrange("p g r -> p (g r)"))

            def scores(b, slot, j, c):
                i, gs = CHUNKS[c]
                n = (b * J1 + j) * NCH + c
                if isinstance(n, int) and n == 0:
                    pe.wait_ge(act_bank_copied, for_act.base + for_act.k)
                    pe.wait_ge(dve_bank_copied, for_dve.base + for_dve.k)
                elif j == 0 and c == 0:
                    pe.wait_ge(act_bank_copied, for_act.base + for_act.k)
                    pe.wait_ge(dve_bank_copied, for_dve.base + for_dve.k)
                if not isinstance(n, int) or n >= 2:
                    pe.wait_ge(maxed, n - 1)
                w = (i + 1) * P
                bank = s_bank[:, (j * NCH + c) % 2, :]
                for k, g in enumerate(gs):
                    pe.matmul(bank[:, k * w:(k + 1) * w], qT[:, slot, j, i * P:(i + 1) * P], kT[:, slot, g, 0:w], start=True, stop=False)
                    last = pe.matmul(bank[:, k * w + i * P:(k + 1) * w], ident_bf[:], mask_ts[:], start=False, stop=True)
                last.then_inc(scores_filled, 1)

            def units(b, slot, j, k):
                n = (b * J1 + j) * NU + k
                if k == 0:
                    pe.wait_ge(act_bank_copied, for_act.base + for_act.k)
                if not isinstance(n, int) or n >= UNIT_BACK[k]:
                    pe.wait_ge(probs_made, n - UNIT_BACK[k] + 1)
                for g, s, col in UNITS[k]:
                    bank = st_bank[:, UNIT_BANK[k], col:col + T - s * P]
                    pe.matmul(bank, kT[:, slot, g, s * P:(s + 1) * P], qmT[:, j % 2, s * P:T], start=True, stop=False)
                    last = pe.matmul(bank[:, 0:P], ident_bf[:], mask_st[:], start=False, stop=True)
                last.then_inc(units_filled, 1)

            def pv(b, slot, j, s):
                n = b * J1 + j
                if s == 0:
                    pe.wait_ge(probs_made, (n + 1) * NU)
                    if not isinstance(n, int) or n >= 1:
                        pe.wait_ge(o_copied, n)
                for g in range(G1):
                    k, col = PLACE[g, s]
                    r = slice(ROWS * g, ROWS * g + ROWS)
                    last = pe.matmul(o_bank[r, s * P:T], v[:, slot, s, g, :], probs[:, j % 2, k, col:col + T - s * P],
                                     start=(s == 0), stop=(s == TT - 1))
                if s == TT - 1:
                    last.then_inc(pv_done, 1)

            def o_turn(b, slot, j):
                pe.wait_ge(o_copied, b * J1 + j + 1)
                n = for_dve.next()
                pe.wait_ge(dve_bank_copied, n)
                for t in range(TT):
                    last = pe.transpose(dve_bank[:, t * P:(t + 1) * P], oT[:, j % 2, t * P:(t + 1) * P], ident[:])
                last.then_inc(dve_bank_filled, 1)
                steps.next()

            def attn_turn(b, slot):
                pe.wait_ge(dve_bank_copied, for_dve.base + for_dve.k)
                act_turn(lambda t: attn[:, slot, t].rearrange("p g j d -> p (g j d)"))

            def out_project(b, slot):
                pe.wait_ge(act_bank_copied, for_act.base + for_act.k)
                n = for_dve.next()
                pe.wait_ge(dve_bank_copied, n)
                for t in range(TT):
                    last = pe.matmul(dve_bank[:, t * P:(t + 1) * P], aT[:, t * P:(t + 1) * P], wo[:], start=True, stop=True)
                last.then_inc(dve_bank_filled, 1)
                for _ in range(2 * NORM + 3):
                    steps.next()

            def u_turn(b, slot):
                pe.wait_ge(dve_step, steps.base + steps.k)
                act_turn(lambda t: z[:, t, :])

            def norm(b, slot):
                for _ in range(NORM):
                    steps.next()

            program(pe, [for_act, for_dve, steps], scores, units, dict(
                norm=norm, x_turn=x_turn, project=project, k_turn=k_turn, q_turn=q_turn, max_turn=max_turn, pv=pv,
                o_turn=o_turn, attn_turn=attn_turn, out_project=out_project, u_turn=u_turn))


DEPTH, HEADS, DH, WIN = 2, 8, 64, 64
INNER = HEADS * DH
PAIRS = HEADS // 2
HID = int(D * 4 * 2 / 3)
HC = -(-HID // P)
HREST = HID - (HC - 1) * P
SPAN = P + WIN
QK_SCALE = 8.0


def xpos_tables():
    half = np.arange(0, DH, 2, dtype=np.float32)
    inv = (np.float32(1.0) / np.power(np.float32(10000.0), half / np.float32(DH))).astype(np.float32)
    t = np.arange(T, dtype=np.float32)
    angle = (t[:, None] * inv[None, :]).astype(np.float32).astype(np.float64)
    base = ((half + 0.4 * DH) / (1.4 * DH)).astype(np.float64)
    scale = base[None, :] ** (((t - T // 2) / float(WIN // 2)).astype(np.float64)[:, None])
    two = lambda a, sign=1.0: np.concatenate([sign * a, a], axis=1)
    rows = np.stack([np.stack([two(np.cos(angle) * s), two(np.cos(angle) / s)] if not k else
                              [two(np.sin(angle) * s, -1.0), two(np.sin(angle) / s, -1.0)], axis=1)
                     for k, s in ((0, scale), (1, scale))], axis=1)
    return np.ascontiguousarray(rows.reshape(TT, P, 2, 2, DH).transpose(1, 0, 2, 3, 4).astype(np.float32))


NORM2 = 3 + 11
USES = {
    "weights": dict(w0=1, w1=1, x=1, dve=1),
    "project": dict(w0=1, w1=1, x=1), "rs": dict(dve=1 + 11), "turn": dict(w0=1, w1=1),
    "max_turn": dict(x=1), "den_turn": dict(x=1, dve=0), "spread": dict(x=1), "out": dict(x=1),
    "stat": dict(x=1, dve=NORM2), "rstd": dict(x=1), "up": dict(w0=1, w1=1), "down": dict(x=1),
}
PART1B = [((1, 0), "h"), ((1, 0), "project", 0), ((1, 1), "project", 1), ((1, 2), "project", 2), ((1, 3), "project", 3),
          ((1, 4), "rs"), ((1, 4), "scale", 0), ((1, 4), "scale", 1), ((1, 5), "turn", 0), ((1, 5), "scale", 2), ((1, 6), "turn", 1),
          ((1, 6), "scale", 3), ((1, 7), "turn", 2), ((1, 7), "turn", 3)]
PART2B = [((1, -1), "max_turn")]
PART3B = [((0, 0), "den_turn", 0), ((0, 0), "den_turn", 1), ((0, 0), "spread", 0), ((0, 0), "spread", 1), ((0, 1), "spread", 2),
          ((0, 1), "spread", 3), ((0, 2), "out"), ((0, 3), "stat"), ((0, 5), "rstd"), ((0, 6), "up", 0), ((0, 7), "up", 1),
          ((0, 7), "up", 2), ((1, -1), "down")]
COUNTED = ("w0", "w1", "x", "dve")
TOTALS = {c: tuple(sum(USES.get(t[1], {}).get(c, 0) for t in part) for part in (PART1B, PART2B, PART3B)) for c in COUNTED}


class Walk:

    def __init__(self, eng, scores, units, pv, tasks):
        self.eng, self.scores, self.units, self.pv, self.tasks = eng, scores, units, pv, tasks
        self.base = dict.fromkeys(COUNTED, 0)
        self.k = dict.fromkeys(COUNTED, 0)

    @property
    def at(self):
        return {c: self.base[c] + self.k[c] for c in COUNTED}

    def task(self, name, l, b, slot, *args):
        if name in self.tasks:
            self.tasks[name](l, b, slot, *args, at=self.at)
        for c, n in USES.get(name, {}).items():
            self.k[c] += n

    def enter(self, l, b):
        for c, (p1, p2, p3) in TOTALS.items():
            w = USES["weights"].get(c, 0)
            self.base[c] = l * (B * (p1 + p2 + p3) + w)
            if b is None:
                self.k[c] = 0
            elif isinstance(b, int) and b == 0:
                assert self.k[c] == w + p1
            elif isinstance(b, int) and b == B:
                self.k[c] = w + B * (p1 + p2 + p3) - p3
            elif isinstance(b, int):
                self.k[c] = w + b * (p1 + p2 + p3) + p1 - p3
            else:
                self.base[c] = self.base[c] + b * (p1 + p2 + p3)
                self.k[c] = w + p1 - p3

    def body(self, l, b, slot, first=False, last=False):
        self.enter(l, b)

        def between(place):
            for at, name, *args in PART3B:
                if at == place and not first:
                    self.task(name, l, b - 1, 1 - slot, *args)
            for at, name, *args in PART2B:
                if at == place:
                    self.task(name, l, b, slot, *args)
            for at, name, *args in PART1B:
                if at == place and not last:
                    self.task(name, l, b + 1, 1 - slot, *args)

        for h in range(HEADS):
            for c in range(2):
                self.scores(l, b, slot, h, c, at=self.at)
            between((0, h))
        between((1, -1))
        for h in range(HEADS):
            for c in range(2):
                self.units(l, b, slot, h, c, at=self.at)
            if h:
                self.pv(l, b, slot, h - 1, at=self.at)
            between((1, h))
        self.pv(l, b, slot, HEADS - 1, at=self.at)

    def run(self):
        with self.eng.Fori(0, DEPTH) as l:
            self.enter(l, None)
            self.task("weights", l, 0, 0)
            for _, name, *args in PART1B:
                self.task(name, l, 0, 0, *args)
            self.body(l, 0, 0, first=True)
            with self.eng.Fori(1, B - 2, 2) as b:
                self.body(l, b, 1)
                self.body(l, b + 1, 0)
            self.body(l, B - 1, 1, last=True)
            self.enter(l, B)
            for _, name, *args in PART3B:
                self.task(name, l, B - 1, 1, *args)


def local_layers(nc, sem, ident, ident_bf, u, Wqkv, q_scale, k_scale, Wo, ln_g, ln_b, W1, B1, W2, B2, tab2):
    with ExitStack() as ctx:
        def sb(name, shape, dt=F32):
            return ctx.enter_context(nc.sbuf_tensor("b_" + name, shape, dt))

        def banks(name, n):
            return ctx.enter_context(nc.psum_tensor("b_" + name, [P, n, 512], F32))

        w_high = sb("w_high", [D, 3 * INNER], F32R)
        w_low = sb("w_low", [D, 3 * INNER], F32R)
        wo = sb("wo", [P, PAIRS, D])
        w1c = sb("w1c", [D, 2, HC * P])
        w2 = sb("w2", [P, HC, D])
        g_col, b_col = sb("g_col", [D, 1]), sb("b_col", [D, 1])
        bias = sb("bias", [P, 8])
        scales = sb("scales", [P, 2, DH])
        tabs = sb("tabs", [P, TT, 2, 2, DH])
        center = sb("center", [D, D])
        ones = sb("ones", [P, ROWS])
        sel = sb("sel", [P, HEADS], F32R)
        mask_q = sb("mask_q", [P, 2, SPAN], BF16)
        mask_k = sb("mask_k", [P, SPAN], BF16)
        h_high, h_low = sb("h_high", [D, T], F32R), sb("h_low", [D, T], F32R)
        raw = sb("raw", [P, 2, 2, INNER])
        sq = sb("sq", [P, 2, INNER])
        part_b = sb("part_b", [P, 2, INNER])
        qk = sb("qk", [P, TT, 2, INNER])
        ss, rs, tmp = (sb(n, [P, TT * 2 * HEADS]) for n in ("ss", "rs", "tmp"))
        qT = sb("qT", [P, 2, PAIRS, 2, T])
        kT = sb("kT", [P, 2, PAIRS, WIN + T])
        v = sb("v", [P, 2, TT, INNER])
        neg_max = sb("neg_max", [P, TT, P])
        mT = sb("mT", [P, T], F32R)
        probs = sb("probs", [P, 2, 2, 2 * SPAN])
        o_raw = sb("o_raw", [P, PAIRS, T])
        denT = sb("denT", [P, 2, T])
        rden = sb("rden", [P, TT, HEADS])
        oT = sb("oT", [P, PAIRS, T])
        x2 = sb("x2", [D, T])
        h2, sq2 = sb("h2", [D, T]), sb("sq2", [D, T])
        moments = sb("moments", [P, 2 * TT])
        var, rstd, tmp4 = (sb(n, [P, TT]) for n in ("var", "rstd", "tmp4"))
        hid = sb("hid", [P, HC, T])
        w_raw = oT[:].rearrange("p c t -> p (c t)")[:, 0:3 * INNER]
        w1g = o_raw[:, 0:2, 0:HID]
        tab = probs[:].rearrange("p a c k -> p (a c k)")[:, 0:TT * 4 * DH].rearrange("p (i s x d) -> p i s x d", i=TT, s=2, x=2)
        idle = raw[:].rearrange("p a x n -> p (a x n)")
        w1 = idle[:, 0:2 * HC * P].rearrange("p (h n) -> p h n", h=2)
        b1r = idle[0:1, 2 * HC * P:4 * HC * P].rearrange("p (h n) -> p h n", h=2)
        b2r = idle[0:1, 4 * HC * P:4 * HC * P + D]

        w_banks = banks("w", 2)
        x_bank = banks("x", 1)[:, 0]
        s_bank = banks("s", 1)[:, 0]
        st_bank = banks("st", 2)
        o_bank = banks("o", 1)[:, 0]
        den_bank = banks("den", 1)[:, 0]
        w0_bank, w1_bank = w_banks[:, 0], w_banks[:, 1]

        (consts_made, loaded, w0_filled, w0_freed, w1_filled, w1_freed, x_filled, x_freed, dve_step, high_made,
         low_made, split_made, tabs_made, squared, ss_made, a_made, pool_step, c_made, scaled, scores_filled, maxed,
         units_filled, probs_made, pv_done, o_copied, den_done, den_copied, h2_made, gates_made) = (sem("b_" + n) for n in
         """consts_made loaded w0_filled w0_freed w1_filled w1_freed x_filled x_freed dve_step high_made
         low_made split_made tabs_made squared ss_made a_made pool_step c_made scaled scores_filled maxed
         units_filled probs_made pv_done o_copied den_done den_copied h2_made gates_made""".split())
        freed = dict(w0=w0_freed, w1=w1_freed, x=x_freed)
        nothing = lambda *a, **k: None
        seq = lambda l, b: l * B + b
        at_start = lambda b: isinstance(b, int) and b == 0
        LOADS = 14
        block = ctx.enter_context(nc.Block())

        def ds_u(b, rows, cols):
            return u[rows, bass.ds(b, 1), cols].rearrange("p a t -> p (a t)")

        LOW, UP = slice(0, DH), slice(DH, P)

        @block.sync
        def _(sp):
            sp.wait_ge(consts_made, CONSTS_MADE)

            def load(l):
                one = lambda a: a[bass.ds(l, 1)]
                loads = [(tab, tab2), (w_raw, one(Wqkv).rearrange("a p n -> (a p) n")),
                         (wo[:], one(Wo).rearrange("a (c p) n -> p (a c) n", p=P)),
                         (w2[0:HREST, HC - 1, :], one(W2)[:, (HC - 1) * P:HID, :].rearrange("a p n -> (a p) n")),
                         (w2[:, 0:HC - 1, :], one(W2)[:, 0:(HC - 1) * P, :].rearrange("a (c p) n -> p (a c) n", p=P)),
                         (b2r, one(B2)),
                         (g_col[:], one(ln_g).rearrange("a (p n) -> (a p) n", n=1)),
                         (b_col[:], one(ln_b).rearrange("a (p n) -> (a p) n", n=1)),
                         (scales[:, 0, :], one(q_scale).to_broadcast([P, DH])),
                         (scales[:, 1, :], one(k_scale).to_broadcast([P, DH]))]
                for half in range(2):
                    loads += [(w1[:, half, 0:HID], one(W1)[:, :, half * HID:(half + 1) * HID].rearrange("a p n -> (a p) n")),
                              (b1r[:, half, 0:HID], one(B1)[:, half * HID:(half + 1) * HID])]
                for dst, src in loads:
                    sp.dma_start(dst, src).then_inc(loaded, 16)
                assert len(loads) == LOADS

            load(0)
            with sp.Fori(1, DEPTH) as l:
                sp.wait_ge(x_freed, l * (B * sum(TOTALS["x"]) + USES["weights"]["x"]))
                load(l)

        @block.gpsimd
        def _(pool):
            zero = [center[:], mask_q[:], mask_k[:], qT[:], kT[:, :, :, 0:WIN], neg_max[:], h_high[:].bitcast(F32),
                    h_low[:].bitcast(F32), h2[:], sq2[:], hid[:], w2[:]]
            for a in zero:
                pool.memset(a, 0.0).then_inc(consts_made, 1)
            pool.memset(ones[:], 1.0).then_inc(consts_made, 1)
            n = len(zero) + 1
            pool.wait_ge(consts_made, n)
            select = lambda a, op, fill, base, pattern, mult: pool.affine_select(
                out=a, in_=a, compare_op=op, fill=fill, base=base, pattern=pattern, channel_multiplier=mult).then_inc(consts_made, 1)
            select(center[:], ALU.not_equal, 1.0, 0, [[-1, D]], 1)
            pool.tensor_copy(sel[:], ident[:, 0:HEADS]).then_inc(consts_made, 1)
            select(mask_q[:], ALU.is_ge, MASKED, 0, [[0, 2], [1, SPAN]], -1)
            select(mask_k[:], ALU.is_ge, MASKED, 0, [[1, SPAN]], -1)
            pool.wait_ge(consts_made, n + 4)
            select(mask_q[:], ALU.is_ge, MASKED, WIN, [[0, 2], [-1, SPAN]], 1)
            select(mask_k[:], ALU.is_ge, MASKED, WIN, [[-1, SPAN]], 1)
            pool.tensor_scalar(center[:], center[:], -1.0 / D, None, ALU.add).then_inc(consts_made, 1)
            pool.wait_ge(consts_made, n + 7)
            select(mask_q[:, 1, :], ALU.is_ge, MASKED, -WIN, [[1, SPAN]], 0)
            assert n + 8 == CONSTS_MADE, n + 8

            def project(l, b, slot, i, at):
                n = seq(l, b) * TT + i
                pool.wait_ge(w0_freed, at["w0"] + 1)
                pool.wait_ge(w1_freed, at["w1"] + 1)
                if not at_start(b) or i > 0:
                    pool.wait_ge(c_made, n)
                if i == 0 and at_start(b):
                    pool.wait_ge(tabs_made, (l + 1) * 3)
                hd = lambda a, lo: a.rearrange("p x (h d) -> p x h d", d=DH)[:, :, :, lo:lo + DH // 2]
                table = lambda x, lo: tabs[:, i, 1, x, lo:lo + DH // 2].rearrange("p (a d) -> p a d", a=1).to_broadcast([P, HEADS, DH // 2])
                for x in range(2):
                    for lo in (0, DH // 2):
                        last = pool.tensor_tensor(part_b[:, x, :].rearrange("p (h d) -> p h d", d=DH)[:, :, lo:lo + DH // 2],
                                                  raw[:, i % 2, x, :].rearrange("p (h d) -> p h d", d=DH)[:, :, DH // 2 - lo:DH - lo],
                                                  table(x, lo), ALU.mult)
                last.then_inc(pool_step, 1)
                pool.wait_ge(pool_step, n + 1)
                pool.wait_ge(a_made, n + 1)
                pool.tensor_tensor(qk[:, i], qk[:, i], part_b[:], ALU.add).then_inc(c_made, 1)

            Walk(pool, nothing, nothing, nothing, dict(project=project)).run()

        @block.scalar
        def _(act):
            act.wait_ge(consts_made, CONSTS_MADE)

            def weights(l, b, slot, at):
                act.wait_ge(loaded, (l + 1) * LOADS * 16)
                act.copy(w_high[:], w_raw).then_inc(split_made, 1)
                act.wait_ge(w0_filled, at["w0"] + 1)
                act.copy(w1c[:, 0, 0:HID], w0_bank[:, 0:HID]).then_inc(w0_freed, 1)
                act.wait_ge(w1_filled, at["w1"] + 1)
                act.copy(w1c[:, 1, 0:HID], w1_bank[:, 0:HID]).then_inc(w1_freed, 1)

            def h(l, b, slot, at):
                act.copy(h_high[LOW, :], ds_u(b, LOW, slice(0, T))).then_inc(high_made, 1)
                act.copy(h_high[UP, 1:T], ds_u(b, UP, slice(0, T - 1))).then_inc(high_made, 1)

            def project(l, b, slot, i, at):
                n = seq(l, b) * TT + i
                act.wait_ge(w0_filled, at["w0"] + 1)
                act.wait_ge(w1_filled, at["w1"] + 1)
                if not at_start(b) or i >= 1:
                    act.wait_ge(ss_made, n)
                if not at_start(b) or i >= 2:
                    act.wait_ge(a_made, n - 1)
                    act.wait_ge(c_made, n - 1)
                act.activation(sq[:], w_banks[:], ACT.Square).then_inc(squared, 1)
                act.copy(raw[:, i % 2, 0, :], w0_bank).then_inc(w0_freed, 1)
                act.copy(raw[:, i % 2, 1, :], w1_bank).then_inc(w1_freed, 1)
                act.wait_ge(x_filled, at["x"] + 1)
                act.copy(v[:, slot, i, :], x_bank).then_inc(x_freed, 1)

            def turn(l, b, slot, i, at):
                act.wait_ge(w1_filled, at["w1"] + 1)
                act.copy(kT[:, slot, :, WIN + i * P:WIN + (i + 1) * P],
                         w1_bank.rearrange("p (c t) -> p c t", c=PAIRS)).then_inc(w1_freed, 1)

            def max_turn(l, b, slot, at):
                act.wait_ge(x_filled, at["x"] + 1)
                act.copy(mT[:], x_bank).then_inc(x_freed, 1)

            def units(l, b, slot, h, c, at):
                n = (seq(l, b) * HEADS + h) * 2 + c
                act.wait_ge(units_filled, n + 1)
                w = 2 * SPAN if c == 0 else SPAN + P
                act.activation(probs[:, h % 2, c, 0:w], st_bank[:, c, 0:w], ACT.Exp, scale=QK_SCALE).then_inc(probs_made, 1)

            def pv(l, b, slot, h, at):
                if h % 2:
                    act.wait_ge(pv_done, seq(l, b) * PAIRS + h // 2 + 1)
                    act.copy(o_raw[:, h // 2, :], o_bank).then_inc(o_copied, 1)
                if h % 4 == 3:
                    act.wait_ge(den_done, seq(l, b) * 2 + h // 4 + 1)
                    act.copy(denT[:, h // 4, :], den_bank).then_inc(den_copied, 1)

            def stat(l, b, slot, at):
                act.wait_ge(x_freed, at["x"])
                act.copy(h2[LOW, :], x2[LOW, :])
                act.copy(h2[UP, 1:T], x2[UP, 0:T - 1])
                act.activation(sq2[LOW, :], x2[LOW, :], ACT.Square)
                act.activation(sq2[UP, 1:T], x2[UP, 0:T - 1], ACT.Square).then_inc(h2_made, 1)

            def up(l, b, slot, c, at):
                act.wait_ge(w0_filled, at["w0"] + 1)
                r = slice(0, P if c < HC - 1 else HREST)
                act.activation(hid[r, c, :], w0_bank[r, :], ACT.Gelu, bias=bias[r, HC + c:HC + c + 1]).then_inc(w0_freed, 1)

            Walk(act, nothing, units, pv, dict(weights=weights, h=h, project=project, turn=turn, max_turn=max_turn,
                                               stat=stat, up=up)).run()

        @block.vector
        def _(dve):
            dve.wait_ge(consts_made, CONSTS_MADE)

            class Steps:
                def __init__(self, at):
                    self.n = at["dve"]

                def __call__(self, instruction):
                    instruction.then_inc(dve_step, 1)
                    self.n = self.n + 1
                    dve.wait_ge(dve_step, self.n)

            def weights(l, b, slot, at):
                step = Steps(at)
                dve.wait_ge(loaded, (l + 1) * LOADS * 16)
                step(dve.tensor_scalar(w1g, w1[:, :, 0:HID], g_col[:], None, ALU.mult))
                dve.wait_ge(split_made, l * 2 + 1)
                dve.tensor_tensor(w_low[:], w_raw, w_high[:].bitcast(F32), ALU.subtract).then_inc(split_made, 1)
                for i in range(TT):
                    last = dve.tensor_tensor(tabs[:, i, 0], tab[:, i, 0], scales[:], ALU.mult)
                last.then_inc(tabs_made, 1)
                for lo in (0, DH // 2):
                    for i in range(TT):
                        last = dve.tensor_tensor(tabs[:, i, 1, :, lo:lo + DH // 2], tab[:, i, 1, :, lo:lo + DH // 2],
                                                 scales[:, :, DH // 2 - lo:DH - lo], ALU.mult)
                    last.then_inc(tabs_made, 1)
                dve.wait_ge(tabs_made, (l + 1) * 3)
                dve.wait_ge(x_filled, at["x"] + 1)
                for first in (0, HC):
                    dve.tensor_copy(bias[:, first:first + HC - 1], x_bank[:, first:first + HC - 1])
                    dve.tensor_copy(bias[0:HREST, first + HC - 1:first + HC], x_bank[0:HREST, first + HC - 1:first + HC])
                dve.tensor_copy(bias[:, 6:7], x_bank[:, 6:7]).then_inc(x_freed, 1)

            def h(l, b, slot, at):
                dve.wait_ge(high_made, seq(l, b) * 2 + 2)
                dve.tensor_tensor(h_low[LOW, :], ds_u(b, LOW, slice(0, T)), h_high[LOW, :].bitcast(F32), ALU.subtract)
                dve.tensor_tensor(h_low[UP, 1:T], ds_u(b, UP, slice(0, T - 1)), h_high[UP, 1:T].bitcast(F32),
                                  ALU.subtract).then_inc(low_made, 1)

            def project(l, b, slot, i, at):
                n = seq(l, b) * TT + i
                dve.wait_ge(squared, n + 1)
                dve.tensor_reduce(ss[:, i * 16:(i + 1) * 16], sq[:].rearrange("p x (h d) -> p (x h) d", d=DH),
                                  AX, ALU.add).then_inc(ss_made, 1)
                dve.wait_ge(w0_freed, at["w0"] + 1)
                dve.wait_ge(w1_freed, at["w1"] + 1)
                for x in range(2):
                    last = dve.tensor_tensor(qk[:, i, x, :].rearrange("p (h d) -> p h d", d=DH),
                                             raw[:, i % 2, x, :].rearrange("p (h d) -> p h d", d=DH),
                                             tabs[:, i, 0, x, :].rearrange("p (a d) -> p a d", a=1).to_broadcast([P, HEADS, DH]), ALU.mult)
                last.then_inc(a_made, 1)

            def rs_(l, b, slot, at):
                step = Steps(at)
                dve.wait_ge(ss_made, seq(l, b) * TT + TT)
                step(dve.tensor_scalar(ss[:], ss[:], 1e-24, None, ALU.max))
                rsqrt(dve, step, rs[:], ss[:], tmp[:])

            def scale(l, b, slot, i, at):
                n = seq(l, b) * TT + i
                dve.wait_ge(c_made, n + 1)
                a = qk[:, i].rearrange("p x (h d) -> p (x h) d", d=DH)
                dve.tensor_tensor(a, a, rs[:, i * 16:(i + 1) * 16].rearrange("p (h a) -> p h a", a=1).to_broadcast([P, 16, DH]),
                                  ALU.mult).then_inc(scaled, 1)

            def turn(l, b, slot, i, at):
                dve.wait_ge(w0_filled, at["w0"] + 1)
                for a, r in enumerate((LOW, UP)):
                    last = dve.tensor_copy(qT[r, slot, :, a, i * P:(i + 1) * P], w0_bank[r, :].rearrange("p (c t) -> p c t", c=PAIRS))
                last.then_inc(w0_freed, 1)

            def scores(l, b, slot, h, c, at):
                n = (seq(l, b) * HEADS + h) * 2 + c
                dve.wait_ge(scores_filled, n + 1)
                dve.tensor_reduce(neg_max[:, 2 * c:2 * c + 2, h], s_bank[:, 0:2 * SPAN].rearrange("p (i k) -> p i k", i=2),
                                  AX, ALU.max, negate=True).then_inc(maxed, 1)

            def den_turn(l, b, slot, g, at):
                dve.wait_ge(x_filled, at["x"] + 1)
                dve.reciprocal(rden[:, :, 4 * g:4 * g + 4],
                               x_bank.rearrange("p (i h r) -> p i h r", i=TT, h=4)[:, :, :, 0]).then_inc(x_freed, 1)

            def spread(l, b, slot, p, at):
                dve.wait_ge(x_filled, at["x"] + 1)
                dve.tensor_tensor(oT[:, p, :], o_raw[:, p, :], x_bank, ALU.mult).then_inc(x_freed, 1)

            def out(l, b, slot, at):
                dve.wait_ge(x_filled, at["x"] + 1)
                dve.tensor_tensor(x2[:], ds_u(b, slice(0, P), slice(0, T)), x_bank, ALU.add).then_inc(x_freed, 1)

            def stat(l, b, slot, at):
                step = Steps(at)
                dve.wait_ge(x_filled, at["x"] + 1)
                dve.tensor_scalar(moments[:], x_bank[:, 0:2 * TT], 1.0 / D, None, ALU.mult).then_inc(x_freed, 1)
                dve.wait_ge(x_freed, at["x"] + 1)
                step(dve.tensor_tensor(tmp4[:], moments[:, 0:TT], moments[:, 0:TT], ALU.mult))
                step(dve.tensor_tensor(var[:], moments[:, TT:2 * TT], tmp4[:], ALU.subtract))
                step(dve.tensor_scalar(var[:], var[:], 0.0, EPS, ALU.max, ALU.add))
                rsqrt(dve, step, rstd[:], var[:], tmp4[:])

            def rstd_(l, b, slot, at):
                dve.wait_ge(x_filled, at["x"] + 1)
                dve.wait_ge(h2_made, seq(l, b) + 1)
                dve.tensor_tensor(h2[:], h2[:], x_bank, ALU.mult).then_inc(x_freed, 1)

            def up(l, b, slot, c, at):
                dve.wait_ge(w1_filled, at["w1"] + 1)
                dve.wait_ge(w0_freed, at["w0"] + 1)
                r = slice(0, P if c < HC - 1 else HREST)
                dve.scalar_tensor_tensor(hid[r, c, :], w1_bank[r, :], bias[r, c:c + 1], hid[r, c, :], ALU.add,
                                         ALU.mult).then_inc(w1_freed, 1)

            def down(l, b, slot, at):
                dve.wait_ge(x_filled, at["x"] + 1)
                dve.scalar_tensor_tensor(ds_u(b, slice(0, P), slice(0, T)), x_bank, bias[:, 6:7], x2[:], ALU.add,
                                         ALU.add).then_inc(x_freed, 1)

            Walk(dve, scores, nothing, nothing, dict(weights=weights, h=h, project=project, rs=rs_, scale=scale, turn=turn,
                 den_turn=den_turn, spread=spread, out=out, stat=stat, rstd=rstd_, up=up, down=down)).run()

        @block.tensor
        def _(pe):
            pe.wait_ge(consts_made, CONSTS_MADE)

            def weights(l, b, slot, at):
                pe.wait_ge(loaded, (l + 1) * LOADS * 16)
                for half in range(2):
                    for c in range(HC):
                        r = P if c < HC - 1 else HREST
                        col = x_bank[0:r, half * HC + c:half * HC + c + 1]
                        pe.matmul(col, w1[:, half, c * P:c * P + r], b_col[:], start=True, stop=False)
                        pe.matmul(col, b1r[:, half, c * P:c * P + r], ones[0:1, 0:1], start=False, stop=True)
                pe.matmul(x_bank[:, 6:7], b2r, ones[0:1, 0:1], start=True, stop=True).then_inc(x_filled, 1)
                pe.wait_ge(dve_step, at["dve"] + 1)
                pe.matmul(w0_bank[:, 0:HID], center[:], w1g[:, 0, :], start=True, stop=True).then_inc(w0_filled, 1)
                pe.matmul(w1_bank[:, 0:HID], center[:], w1g[:, 1, :], start=True, stop=True).then_inc(w1_filled, 1)
                pe.wait_ge(split_made, l * 2 + 2)

            def project(l, b, slot, i, at):
                for c, f in freed.items():
                    pe.wait_ge(f, at[c])
                if i == 0:
                    pe.wait_ge(low_made, seq(l, b) + 1)
                t = slice(i * P, (i + 1) * P)
                outs = (w0_bank, w1_bank, x_bank)
                fills = (w0_filled, w1_filled, x_filled)
                for hh, ww, st in ((h_high, w_high, 0), (h_high, w_low, 1), (h_low, w_high, 2)):
                    for o in range(3):
                        last = pe.matmul(outs[o], hh[:, t], ww[:, o * INNER:(o + 1) * INNER], start=(st == 0), stop=(st == 2))
                        if st == 2:
                            last.then_inc(fills[o], 1)

            def turn(l, b, slot, i, at):
                pe.wait_ge(scaled, seq(l, b) * TT + i + 1)
                for x, (o, fl) in enumerate(((w0_bank, w0_filled), (w1_bank, w1_filled))):
                    pe.wait_ge((w0_freed, w1_freed)[x], at[("w0", "w1")[x]])
                    for p in range(PAIRS):
                        last = pe.transpose(o[:, p * P:(p + 1) * P], qk[:, i, x, p * P:(p + 1) * P], ident[:])
                    last.then_inc(fl, 1)

            def scores(l, b, slot, h, c, at):
                n = (seq(l, b) * HEADS + h) * 2 + c
                if h == 0 and c == 0:
                    pe.wait_ge(w0_freed, at["w0"])
                    pe.wait_ge(w1_freed, at["w1"])
                    if not at_start(b):
                        pe.wait_ge(maxed, n)
                else:
                    pe.wait_ge(maxed, n)
                for k in range(2):
                    i = 2 * c + k
                    out = s_bank[:, k * SPAN:(k + 1) * SPAN]
                    pe.matmul(out, qT[:, slot, h // 2, h % 2, i * P:(i + 1) * P], kT[:, slot, h // 2, i * P:i * P + SPAN],
                              start=True, stop=False)
                    last = pe.matmul(out, ident_bf[:], mask_q[:, int(i == 0), :], start=False, stop=True)
                last.then_inc(scores_filled, 1)

            def max_turn(l, b, slot, at):
                pe.wait_ge(maxed, (seq(l, b) + 1) * HEADS * 2)
                pe.wait_ge(x_freed, at["x"])
                for i in range(TT):
                    last = pe.transpose(x_bank[:, i * P:(i + 1) * P], neg_max[:, i, :], ident[:])
                last.then_inc(x_filled, 1)

            def units(l, b, slot, h, c, at):
                n = (seq(l, b) * HEADS + h) * 2 + c
                if h == 0:
                    pe.wait_ge(x_freed, at["x"])
                if not at_start(b) or h > 0:
                    pe.wait_ge(probs_made, n - 1)
                for k in range(2):
                    j = 2 * c + k
                    w = SPAN if j < TT - 1 else P
                    out = st_bank[:, c, k * SPAN:k * SPAN + w]
                    q = slice(j * P, j * P + w)
                    pe.matmul(out, kT[:, slot, h // 2, WIN + j * P:WIN + (j + 1) * P], qT[:, slot, h // 2, h % 2, q],
                              start=True, stop=False)
                    pe.matmul(out, ident_bf[:], mask_k[:, 0:w], start=False, stop=False)
                    last = pe.matmul(out, sel[:, h:h + 1].to_broadcast([P, P]), mT[:, q], start=False, stop=True)
                last.then_inc(units_filled, 1)

            def pv(l, b, slot, h, at):
                n = seq(l, b)
                pe.wait_ge(probs_made, (n * HEADS + h + 1) * 2)
                if h % 2 == 0 and not (at_start(b) and h == 0):
                    pe.wait_ge(o_copied, n * PAIRS + h // 2)
                if h % 4 == 0 and not (at_start(b) and h == 0):
                    pe.wait_ge(den_copied, n * 2 + h // 4)
                a = h % 2
                ro, rd = slice(DH * a, DH * a + DH), slice(ROWS * (h % 4), ROWS * (h % 4) + ROWS)
                for j in range(TT):
                    w = SPAN if j < TT - 1 else P
                    pr = probs[:, h % 2, j // 2, (j % 2) * SPAN:(j % 2) * SPAN + w]
                    t = slice(j * P, j * P + w)
                    flags = dict(start=(j == 0), stop=(j == TT - 1), skip_group_check=True)
                    o = pe.matmul(o_bank[ro, t], v[:, slot, j, h * DH:(h + 1) * DH], pr, **flags)
                    d = pe.matmul(den_bank[rd, t], ones[:], pr, **flags)
                if a:
                    o.then_inc(pv_done, 1)
                if h % 4 == 3:
                    d.then_inc(den_done, 1)

            def den_turn(l, b, slot, g, at):
                pe.wait_ge(den_copied, seq(l, b) * 2 + g + 1)
                pe.wait_ge(x_freed, at["x"])
                for i in range(TT):
                    last = pe.transpose(x_bank[:, i * P:(i + 1) * P], denT[:, g, i * P:(i + 1) * P], ident[:])
                last.then_inc(x_filled, 1)

            def spread(l, b, slot, p, at):
                pe.wait_ge(x_freed, at["x"])
                for i in range(TT):
                    for a, r in enumerate((LOW, UP)):
                        last = pe.matmul(x_bank[r, i * P:(i + 1) * P], rden[:, i, 2 * p + a:2 * p + a + 1].to_broadcast([P, DH]),
                                         ident[:], start=True, stop=True)
                last.then_inc(x_filled, 1)

            def out(l, b, slot, at):
                pe.wait_ge(x_freed, at["x"])
                for p in range(PAIRS):
                    last = pe.matmul(x_bank, wo[:, p, :], oT[:, p, :], start=(p == 0), stop=(p == PAIRS - 1))
                last.then_inc(x_filled, 1)

            def stat(l, b, slot, at):
                pe.wait_ge(h2_made, seq(l, b) + 1)
                pe.wait_ge(x_freed, at["x"])
                for k, src in enumerate((h2, sq2)):
                    for i in range(TT):
                        last = pe.matmul(x_bank[:, k * TT + i:k * TT + i + 1], src[:, i * P:(i + 1) * P], ones[:, 0:1], start=True, stop=True)
                last.then_inc(x_filled, 1)

            def rstd_(l, b, slot, at):
                pe.wait_ge(dve_step, at["dve"])
                for i in range(TT):
                    last = pe.transpose(x_bank[:, i * P:(i + 1) * P], rstd[:, i:i + 1].to_broadcast([P, P]), ident[:])
                last.then_inc(x_filled, 1)

            def up(l, b, slot, c, at):
                if c == 0:
                    pe.wait_ge(x_freed, at["x"])
                r = P if c < HC - 1 else HREST
                for half, bank, fr, fl in ((1, w0_bank, "w0", w0_filled), (0, w1_bank, "w1", w1_filled)):
                    pe.wait_ge(freed[fr], at[fr])
                    pe.matmul(bank[0:r, :], w1c[:, half, c * P:c * P + r], h2[:], start=True, stop=True).then_inc(fl, 1)

            def down(l, b, slot, at):
                pe.wait_ge(w1_freed, at["w1"])
                pe.wait_ge(x_freed, at["x"])
                for c in range(HC):
                    last = pe.matmul(x_bank, w2[:, c, :], hid[:, c, :], start=(c == 0), stop=(c == HC - 1))
                last.then_inc(x_filled, 1)

            Walk(pe, scores, units, pv, dict(weights=weights, project=project, turn=turn, max_turn=max_turn, den_turn=den_turn,
                 spread=spread, out=out, stat=stat, rstd=rstd_, up=up, down=down)).run()


CONSTS_MADE = 21


def last_norm(nc, sem, ident, u, x1_v, out_v):
    with ExitStack() as ctx:
        sb = lambda name, shape: ctx.enter_context(nc.sbuf_tensor("c_" + name, shape, F32))
        uf = sb("uf", [D, 2, T])
        x1 = sb("x1", [P, B, TT, D])
        y = sb("y", [P, 2, TT, D])
        stats = sb("stats", [P, TT, 6])
        mv = sb("mv", [P, TT, 2])
        var, rstd, tmp = (sb(n, [P, TT]) for n in ("var", "rstd", "tmp"))
        pause = sb("pause", [P, 1])
        bank = ctx.enter_context(nc.psum_tensor("c_bank", [P, 2, TT, D], F32))
        x1_loaded, copied, turned, dve_step, made = (sem("c_" + n) for n in "x1_loaded copied turned dve_step made".split())
        stored = [sem(f"c_stored_{slot}") for slot in range(2)]
        STEPS = 3 + 11 + 1
        block = ctx.enter_context(nc.Block())

        def twice(eng, one):
            one(0, 0)
            one(1, 1)
            with eng.Fori(2, B - 1, 2) as b:
                one(b, 0)
                one(b + 1, 1)

        @block.sync
        def _(sp):
            sp.dma_start(x1[:], x1_v).then_inc(x1_loaded, 16)

            def one(b, slot):
                sp.wait_ge(made, b + 1)
                sp.dma_start(out_v[:, bass.ds(b, 1)], y[:, slot:slot + 1]).then_inc(stored[slot], 16)
            twice(sp, one)
            for slot in range(2):
                sp.wait_ge(stored[slot], 16 * B // 2)

        @block.scalar
        def _(act):
            def one(b, slot):
                if not isinstance(b, int):
                    act.wait_ge(turned, b - 1)
                act.copy(uf[:, slot, :], u[:, bass.ds(b, 1), :].rearrange("p a t -> p (a t)")).then_inc(copied, 1)
            twice(act, one)

        @block.tensor
        def _(pe):
            def one(b, slot):
                pe.wait_ge(copied, b + 1)
                if not isinstance(b, int):
                    pe.wait_ge(made, b - 1)
                for i in range(TT):
                    last = pe.transpose(bank[:, slot, i, :], uf[:, slot, i * P:(i + 1) * P], ident[:])
                last.then_inc(turned, 1)
            twice(pe, one)

        @block.vector
        def _(dve):
            dve.wait_ge(x1_loaded, 16)

            def one(b, slot):
                count = [b * STEPS]

                def step(instruction, then_stats=False):
                    instruction.then_inc(dve_step, 1)
                    count[0] = count[0] + 1
                    dve.wait_ge(dve_step, count[0])
                    if then_stats:
                        dve.memset(pause[:], 0.0)

                dve.wait_ge(turned, b + 1)
                dve.memset(pause[:], 0.0)
                for i in range(TT):
                    last = dve.bn_stats(stats[:, i, :], bank[:, slot, i, :])
                step(last, then_stats=True)
                for i in range(TT):
                    last = dve.bn_aggr(mv[:, i, :], stats[:, i, :])
                step(last)
                step(dve.tensor_scalar(var[:], mv[:, :, 1], EPS, None, ALU.add))
                rsqrt(dve, step, rstd[:], var[:], tmp[:])
                if not isinstance(b, int):
                    dve.wait_ge(stored[slot], (b - slot) * 8)
                for i in range(TT):
                    last = dve.tensor_scalar(y[:, slot, i, :], bank[:, slot, i, :], mv[:, i, 0:1], rstd[:, i:i + 1],
                                             ALU.subtract, ALU.mult)
                step(last)
                dve.tensor_tensor(y[:, slot], y[:, slot], x1[:, bass.ds(b, 1)].rearrange("p a i d -> p (a i) d"),
                                  ALU.add).then_inc(made, 1)
            twice(dve, one)


NORM = 3 + 11


_INS = ['L0_attn_x', 'L0_attn_Wq', 'L0_attn_bq', 'L0_attn_Wk', 'L0_attn_bk', 'L0_attn_Wv', 'L0_attn_bv', 'L0_attn_Wo', 'L0_attn_bo',
        'L0_ffn_wqkv', 'L0_ffn_q_scale', 'L0_ffn_k_scale', 'L0_ffn_wo', 'L0_ffn_ln_g', 'L0_ffn_ln_b', 'L0_ffn_w1', 'L0_ffn_b1',
        'L0_ffn_w2', 'L0_ffn_b2']


def kernel(**inputs):
    import numpy as _np
    import concourse.bacc as _bacc
    from concourse import mybir as _mybir
    from concourse.bass_utils import run_bass_kernel_spmd as _run

    nc = _bacc.Bacc("TRN2", target_bir_lowering=False, num_devices=1)
    arrays = {f"in_{n}": _np.ascontiguousarray(inputs[n]) for n in _INS}
    arrays["cos1"], arrays["sin1"] = rope_tables()
    arrays["tab2"] = xpos_tables()
    args = [nc.dram_tensor(n, a.shape, _mybir.dt.from_np(a.dtype), kind="ExternalInput").ap() for n, a in arrays.items()]
    args.append(nc.dram_tensor("out_0", (B, T, D), _mybir.dt.float32, kind="ExternalOutput").ap())
    sandwich_kernel(nc, *args)
    r = _run(nc, [arrays], core_ids=[0])
    return r.results[0]["out_0"]
```

```python
from contextlib import ExitStack

import numpy as np
import concourse.bass as bass
from concourse import mybir

F32 = mybir.dt.float32
F32R = mybir.dt.float32r
BF16 = mybir.dt.bfloat16
I32 = mybir.dt.int32
ALU = mybir.AluOpType
ACT = mybir.ActivationFunctionType
AX = mybir.AxisListType.X

P = 128
B, T, D = 16, 512, 128
TT = T // P
EPS = 1e-5
MASKED = -1e30
RSQRT_SEED = 0x5F3759DF

H1, G1, DH1 = 16, 4, 8
J1 = H1 // G1
QK1 = H1 * DH1 + G1 * DH1
QKV1 = QK1 + G1 * DH1
ROWS = P // G1
NEG_MAX = 3 * DH1
SCALE1 = 1.0 / float(np.sqrt(np.float32(DH1)))

CHUNKS = [(3, [g]) for g in range(G1)] + [(2, [g]) for g in range(G1)] + [(1, [0, 1]), (1, [2, 3]), (0, [0, 1, 2, 3])]
NCH = len(CHUNKS)
UNITS = []
for _gp in range(G1 // 2):
    for _g in (2 * _gp, 2 * _gp + 1):
        UNITS += [[(_g, 0, 0)], [(_g, 1, 0), (_g, 3, 384)]]
    UNITS += [[(2 * _gp, 2, 0), (2 * _gp + 1, 2, 256)]]
NU = len(UNITS)
PLACE = {(g, s): (n, c) for n, un in enumerate(UNITS) for g, s, c in un}
UNIT_BANK = [0, 1, 2, 0, 1, 2, 0, 1, 2, 1]
UNIT_BACK = [next(d for d in range(1, NU + 1) if UNIT_BANK[(n - d) % NU] == UNIT_BANK[n]) for n in range(NU)]


def rope_tables():
    d = np.arange(0, DH1, 2, dtype=np.float32) / np.float32(DH1)
    freq = np.exp(-d * np.log(np.float32(10000.0))).astype(np.float32)
    angle = (np.arange(T, dtype=np.float32)[:, None] * freq).astype(np.float32).astype(np.float64)
    cos = np.repeat(np.cos(angle), 2, axis=1)
    sin = np.repeat(np.sin(angle), 2, axis=1) * np.tile([-1.0, 1.0], DH1 // 2)
    lay = lambda a: np.tile(a, (1, QK1 // DH1)).reshape(TT, P, QK1).transpose(1, 0, 2).astype(np.float32)
    return np.ascontiguousarray(lay(cos)), np.ascontiguousarray(lay(sin))


class Tally:

    def __init__(self, parts):
        self.parts = parts
        self.base, self.k = 0, 0

    def body(self, b):
        p1, p2, p3 = self.parts
        self.base = p1 if isinstance(b, int) and b == 0 else b * (p1 + p2 + p3) + (p1 - p3)
        self.k = 0

    def epilogue(self):
        p1, p2, p3 = self.parts
        self.base, self.k = B * (p1 + p2 + p3) - p3, 0

    def check(self, want):
        assert self.k == want, (self.k, want, self.parts)

    def next(self):
        self.k += 1
        return self.base + (self.k - 1)


def skewed(eng, tallies, prologue, body, epilogue):
    prologue()
    for t in tallies:
        t.check(t.parts[0])

    def one(b, slot, first=False, last=False):
        for t in tallies:
            t.body(b)
        body(b, slot, first, last)
        for t in tallies:
            t.check(sum(t.parts) - (t.parts[2] if first else 0) - (t.parts[0] if last else 0))

    one(0, 0, first=True)
    with eng.Fori(1, B - 2, 2) as b:
        one(b, 1)
        one(b + 1, 0)
    one(B - 1, 1, last=True)
    for t in tallies:
        t.epilogue()
    epilogue()


def sandwich_kernel(nc, x, Wq, bq, Wk, bk, Wv, bv, Wo, bo, wqkv, q_scale, k_scale, wo, ln_g, ln_b, w1, b1, w2, b2,
                    cos1, sin1, tab2, out):
    x_v = x.rearrange("b (i p) d -> p b i d", p=P)
    out_v = out.rearrange("b (i p) d -> p b i d", p=P)

    with ExitStack() as whole:
        def sem(name):
            return whole.enter_context(nc.semaphore(name))

        def resident(name, shape, dt=F32):
            return whole.enter_context(nc.sbuf_tensor(name, shape, dt))

        ident = resident("ident", [P, P])
        ident_bf = resident("ident_bf", [P, P], BF16)
        u = resident("u", [P, B, T])

        x1_dram = nc.dram_tensor("x1_scratch", (B, T, D), F32, kind="Internal").ap()
        x1_v = x1_dram.rearrange("b (i p) d -> p b i d", p=P)

        causal_attention(nc, sem, ident, ident_bf, x1_v, u, x_v, Wq, bq, Wk, bk, Wv, bv, Wo, bo, cos1, sin1)
        local_layers(nc, sem, ident, ident_bf, u, wqkv, q_scale, k_scale, wo, ln_g, ln_b, w1, b1, w2, b2, tab2)
        last_norm(nc, sem, ident, u, x1_v, out_v)


def rsqrt_steps(dve, y, v, t):
    seed = [lambda: dve.tensor_scalar(y.bitcast(I32), v.bitcast(I32), 1, None, ALU.logical_shift_right),
            lambda: dve.tensor_scalar(y.bitcast(I32), y.bitcast(I32), -1.0, float(RSQRT_SEED), ALU.mult, ALU.add)]
    newton = [lambda: dve.tensor_tensor(t, y, y, ALU.mult),
              lambda: dve.scalar_tensor_tensor(t, t, -0.5, v, ALU.mult, ALU.mult),
              lambda: dve.scalar_tensor_tensor(y, t, 1.5, y, ALU.add, ALU.mult)]
    return seed + 3 * newton


def rsqrt(dve, step, y, v, t):
    for instruction in rsqrt_steps(dve, y, v, t):
        step(instruction())


def causal_attention(nc, sem, ident, ident_bf, x1_v, u, x_v, Wq, bq, Wk, bk, Wv, bv, Wo, bo, cos1, sin1):
    with ExitStack() as ctx:
        def sb(name, shape, dt=F32):
            return ctx.enter_context(nc.sbuf_tensor("a_" + name, shape, dt))

        def banks(name, n):
            return ctx.enter_context(nc.psum_tensor("a_" + name, [P, n, 512], F32))

        x1 = sb("x1", [P, B, TT, D])
        wqkv = sb("wqkv", [D, QKV1])
        wo = sb("wo", [D, D])
        bqkv = sb("bqkv", [P, QKV1])
        bo_b = sb("bo", [P, D])
        cos = sb("cos", [P, TT, QK1])
        sin = sb("sin", [P, TT, QK1])
        mask_ts = sb("mask_ts", [P, P], BF16)
        mask_st = sb("mask_st", [P, P], BF16)
        xn = sb("xn", [P, TT, D])
        xT = sb("xT", [D, T])
        qkv = sb("qkv", [P, TT, QKV1])
        turned = sb("turned", [P, TT, QK1])
        crossed = sb("crossed", [P, TT, QK1])
        qpack = sb("qpack", [P, 2, TT, J1, G1, ROWS])
        kpack = sb("kpack", [P, TT, G1, ROWS])
        qT = sb("qT", [P, 2, J1, T], F32R)
        qmT = sb("qmT", [P, 2, T], F32R)
        kT = sb("kT", [P, 2, G1, T], F32R)
        v = sb("v", [P, 2, TT, G1, ROWS])
        probs = sb("probs", [P, 2, NU, 512])
        oT = sb("oT", [P, 2, T])
        rden = sb("rden", [P, TT, G1])
        attn = sb("attn", [P, 2, TT, G1, J1, DH1])
        aT = sb("aT", [D, T])
        z = sb("z", [P, TT, D])
        stats_2 = sb("stats", [P, 2, TT, 6])
        mv_2 = sb("mv", [P, 2, TT, 2])
        var_2, rstd_2, tmp_2 = (sb(n, [P, 2, TT]) for n in ("var", "rstd", "tmp"))
        pause = sb("pause", [P, 1])

        s_bank = banks("s", 2)
        st_bank = banks("st", 3)
        o_bank = banks("o", 1)[:, 0]
        act_bank = banks("for_act", 1)[:, 0]
        dve_bank = banks("for_dve", 1)[:, 0]

        (consts_loaded, first_loaded, rest_loaded, consts_made, xn_made, act_bank_filled, act_bank_copied,
         dve_bank_filled, dve_bank_copied, rope_step, high_made, packed, scores_filled, maxed, units_filled,
         probs_made, pv_done, o_copied, attn_made, dve_step, x1_made, x1_stored) = (
            sem("a_" + n) for n in """consts_loaded first_loaded rest_loaded consts_made xn_made act_bank_filled act_bank_copied
            dve_bank_filled dve_bank_copied rope_step high_made packed scores_filled maxed units_filled
            probs_made pv_done o_copied attn_made dve_step x1_made x1_stored""".split())

        LOADS, CONSTS_MADE = 10, 13
        def act_uses():
            return Tally((1 + 1 + 2 + 1, J1 - 1, 2))
        def dve_uses():
            return Tally((2 + 2, J1 - 1, 2))

        def quads(b, slot, first, last, scores, units, tasks):
            def task(name, *args):
                if name in tasks:
                    tasks[name](*args)

            for j in range(J1):
                after = (b, slot, j + 1) if j < J1 - 1 else (b + 1, 1 - slot, 0)
                before = (b, slot, j - 1) if j else (b - 1, 1 - slot, J1 - 1)
                for k in range(NCH):
                    if j < J1 - 1 or not last:
                        for c in CHUNKS_AT[k]:
                            scores(*after, c)
                    if k < NU:
                        units(b, slot, j, k)
                    if (j or not first) and 1 <= k <= TT:
                        task("pv", *before, k - 1)
                    if (j or not first) and k == 6:
                        task("o_copy", *before)
                    if (j or not first) and k == 8:
                        task("o_turn", *before)
                    if not last:
                        for at, name, *args in PART1:
                            if at == (j, k):
                                task(name, b + 1, 1 - slot, *args)
                    if not first:
                        for at, name, *args in PART3:
                            if at == (j, k):
                                task(name, b - 1, 1 - slot, *args)

                    if k == NCH - 1 and (j < J1 - 1 or not last):
                        task("max_turn", *after)

        CHUNKS_AT = [[0, 1], [2, 3]] + [[c] for c in range(4, NCH)] + [[], []]
        pairs = lambda name, first, count, j, k: [((j + (k + n // 2) // NCH, (k + n // 2) % NCH), name, first + n) for n in range(count)]
        PART1 = [*pairs("norm", 0, NORM + 1, 0, 0), ((0, 9), "x_turn"), ((1, 0), "project", 0), ((1, 3), "project", 1), ((1, 4), "rope"),
                 ((1, 10), "high"), ((2, 5), "k_turn"), ((2, 6), "q_turn", 1), ((2, 7), "q_turn", 0), ((2, 8), "q_turn", 3),
                 ((2, 9), "q_turn", 2)]
        PART3 = [((1, 0), "attn_turn"), ((1, 1), "out_project"), ((1, 2), "last_norms", 0), ((1, 3), "last_norms", 1),
                 *pairs("last_norms", 2, 2 * NORM + 2, 1, 4), ((3, 0), "u_turn")]

        def prologue(scores, tasks):
            for _, name, *args in PART1:
                if name in tasks:
                    tasks[name](0, 0, *args)
            for c in range(NCH):
                scores(0, 0, 0, c)
            if "max_turn" in tasks:
                tasks["max_turn"](0, 0, 0)

        def epilogue(tasks):
            for k in range(TT):
                if "pv" in tasks:
                    tasks["pv"](B - 1, 1, J1 - 1, k)
            for name in ("o_copy", "o_turn"):
                if name in tasks:
                    tasks[name](B - 1, 1, J1 - 1)
            for _, name, *args in PART3:
                if name in tasks:
                    tasks[name](B - 1, 1, *args)

        def program(eng, tallies, scores, units, tasks):
            skewed(eng, tallies, lambda: prologue(scores, tasks),
                   lambda b, slot, first, last: quads(b, slot, first, last, scores, units, tasks),
                   lambda: epilogue(tasks))

        nothing = lambda *a: None
        block = ctx.enter_context(nc.Block())

        @block.sync
        def _(sp):
            row = lambda a: a.rearrange("(a n) -> a n", a=1)
            sp.dma_start(x1[:, 0], x_v[:, 0]).then_inc(first_loaded, 16)
            for dst, src in [
                    (wqkv[:, 0:128], Wq), (wqkv[:, 128:160], Wk), (wqkv[:, 160:192], Wv), (wo[:], Wo),
                    (bqkv[:, 0:128], row(bq).to_broadcast([P, 128])), (bqkv[:, 128:160], row(bk).to_broadcast([P, 32])),
                    (bqkv[:, 160:192], row(bv).to_broadcast([P, 32])), (bo_b[:], row(bo).to_broadcast([P, D])),
                    (cos[:], cos1), (sin[:], sin1)]:
                sp.dma_start(dst, src).then_inc(consts_loaded, 16)
            sp.dma_start(x1[:, 1:B], x_v[:, 1:B]).then_inc(rest_loaded, 16)
            with sp.Fori(0, B) as b:
                sp.wait_ge(x1_made, b + 1)
                sp.dma_start(x1_v[:, bass.ds(b, 1)], x1[:, bass.ds(b, 1)]).then_inc(x1_stored, 16)
            sp.wait_ge(x1_stored, 16 * B)

        @block.gpsimd
        def _(pool):
            for t, val in [(ident, 0.0), (ident_bf, 0.0), (mask_ts, 0.0), (mask_st, 0.0), (qpack, 0.0), (kpack, 0.0), (v, 1.0)]:
                pool.memset(t[:], val).then_inc(consts_made, 1)
            pool.memset(kT[:].bitcast(F32), 0.0).then_inc(consts_made, 1)
            pool.wait_ge(consts_made, 8)
            for t in (ident, ident_bf):
                pool.affine_select(out=t[:], in_=t[:], compare_op=ALU.not_equal, fill=1.0, base=0,
                                   pattern=[[-1, P]], channel_multiplier=1).then_inc(consts_made, 1)
            pool.affine_select(out=mask_ts[:], in_=mask_ts[:], compare_op=ALU.is_ge, fill=MASKED, base=0,
                               pattern=[[-1, P]], channel_multiplier=1).then_inc(consts_made, 1)
            pool.affine_select(out=mask_st[:], in_=mask_st[:], compare_op=ALU.is_ge, fill=MASKED, base=0,
                               pattern=[[1, P]], channel_multiplier=-1).then_inc(consts_made, 1)
            pool.memset(kpack[:, :, :, NEG_MAX:NEG_MAX + 1], 1.0).then_inc(consts_made, 1)
            pool.wait_ge(consts_loaded, 16 * LOADS)
            dve = dve_uses()

            def project(b, slot, half):
                dve.next()

            def rope(b, slot):
                pool.wait_ge(dve_bank_copied, dve.base + dve.k)
                pool.tensor_tensor(turned[:], qkv[:, :, 0:QK1], cos[:], ALU.mult).then_inc(rope_step, 1)
                pick = lambda a, e: a.rearrange("p i (n e) -> p i n e", e=2)[:, :, :, e]
                for e in range(2):
                    pool.tensor_tensor(pick(crossed[:], e), pick(qkv[:, :, 0:QK1], 1 - e), pick(sin[:], e),
                                       ALU.mult).then_inc(rope_step, 1)
                pool.wait_ge(rope_step, b * 4 + 3)
                pool.tensor_tensor(turned[:], turned[:], crossed[:], ALU.add).then_inc(rope_step, 1)
                for t in range(TT):
                    last = pool.tensor_copy(v[:, slot, t, :, 0:DH1], qkv[:, t, QK1:QKV1].rearrange("p (g d) -> p g d", g=G1))

            def high(b, slot):
                pool.wait_ge(high_made, (b + 1) * 5)
                for t in range(TT):
                    q = turned[:, t, 0:128].rearrange("p (g j d) -> p j g d", g=G1, j=J1)
                    pool.tensor_tensor(qpack[:, slot, t, :, :, 8:16], q, qpack[:, slot, t, :, :, 0:8], ALU.subtract)
                    pool.memset(qpack[:, slot, t, :, :, NEG_MAX:NEG_MAX + 1], 0.0)
                    pool.tensor_copy(qpack[:, slot, t, :, :, 16:24], qpack[:, slot, t, :, :, 0:8])
                k = turned[:, :, 128:160].rearrange("p i (g d) -> p i g d", g=G1)
                pool.tensor_copy(kpack[:, :, :, 8:16], kpack[:, :, :, 0:8])
                pool.tensor_tensor(kpack[:, :, :, 16:24], k, kpack[:, :, :, 0:8], ALU.subtract).then_inc(packed, 1)

            program(pool, [dve], nothing, nothing, dict(
                project=project, rope=rope, high=high, q_turn=lambda b, s, j: j % 2 and dve.next(),
                o_turn=lambda *a: dve.next(), last_norms=lambda b, s, n: n or dve.next()))

        @block.scalar
        def _(act):
            uses = act_uses()

            def copy_out(dst, src):
                n = uses.next()
                act.wait_ge(act_bank_filled, n + 1)
                act.copy(dst, src).then_inc(act_bank_copied, 1)

            def k_turn(b, slot):
                n = uses.next()
                act.wait_ge(act_bank_filled, n + 1)
                for g in range(G1):
                    r = slice(ROWS * g, ROWS * g + ROWS)
                    last = act.copy(kT[r, slot, g, :], act_bank[r, :])
                last.then_inc(act_bank_copied, 1)

            def units(b, slot, j, k):
                n = (b * J1 + j) * NU + k
                act.wait_ge(units_filled, n + 1)
                act.activation(probs[:, j % 2, k, :], st_bank[:, UNIT_BANK[k], :], ACT.Exp, scale=SCALE1).then_inc(probs_made, 1)

            def o_copy(b, slot, j):
                act.wait_ge(pv_done, b * J1 + j + 1)
                act.copy(oT[:, j % 2, :], o_bank).then_inc(o_copied, 1)

            def u_turn(b, slot):
                n = uses.next()
                act.wait_ge(act_bank_filled, n + 1)
                act.copy(u[:, bass.ds(b, 1), :].rearrange("p a t -> p (a t)"), act_bank).then_inc(act_bank_copied, 1)

            act.wait_ge(consts_made, CONSTS_MADE)
            program(act, [uses], nothing, units, dict(
                max_turn=lambda b, slot, j: copy_out(qmT[:, j % 2, :], act_bank),
                x_turn=lambda b, slot: copy_out(xT[:], act_bank), k_turn=k_turn,
                q_turn=lambda b, slot, j: j % 2 or copy_out(qT[:, slot, j, :], act_bank),
                o_copy=o_copy, attn_turn=lambda b, slot: copy_out(aT[:], act_bank), u_turn=u_turn))

        @block.vector
        def _(dve):
            uses, steps = dve_uses(), Tally((NORM, J1 - 1, 2 * NORM + 4))

            def step(instruction, stats=False):
                n = steps.next()
                if not isinstance(n, int) or n > 0:
                    dve.wait_ge(dve_step, n)
                    if stats:
                        dve.memset(pause[:], 0.0)
                instruction().then_inc(dve_step, 1)

            def each(instruction):
                for t in range(TT):
                    last = instruction(t)
                return last

            def norm_steps(src, which):
                stats, mv, var, rstd, tmp = (a[:, which] for a in (stats_2, mv_2, var_2, rstd_2, tmp_2))
                return [lambda: step(lambda: each(lambda t: dve.bn_stats(stats[:, t, :], src(t))), stats=True),
                        lambda: step(lambda: each(lambda t: dve.bn_aggr(mv[:, t, :], stats[:, t, :])), stats=True),
                        lambda: step(lambda: dve.tensor_scalar(var, mv[:, :, 1], EPS, None, ALU.add)),
                        *[lambda one=one: step(one) for one in rsqrt_steps(dve, rstd, var, tmp)]]

            def normed(dst, src, which, whole=None):
                for t in range(TT):
                    last = dve.tensor_scalar(dst(t), src(t), mv_2[:, which, t, 0:1], rstd_2[:, which, t:t + 1], ALU.subtract, ALU.mult)
                    if whole and not t:
                        last.then_inc(whole, 1)
                return last

            def tokens(b):
                return lambda t: x1[:, bass.ds(b, 1), t, :].rearrange("p a d -> p (a d)")

            def norm(b, slot, n):
                if isinstance(b, int) and n == 0:
                    dve.wait_ge(first_loaded if b == 0 else rest_loaded, 16)
                if n < NORM:
                    norm_steps(tokens(b), 0)[n]()
                    return
                steps_before = steps.base + steps.k
                dve.wait_ge(dve_step, steps_before)
                normed(lambda t: xn[:, t, :], tokens(b), 0).then_inc(xn_made, 1)

            def project(b, slot, half):
                n = uses.next()
                dve.wait_ge(dve_bank_filled, n + 1)
                for t in range(2):
                    last = dve.tensor_tensor(qkv[:, 2 * half + t, :], dve_bank[:, t * QKV1:(t + 1) * QKV1], bqkv[:], ALU.add)
                last.then_inc(dve_bank_copied, 1)

            def high(b, slot):
                dve.wait_ge(rope_step, b * 4 + 4)
                for t in range(TT):
                    dve.tensor_copy(qpack[:, slot, t, :, :, 0:8].bitcast(F32R),
                                    turned[:, t, 0:128].rearrange("p (g j d) -> p j g d", g=G1, j=J1)).then_inc(high_made, 1)
                dve.tensor_copy(kpack[:, :, :, 0:8].bitcast(F32R),
                                turned[:, :, 128:160].rearrange("p i (g d) -> p i g d", g=G1)).then_inc(high_made, 1)

            def q_turn(b, slot, j):
                if j % 2:
                    n = uses.next()
                    dve.wait_ge(dve_bank_filled, n + 1)
                    dve.tensor_copy(qT[:, slot, j, :], dve_bank).then_inc(dve_bank_copied, 1)

            def scores(b, slot, j, c):
                i, gs = CHUNKS[c]
                n = (b * J1 + j) * NCH + c
                dve.wait_ge(scores_filled, n + 1)
                w = (i + 1) * P
                dve.tensor_reduce(qpack[:, slot, i, j, gs[0]:gs[-1] + 1, NEG_MAX],
                                  s_bank[:, (j * NCH + c) % 2, 0:w * len(gs)].rearrange("p (g s) -> p g s", g=len(gs)),
                                  AX, ALU.max, negate=True).then_inc(maxed, 1)

            def o_turn(b, slot, j):
                n = uses.next()
                dve.wait_ge(dve_bank_filled, n + 1)
                o = dve_bank.rearrange("p (i g d) -> p i g d", i=TT, g=G1)
                step(lambda: dve.reciprocal(rden[:], o[:, :, :, DH1]))
                dve.wait_ge(dve_step, steps.base + steps.k)
                for t in range(TT):
                    last = dve.tensor_tensor(attn[:, slot, t, :, j, :], o[:, t, :, 0:DH1],
                                             rden[:, t, :].rearrange("p (g a) -> p g a", a=1).to_broadcast([P, G1, DH1]), ALU.mult)
                last.then_inc(dve_bank_copied, 1)

            def last_norms(b, slot, n):
                if n == 0:
                    m = uses.next()
                    dve.wait_ge(dve_bank_filled, m + 1)
                    dve.tensor_tensor(z[:], dve_bank.rearrange("p (i d) -> p i d", i=TT),
                                      bo_b[:].rearrange("p (a d) -> p a d", a=1).to_broadcast([P, TT, D]), ALU.add).then_inc(dve_bank_copied, 1)
                    return
                if n == 1:
                    dve.wait_ge(dve_bank_copied, uses.base + uses.k)
                zs = lambda t: z[:, t, :]
                row = x1[:, bass.ds(b, 1), :, :].rearrange("p a i d -> p (a i) d")
                chain = [*norm_steps(zs, 1),
                         lambda: step(lambda: normed(zs, zs, 1)),
                         lambda: step(lambda: dve.tensor_tensor(row, row, z[:], ALU.add)),
                         *norm_steps(tokens(b), 1),
                         lambda: step(lambda: normed(zs, tokens(b), 1, x1_made))]
                chain[n - 1]()

            dve.wait_ge(consts_loaded, 16 * LOADS)
            dve.wait_ge(consts_made, CONSTS_MADE)
            program(dve, [uses, steps], scores, nothing, dict(
                norm=norm, project=project, high=high, q_turn=q_turn, o_turn=o_turn, last_norms=last_norms))

        @block.tensor
        def _(pe):
            for_act, for_dve, steps = act_uses(), dve_uses(), Tally((NORM, J1 - 1, 2 * NORM + 4))
            pe.wait_ge(consts_made, CONSTS_MADE)
            pe.wait_ge(consts_loaded, 16 * LOADS)

            def act_turn(src):
                n = for_act.next()
                pe.wait_ge(act_bank_copied, n)
                for t in range(TT):
                    last = pe.transpose(act_bank[:, t * P:(t + 1) * P], src(t), ident[:])
                last.then_inc(act_bank_filled, 1)
                return last

            def x_turn(b, slot):
                pe.wait_ge(xn_made, b + 1)
                act_turn(lambda t: xn[:, t, :])

            def project(b, slot, half):
                pe.wait_ge(act_bank_copied, for_act.base + for_act.k)
                n = for_dve.next()
                pe.wait_ge(dve_bank_copied, n)
                for t in range(2):
                    i = 2 * half + t
                    last = pe.matmul(dve_bank[:, t * QKV1:(t + 1) * QKV1], xT[:, i * P:(i + 1) * P], wqkv[:], start=True, stop=True)
                last.then_inc(dve_bank_filled, 1)

            def k_turn(b, slot):
                pe.wait_ge(packed, b + 1)
                act_turn(lambda t: kpack[:, t, :, :].rearrange("p g r -> p (g r)"))

            def q_turn(b, slot, j):
                src = lambda t: qpack[:, slot, t, j, :, :].rearrange("p g r -> p (g r)")
                if j % 2 == 0:
                    act_turn(src)
                    return
                n = for_dve.next()
                pe.wait_ge(dve_bank_copied, n)
                for t in range(TT):
                    last = pe.transpose(dve_bank[:, t * P:(t + 1) * P], src(t), ident[:])
                last.then_inc(dve_bank_filled, 1)

            def max_turn(b, slot, j):
                pe.wait_ge(maxed, (b * J1 + j + 1) * NCH)
                act_turn(lambda t: qpack[:, slot, t, j, :, :].rearrange("p g r -> p (g r)"))

            def scores(b, slot, j, c):
                i, gs = CHUNKS[c]
                n = (b * J1 + j) * NCH + c
                if isinstance(n, int) and n == 0:
                    pe.wait_ge(act_bank_copied, for_act.base + for_act.k)
                    pe.wait_ge(dve_bank_copied, for_dve.base + for_dve.k)
                elif j == 0 and c == 0:
                    pe.wait_ge(act_bank_copied, for_act.base + for_act.k)
                    pe.wait_ge(dve_bank_copied, for_dve.base + for_dve.k)
                if not isinstance(n, int) or n >= 2:
                    pe.wait_ge(maxed, n - 1)
                w = (i + 1) * P
                bank = s_bank[:, (j * NCH + c) % 2, :]
                for k, g in enumerate(gs):
                    pe.matmul(bank[:, k * w:(k + 1) * w], qT[:, slot, j, i * P:(i + 1) * P], kT[:, slot, g, 0:w], start=True, stop=False)
                    last = pe.matmul(bank[:, k * w + i * P:(k + 1) * w], ident_bf[:], mask_ts[:], start=False, stop=True)
                last.then_inc(scores_filled, 1)

            def units(b, slot, j, k):
                n = (b * J1 + j) * NU + k
                if k == 0:
                    pe.wait_ge(act_bank_copied, for_act.base + for_act.k)
                if not isinstance(n, int) or n >= UNIT_BACK[k]:
                    pe.wait_ge(probs_made, n - UNIT_BACK[k] + 1)
                for g, s, col in UNITS[k]:
                    bank = st_bank[:, UNIT_BANK[k], col:col + T - s * P]
                    pe.matmul(bank, kT[:, slot, g, s * P:(s + 1) * P], qmT[:, j % 2, s * P:T], start=True, stop=False)
                    last = pe.matmul(bank[:, 0:P], ident_bf[:], mask_st[:], start=False, stop=True)
                last.then_inc(units_filled, 1)

            def pv(b, slot, j, s):
                n = b * J1 + j
                if s == 0:
                    pe.wait_ge(probs_made, (n + 1) * NU)
                    if not isinstance(n, int) or n >= 1:
                        pe.wait_ge(o_copied, n)
                for g in range(G1):
                    k, col = PLACE[g, s]
                    r = slice(ROWS * g, ROWS * g + ROWS)
                    last = pe.matmul(o_bank[r, s * P:T], v[:, slot, s, g, :], probs[:, j % 2, k, col:col + T - s * P],
                                     start=(s == 0), stop=(s == TT - 1))
                if s == TT - 1:
                    last.then_inc(pv_done, 1)

            def o_turn(b, slot, j):
                pe.wait_ge(o_copied, b * J1 + j + 1)
                n = for_dve.next()
                pe.wait_ge(dve_bank_copied, n)
                for t in range(TT):
                    last = pe.transpose(dve_bank[:, t * P:(t + 1) * P], oT[:, j % 2, t * P:(t + 1) * P], ident[:])
                last.then_inc(dve_bank_filled, 1)
                steps.next()

            def attn_turn(b, slot):
                pe.wait_ge(dve_bank_copied, for_dve.base + for_dve.k)
                act_turn(lambda t: attn[:, slot, t].rearrange("p g j d -> p (g j d)"))

            def out_project(b, slot):
                pe.wait_ge(act_bank_copied, for_act.base + for_act.k)
                n = for_dve.next()
                pe.wait_ge(dve_bank_copied, n)
                for t in range(TT):
                    last = pe.matmul(dve_bank[:, t * P:(t + 1) * P], aT[:, t * P:(t + 1) * P], wo[:], start=True, stop=True)
                last.then_inc(dve_bank_filled, 1)

            def last_norms(b, slot, n):
                if n:
                    steps.next()

            def u_turn(b, slot):
                pe.wait_ge(dve_step, steps.base + steps.k)
                act_turn(lambda t: z[:, t, :])

            def norm(b, slot, n):
                if n < NORM:
                    steps.next()

            program(pe, [for_act, for_dve, steps], scores, units, dict(
                norm=norm, x_turn=x_turn, project=project, k_turn=k_turn, q_turn=q_turn, max_turn=max_turn, pv=pv,
                o_turn=o_turn, attn_turn=attn_turn, out_project=out_project, last_norms=last_norms, u_turn=u_turn))


DEPTH, HEADS, DH, WIN = 2, 8, 64, 64
INNER = HEADS * DH
PAIRS = HEADS // 2
HID = int(D * 4 * 2 / 3)
HC = -(-HID // P)
HREST = HID - (HC - 1) * P
SPAN = P + WIN
QK_SCALE = 8.0


def xpos_tables():
    half = np.arange(0, DH, 2, dtype=np.float32)
    inv = (np.float32(1.0) / np.power(np.float32(10000.0), half / np.float32(DH))).astype(np.float32)
    t = np.arange(T, dtype=np.float32)
    angle = (t[:, None] * inv[None, :]).astype(np.float32).astype(np.float64)
    base = ((half + 0.4 * DH) / (1.4 * DH)).astype(np.float64)
    scale = base[None, :] ** (((t - T // 2) / float(WIN // 2)).astype(np.float64)[:, None])
    two = lambda a, sign=1.0: np.concatenate([sign * a, a], axis=1)
    q_by, k_by = scale * QK_SCALE, 1.0 / scale
    rows = np.stack([np.stack([two(wave(angle) * q_by, sign), two(wave(angle) * k_by, sign)], axis=1)
                     for wave, sign in ((np.cos, 1.0), (np.sin, -1.0))], axis=1)
    return np.ascontiguousarray(rows.reshape(TT, P, 2, 2, DH).transpose(1, 0, 2, 3, 4).astype(np.float32))


STEPS2 = 2 * HEADS
NORM2 = 2 + 11
USES = {
    "weights": dict(w0=1, w1=1, x=1, dve=1),
    "project": dict(w0=1, w1=1, x=1), "rs": dict(dve=1 + 11), "turn": dict(w0=1, w1=1),
    "recip": dict(dve=3), "den": dict(x=1), "spread": dict(w0=1, w1=1, x=1), "spread_last": dict(x=1), "out": dict(x=1),
    "stat": dict(x=1, dve=NORM2), "rstd": dict(x=1), "gates": dict(w0=1, w1=1, x=1), "values": dict(w0=1, w1=1, x=1),
    "down": dict(x=1),
}
PART1B = [(1, "h"), (2, "low"), (3, "project", 0), (4, "sums", 0), (4, "project", 1), (5, "sums", 1), (6, "project", 2), (7, "sums", 2), (7, "project", 3), (8, "sums", 3), (9, "rs"), (10, "scale", 0), (10, "scale", 1), (11, "scale", 2), (11, "turn", 0), (11, "scale", 3), (12, "turn", 1), (13, "turn", 2), (14, "turn", 3)]
PART3B = [(0, "recip"), (1, "den"), (2, "spread"), (3, "spread_last"), (4, "out"), (5, "shift"), (6, "stat"), (9, "rstd"), (10, "gates"), (11, "values"), (13, "down")]
COUNTED = ("w0", "w1", "x", "dve")
TOTALS = {c: tuple(sum(USES.get(t[1], {}).get(c, 0) for t in part) for part in (PART1B, PART3B)) for c in COUNTED}


class Walk:

    def __init__(self, eng, scores, turn_probs, pv, tasks, copies_first=False):
        self.eng, self.scores, self.turn_probs, self.pv, self.tasks = eng, scores, turn_probs, pv, tasks
        self.copies_first = copies_first
        self.projected = {}
        self.base = dict.fromkeys(COUNTED, 0)
        self.k = dict.fromkeys(COUNTED, 0)

    @property
    def at(self):
        return {c: self.base[c] + self.k[c] for c in COUNTED}

    def task(self, name, l, b, slot, *args):
        if name == "project":
            self.projected[args] = self.at
        if name in self.tasks:
            self.tasks[name](l, b, slot, *args, at=self.projected[args] if name == "sums" else self.at)
        for c, n in USES.get(name, {}).items():
            self.k[c] += n

    def enter(self, l, b):
        for c, (p1, p3) in TOTALS.items():
            w = USES["weights"].get(c, 0)
            self.base[c] = l * (B * (p1 + p3) + w)
            if b is None:
                self.k[c] = 0
            elif isinstance(b, int) and b == 0:
                assert self.k[c] == w + p1
            elif isinstance(b, int):
                self.k[c] = w + b * (p1 + p3) + (p1 if b < B else 0) - p3
            else:
                self.base[c] = self.base[c] + b * (p1 + p3)
                self.k[c] = w + p1 - p3

    def lagging(self, l, b, slot, s, first, lag, do):
        if s >= lag:
            do(l, b, slot, s - lag)
        elif not first:
            do(l, b - 1, 1 - slot, s - lag + STEPS2)

    def body(self, l, b, slot, first=False, last=False):
        self.enter(l, b)
        for s in range(STEPS2):
            for at, name, *args in PART3B:
                if at == s and not first:
                    self.task(name, l, b - 1, 1 - slot, *args)
            self.lagging(l, b, slot, s, first, 2, self.turn_probs)
            if self.copies_first:
                self.lagging(l, b, slot, s, first, 3, self.pv)
            self.scores(l, b, slot, s, at=self.at)
            if not self.copies_first:
                self.lagging(l, b, slot, s, first, 3, self.pv)
            for at, name, *args in PART1B:
                if at == s and not last:
                    self.task(name, l, b + 1, 1 - slot, *args)

    def run(self):
        with self.eng.Fori(0, DEPTH) as l:
            self.enter(l, None)
            self.task("weights", l, 0, 0)
            for _, name, *args in PART1B:
                self.task(name, l, 0, 0, *args)
            self.body(l, 0, 0, first=True)
            with self.eng.Fori(1, B - 2, 2) as b:
                self.body(l, b, 1)
                self.body(l, b + 1, 0)
            self.body(l, B - 1, 1, last=True)
            self.enter(l, B)
            for s in range(STEPS2, STEPS2 + 3):
                if s < STEPS2 + 2:
                    self.turn_probs(l, B - 1, 1, s - 2)
                self.pv(l, B - 1, 1, s - 3)
            for _, name, *args in PART3B:
                self.task(name, l, B - 1, 1, *args)


def local_layers(nc, sem, ident, ident_bf, u, Wqkv, q_scale, k_scale, Wo, ln_g, ln_b, W1, B1, W2, B2, tab2):
    with ExitStack() as ctx:
        def sb(name, shape, dt=F32):
            return ctx.enter_context(nc.sbuf_tensor("b_" + name, shape, dt))

        def banks(name, n):
            return ctx.enter_context(nc.psum_tensor("b_" + name, [P, n, 512], F32))

        w_high = sb("w_high", [D, 3 * INNER], F32R)
        w_low = sb("w_low", [D, 3 * INNER], F32R)
        wo = sb("wo", [P, PAIRS, D])
        w1c = sb("w1c", [D, 2, HC * P])
        w2 = sb("w2", [P, HC, D])
        g_col, b_col = sb("g_col", [D, 1]), sb("b_col", [D, 1])
        bias = sb("bias", [P, 8])
        scales = sb("scales", [P, 2, DH])
        tabs = sb("tabs", [P, TT, 2, 2, DH])
        center = sb("center", [D, D])
        ones = sb("ones", [P, ROWS])
        sel_f = sb("sel_f", [P, 2 * HEADS, DH])
        sel = sb("sel", [P, PAIRS, P], F32R)
        mask_q = sb("mask_q", [P, 2, SPAN], BF16)
        h_high, h_low = sb("h_high", [D, T], F32R), sb("h_low", [D, T], F32R)
        raw = sb("raw", [P, 2, 2, INNER])
        sq = sb("sq", [P, 2, INNER])
        part_b = sb("part_b", [P, 2, INNER])
        qk = sb("qk", [P, TT, 2, INNER])
        ss, rs, tmp = (sb(n, [P, TT * 2 * HEADS]) for n in ("ss", "rs", "tmp"))
        qT = sb("qT", [P, 2, PAIRS, 2, T])
        kT = sb("kT", [P, 2, PAIRS, T])
        v = sb("v", [P, 2, TT, INNER])
        neg_max = sb("neg_max", [P, 2, HEADS, TT])
        dens = sb("dens", [P, 2, HEADS, TT])
        probs = sb("probs", [P, 2, 2, WIN + SPAN])
        pT = sb("pT", [P, 2, 2 * P + 2 * WIN])
        o_raw = sb("o_raw", [P, PAIRS, T])
        rden = sb("rden", [P, HEADS, TT])
        rpack = sb("rpack", [P, TT, P])
        rT = sb("rT", [P, T], F32R)
        oT = sb("oT", [P, PAIRS, T])
        x2 = sb("x2", [D, T])
        h2 = sb("h2", [D, T])
        stats, mv, pause = sb("stats", [P, TT, 6]), sb("mv", [P, TT, 2]), sb("pause", [P, 1])
        var, rstd, tmp4 = (sb(n, [P, TT]) for n in ("var", "rstd", "tmp4"))
        hid = sb("hid", [P, HC, T])
        w_raw = oT[:].rearrange("p c t -> p (c t)")[:, 0:3 * INNER]
        w1g = o_raw[:, 0:2, 0:HID]
        tab = qk[:].rearrange("p i x n -> p (i x n)")[:, 0:TT * 4 * DH].rearrange("p (i s x d) -> p i s x d", i=TT, s=2, x=2)
        idle = raw[:].rearrange("p a x n -> p (a x n)")
        w1 = idle[:, 0:2 * HC * P].rearrange("p (h n) -> p h n", h=2)
        b1r = idle[0:1, 2 * HC * P:4 * HC * P].rearrange("p (h n) -> p h n", h=2)
        b2r = idle[0:1, 4 * HC * P:4 * HC * P + D]

        w_banks = banks("w", 2)
        x_bank = banks("x", 1)[:, 0]
        s_bank = banks("s", 2)
        pt_bank = banks("pt", 2)
        o_bank = banks("o", 1)[:, 0]
        w0_bank, w1_bank = w_banks[:, 0], w_banks[:, 1]

        (consts_made, loaded, w0_filled, w0_freed, w1_filled, w1_freed, x_filled, x_freed, dve_step, high_made,
         low_made, split_made, tabs_made, squared, ss_made, a_made, pool_step, c_made, scaled, scores_filled, maxed,
         probs_made, pt_filled, pt_copied, pv_done, o_copied, h2_made) = (sem("b_" + n) for n in
         """consts_made loaded w0_filled w0_freed w1_filled w1_freed x_filled x_freed dve_step high_made
         low_made split_made tabs_made squared ss_made a_made pool_step c_made scaled scores_filled maxed
         probs_made pt_filled pt_copied pv_done o_copied h2_made""".split())
        work_banks = (("w0", w0_bank), ("w1", w1_bank), ("x", x_bank))
        filled = dict(w0=w0_filled, w1=w1_filled, x=x_filled)
        freed = dict(w0=w0_freed, w1=w1_freed, x=x_freed)
        nothing = lambda *a, **k: None
        seq = lambda l, b: l * B + b
        chunk = lambda l, b, s: seq(l, b) * STEPS2 + s
        at_start = lambda b: isinstance(b, int) and b == 0
        LOADS = 14
        block = ctx.enter_context(nc.Block())

        def ds_u(b, rows, cols):
            return u[rows, bass.ds(b, 1), cols].rearrange("p a t -> p (a t)")

        LOW, UP = slice(0, DH), slice(DH, P)

        def window(k):
            return slice(2 * P + (1 - k) * WIN, 2 * P + (2 - k) * WIN)

        @block.sync
        def _(sp):
            sp.wait_ge(consts_made, CONSTS_MADE)

            def load(l):
                one = lambda a: a[bass.ds(l, 1)]
                loads = [(tab, tab2), (w_raw, one(Wqkv).rearrange("a p n -> (a p) n")),
                         (wo[:], one(Wo).rearrange("a (c p) n -> p (a c) n", p=P)),
                         (w2[0:HREST, HC - 1, :], one(W2)[:, (HC - 1) * P:HID, :].rearrange("a p n -> (a p) n")),
                         (w2[:, 0:HC - 1, :], one(W2)[:, 0:(HC - 1) * P, :].rearrange("a (c p) n -> p (a c) n", p=P)),
                         (b2r, one(B2)),
                         (g_col[:], one(ln_g).rearrange("a (p n) -> (a p) n", n=1)),
                         (b_col[:], one(ln_b).rearrange("a (p n) -> (a p) n", n=1)),
                         (scales[:, 0, :], one(q_scale).to_broadcast([P, DH])),
                         (scales[:, 1, :], one(k_scale).to_broadcast([P, DH]))]
                for half in range(2):
                    loads += [(w1[:, half, 0:HID], one(W1)[:, :, half * HID:(half + 1) * HID].rearrange("a p n -> (a p) n")),
                              (b1r[:, half, 0:HID], one(B1)[:, half * HID:(half + 1) * HID])]
                for dst, src in loads:
                    sp.dma_start(dst, src).then_inc(loaded, 16)
                assert len(loads) == LOADS

            load(0)
            with sp.Fori(1, DEPTH) as l:
                sp.wait_ge(x_freed, l * (B * sum(TOTALS["x"]) + USES["weights"]["x"]))
                load(l)

        @block.gpsimd
        def _(pool):
            zero = [center[:], mask_q[:], qT[:], sel_f[:], probs[:], rpack[:], h_high[:].bitcast(F32),
                    h_low[:].bitcast(F32), h2[:], hid[:], w2[:]]
            for a in zero:
                pool.memset(a, 0.0).then_inc(consts_made, 1)
            pool.memset(ones[:], 1.0).then_inc(consts_made, 1)
            n = len(zero) + 1
            pool.wait_ge(consts_made, n)
            select = lambda a, op, fill, base, pattern, mult: pool.affine_select(
                out=a, in_=a, compare_op=op, fill=fill, base=base, pattern=pattern, channel_multiplier=mult).then_inc(consts_made, 1)
            select(center[:], ALU.not_equal, 1.0, 0, [[-1, D]], 1)
            for half in range(2):
                select(sel_f[:, half * HEADS:(half + 1) * HEADS, :], ALU.not_equal, 1.0, -half * HEADS, [[-1, HEADS], [0, DH]], 1)
            select(mask_q[:], ALU.is_ge, MASKED, 0, [[0, 2], [1, SPAN]], -1)
            pool.wait_ge(consts_made, n + 4)
            select(mask_q[:], ALU.is_ge, MASKED, WIN, [[0, 2], [-1, SPAN]], 1)
            pool.tensor_tensor(sel[:].rearrange("p c n -> p (c n)"), sel_f[:, 0:HEADS, :].rearrange("p h d -> p (h d)"),
                               sel_f[:, HEADS:2 * HEADS, :].rearrange("p h d -> p (h d)"), ALU.add).then_inc(consts_made, 1)
            pool.tensor_scalar(center[:], center[:], -1.0 / D, None, ALU.add).then_inc(consts_made, 1)
            pool.wait_ge(consts_made, n + 7)
            select(mask_q[:, 1, :], ALU.is_ge, MASKED, -WIN, [[1, SPAN]], 0)
            assert n + 8 == CONSTS_MADE, n + 8

            def project(l, b, slot, i, at):
                n = seq(l, b) * TT + i
                pool.wait_ge(w0_freed, at["w0"] + 1)
                pool.wait_ge(w1_freed, at["w1"] + 1)
                if not at_start(b) or i > 0:
                    pool.wait_ge(c_made, n)
                if i == 0 and at_start(b):
                    pool.wait_ge(tabs_made, (l + 1) * 3)
                hd = lambda a, lo: a.rearrange("p x (h d) -> p x h d", d=DH)[:, :, :, lo:lo + DH // 2]
                table = lambda x, lo: tabs[:, i, 1, x, lo:lo + DH // 2].rearrange("p (a d) -> p a d", a=1).to_broadcast([P, HEADS, DH // 2])
                for x in range(2):
                    for lo in (0, DH // 2):
                        last = pool.tensor_tensor(part_b[:, x, :].rearrange("p (h d) -> p h d", d=DH)[:, :, lo:lo + DH // 2],
                                                  raw[:, i % 2, x, :].rearrange("p (h d) -> p h d", d=DH)[:, :, DH // 2 - lo:DH - lo],
                                                  table(x, lo), ALU.mult)
                last.then_inc(pool_step, 1)
                pool.wait_ge(pool_step, n + 1)
                pool.wait_ge(a_made, n + 1)
                pool.tensor_tensor(qk[:, i], qk[:, i], part_b[:], ALU.add).then_inc(c_made, 1)

            Walk(pool, nothing, nothing, nothing, dict(project=project)).run()

        @block.scalar
        def _(act):
            act.wait_ge(consts_made, CONSTS_MADE)

            def weights(l, b, slot, at):
                act.wait_ge(loaded, (l + 1) * LOADS * 16)
                act.copy(w_high[:], w_raw).then_inc(split_made, 1)
                act.wait_ge(w0_filled, at["w0"] + 1)
                act.copy(w1c[:, 0, 0:HID], w0_bank[:, 0:HID]).then_inc(w0_freed, 1)
                act.wait_ge(w1_filled, at["w1"] + 1)
                act.copy(w1c[:, 1, 0:HID], w1_bank[:, 0:HID]).then_inc(w1_freed, 1)

            def h(l, b, slot, at):
                act.copy(h_high[LOW, :], ds_u(b, LOW, slice(0, T))).then_inc(high_made, 1)
                act.copy(h_high[UP, 1:T], ds_u(b, UP, slice(0, T - 1))).then_inc(high_made, 1)

            def project(l, b, slot, i, at):
                n = seq(l, b) * TT + i
                act.wait_ge(x_filled, at["x"] + 1)
                act.copy(v[:, slot, i, :], x_bank).then_inc(x_freed, 1)
                act.wait_ge(w0_filled, at["w0"] + 1)
                act.wait_ge(w1_filled, at["w1"] + 1)
                if not at_start(b) or i >= 1:
                    act.wait_ge(ss_made, n)
                if not at_start(b) or i >= 2:
                    act.wait_ge(a_made, n - 1)
                    act.wait_ge(c_made, n - 1)
                act.activation(sq[:], w_banks[:], ACT.Square).then_inc(squared, 1)
                act.copy(raw[:, i % 2, 0, :], w0_bank).then_inc(w0_freed, 1)
                act.copy(raw[:, i % 2, 1, :], w1_bank).then_inc(w1_freed, 1)

            def turn(l, b, slot, i, at):
                act.wait_ge(w1_filled, at["w1"] + 1)
                act.copy(kT[:, slot, :, i * P:(i + 1) * P],
                         w1_bank.rearrange("p (c t) -> p c t", c=PAIRS)).then_inc(w1_freed, 1)

            def scores(l, b, slot, s, at):
                h, c = divmod(s, 2)
                act.wait_ge(maxed, chunk(l, b, s) + 1)
                for k in range(2):
                    last = act.activation(probs[:, c, k, WIN:WIN + SPAN], s_bank[:, c, k * SPAN:(k + 1) * SPAN], ACT.Exp,
                                          bias=neg_max[:, slot, h, 2 * c + k:2 * c + k + 1],
                                          accum_out=dens[:, slot, h, 2 * c + k:2 * c + k + 1])
                last.then_inc(probs_made, 1)

            def turn_probs(l, b, slot, s):
                c, n = s % 2, chunk(l, b, s)
                act.wait_ge(pt_filled, n + 1)
                if not at_start(b) or s >= 2:
                    act.wait_ge(pv_done, n - 1)
                w = 2 * P + (1 + c) * WIN
                act.copy(pT[:, c, 0:w], pt_bank[:, c, 0:w]).then_inc(pt_copied, 1)

            def pv(l, b, slot, s):
                if s % 4 == 3:
                    act.wait_ge(pv_done, chunk(l, b, s) + 1)
                    act.copy(o_raw[:, s // 4, :], o_bank).then_inc(o_copied, 1)

            def den(l, b, slot, at):
                act.wait_ge(x_filled, at["x"] + 1)
                act.copy(rT[:], x_bank).then_inc(x_freed, 1)

            def shift(l, b, slot, at):
                act.wait_ge(x_freed, at["x"])
                act.copy(h2[LOW, :], x2[LOW, :])
                act.copy(h2[UP, 1:T], x2[UP, 0:T - 1]).then_inc(h2_made, 1)

            def gates(l, b, slot, at):
                for c, (name, bank) in enumerate(work_banks):
                    act.wait_ge(filled[name], at[name] + 1)
                    r = slice(0, P if c < HC - 1 else HREST)
                    act.activation(hid[r, c, :], bank[r, :], ACT.Gelu, bias=bias[r, HC + c:HC + c + 1]).then_inc(freed[name], 1)

            Walk(act, scores, turn_probs, pv, dict(weights=weights, h=h, project=project, turn=turn, den=den,
                                                   shift=shift, gates=gates), copies_first=True).run()

        @block.vector
        def _(dve):
            dve.wait_ge(consts_made, CONSTS_MADE)

            class Steps:
                def __init__(self, at):
                    self.n = at["dve"]

                def __call__(self, instruction):
                    instruction.then_inc(dve_step, 1)
                    self.n = self.n + 1
                    dve.wait_ge(dve_step, self.n)

            def weights(l, b, slot, at):
                step = Steps(at)
                dve.wait_ge(loaded, (l + 1) * LOADS * 16)
                step(dve.tensor_scalar(w1g, w1[:, :, 0:HID], g_col[:], None, ALU.mult))
                dve.wait_ge(split_made, l * 2 + 1)
                dve.tensor_tensor(w_low[:], w_raw, w_high[:].bitcast(F32), ALU.subtract).then_inc(split_made, 1)
                for i in range(TT):
                    last = dve.tensor_tensor(tabs[:, i, 0], tab[:, i, 0], scales[:], ALU.mult)
                last.then_inc(tabs_made, 1)
                for lo in (0, DH // 2):
                    for i in range(TT):
                        last = dve.tensor_tensor(tabs[:, i, 1, :, lo:lo + DH // 2], tab[:, i, 1, :, lo:lo + DH // 2],
                                                 scales[:, :, DH // 2 - lo:DH - lo], ALU.mult)
                    last.then_inc(tabs_made, 1)
                dve.wait_ge(tabs_made, (l + 1) * 3)
                dve.wait_ge(x_filled, at["x"] + 1)
                for first in (0, HC):
                    dve.tensor_copy(bias[:, first:first + HC - 1], x_bank[:, first:first + HC - 1])
                    dve.tensor_copy(bias[0:HREST, first + HC - 1:first + HC], x_bank[0:HREST, first + HC - 1:first + HC])
                dve.tensor_copy(bias[:, 6:7], x_bank[:, 6:7]).then_inc(x_freed, 1)

            def low(l, b, slot, at):
                dve.wait_ge(high_made, seq(l, b) * 2 + 2)
                dve.tensor_tensor(h_low[LOW, :], ds_u(b, LOW, slice(0, T)), h_high[LOW, :].bitcast(F32), ALU.subtract)
                dve.tensor_tensor(h_low[UP, 1:T], ds_u(b, UP, slice(0, T - 1)), h_high[UP, 1:T].bitcast(F32),
                                  ALU.subtract).then_inc(low_made, 1)

            def sums(l, b, slot, i, at):
                n = seq(l, b) * TT + i
                dve.wait_ge(squared, n + 1)
                dve.tensor_reduce(ss[:, i * 16:(i + 1) * 16], sq[:].rearrange("p x (h d) -> p (x h) d", d=DH),
                                  AX, ALU.add).then_inc(ss_made, 1)
                dve.wait_ge(w0_freed, at["w0"] + 1)
                dve.wait_ge(w1_freed, at["w1"] + 1)
                for x in range(2):
                    last = dve.tensor_tensor(qk[:, i, x, :].rearrange("p (h d) -> p h d", d=DH),
                                             raw[:, i % 2, x, :].rearrange("p (h d) -> p h d", d=DH),
                                             tabs[:, i, 0, x, :].rearrange("p (a d) -> p a d", a=1).to_broadcast([P, HEADS, DH]), ALU.mult)
                last.then_inc(a_made, 1)

            def rs_(l, b, slot, at):
                step = Steps(at)
                dve.wait_ge(ss_made, seq(l, b) * TT + TT)
                step(dve.tensor_scalar(ss[:], ss[:], 1e-24, None, ALU.max))
                rsqrt(dve, step, rs[:], ss[:], tmp[:])

            def scale(l, b, slot, i, at):
                n = seq(l, b) * TT + i
                dve.wait_ge(c_made, n + 1)
                a = qk[:, i].rearrange("p x (h d) -> p (x h) d", d=DH)
                dve.tensor_tensor(a, a, rs[:, i * 16:(i + 1) * 16].rearrange("p (h a) -> p h a", a=1).to_broadcast([P, 16, DH]),
                                  ALU.mult).then_inc(scaled, 1)

            def turn(l, b, slot, i, at):
                dve.wait_ge(w0_filled, at["w0"] + 1)
                for a, r in enumerate((LOW, UP)):
                    last = dve.tensor_copy(qT[r, slot, :, a, i * P:(i + 1) * P], w0_bank[r, :].rearrange("p (c t) -> p c t", c=PAIRS))
                last.then_inc(w0_freed, 1)

            def scores(l, b, slot, s, at):
                h, c = divmod(s, 2)
                dve.wait_ge(scores_filled, chunk(l, b, s) + 1)
                dve.tensor_reduce(neg_max[:, slot, h, 2 * c:2 * c + 2], s_bank[:, c, 0:2 * SPAN].rearrange("p (i k) -> p i k", i=2),
                                  AX, ALU.max, negate=True).then_inc(maxed, 1)

            def recip(l, b, slot, at):
                step = Steps(at)
                dve.wait_ge(probs_made, chunk(l, b, STEPS2))
                step(dve.reciprocal(rden[:], dens[:, slot]))
                high = rpack[:, :, 0:HEADS].rearrange("p i h -> p h i")
                step(dve.tensor_copy(high.bitcast(F32R), rden[:]))
                step(dve.tensor_tensor(rpack[:, :, HEADS:2 * HEADS].rearrange("p i h -> p h i"), rden[:], high, ALU.subtract))

            def normed(p, l, b, at, bank, name):
                dve.wait_ge(o_copied, seq(l, b) * PAIRS + p + 1)
                dve.wait_ge(filled[name], at[name] + 1)
                dve.tensor_tensor(oT[:, p, :], o_raw[:, p, :], bank, ALU.mult).then_inc(freed[name], 1)

            def spread(l, b, slot, at):
                for p, (name, bank) in enumerate(work_banks):
                    normed(p, l, b, at, bank, name)

            def spread_last(l, b, slot, at):
                normed(PAIRS - 1, l, b, at, x_bank, "x")

            def out(l, b, slot, at):
                dve.wait_ge(x_filled, at["x"] + 1)
                dve.tensor_tensor(x2[:], ds_u(b, slice(0, P), slice(0, T)), x_bank, ALU.add).then_inc(x_freed, 1)

            def stat(l, b, slot, at):
                step = Steps(at)
                dve.wait_ge(x_filled, at["x"] + 1)
                for i in range(TT):
                    last = dve.bn_stats(stats[:, i, :], x_bank[:, i * P:(i + 1) * P])
                last.then_inc(x_freed, 1)
                dve.wait_ge(x_freed, at["x"] + 1)
                dve.memset(pause[:], 0.0)
                for i in range(TT):
                    last = dve.bn_aggr(mv[:, i, :], stats[:, i, :])
                step(last)
                step(dve.tensor_scalar(var[:], mv[:, :, 1], EPS, None, ALU.add))
                rsqrt(dve, step, rstd[:], var[:], tmp4[:])

            def rstd_(l, b, slot, at):
                dve.wait_ge(x_filled, at["x"] + 1)
                dve.wait_ge(h2_made, seq(l, b) + 1)
                dve.tensor_tensor(h2[:], h2[:], x_bank, ALU.mult).then_inc(x_freed, 1)

            def values(l, b, slot, at):
                for c, (name, bank) in enumerate(work_banks):
                    dve.wait_ge(filled[name], at[name] + 1)
                    r = slice(0, P if c < HC - 1 else HREST)
                    dve.scalar_tensor_tensor(hid[r, c, :], bank[r, :], bias[r, c:c + 1], hid[r, c, :], ALU.add,
                                             ALU.mult).then_inc(freed[name], 1)

            def down(l, b, slot, at):
                dve.wait_ge(x_filled, at["x"] + 1)
                dve.scalar_tensor_tensor(ds_u(b, slice(0, P), slice(0, T)), x_bank, bias[:, 6:7], x2[:], ALU.add,
                                         ALU.add).then_inc(x_freed, 1)

            Walk(dve, scores, nothing, nothing, dict(weights=weights, low=low, sums=sums, rs=rs_, scale=scale, turn=turn,
                 recip=recip, spread=spread, spread_last=spread_last, out=out, stat=stat, rstd=rstd_, values=values, down=down)).run()

        @block.tensor
        def _(pe):
            pe.wait_ge(consts_made, CONSTS_MADE)

            def weights(l, b, slot, at):
                pe.wait_ge(loaded, (l + 1) * LOADS * 16)
                for half in range(2):
                    for c in range(HC):
                        r = P if c < HC - 1 else HREST
                        col = x_bank[0:r, half * HC + c:half * HC + c + 1]
                        pe.matmul(col, w1[:, half, c * P:c * P + r], b_col[:], start=True, stop=False)
                        pe.matmul(col, b1r[:, half, c * P:c * P + r], ones[0:1, 0:1], start=False, stop=True)
                pe.matmul(x_bank[:, 6:7], b2r, ones[0:1, 0:1], start=True, stop=True).then_inc(x_filled, 1)
                pe.wait_ge(dve_step, at["dve"] + 1)
                pe.matmul(w0_bank[:, 0:HID], center[:], w1g[:, 0, :], start=True, stop=True).then_inc(w0_filled, 1)
                pe.matmul(w1_bank[:, 0:HID], center[:], w1g[:, 1, :], start=True, stop=True).then_inc(w1_filled, 1)
                pe.wait_ge(split_made, l * 2 + 2)

            def project(l, b, slot, i, at):
                if i == 0:
                    pe.wait_ge(low_made, seq(l, b) + 1)
                t = slice(i * P, (i + 1) * P)
                for o, name, bank in ((2, "x", x_bank), (0, "w0", w0_bank), (1, "w1", w1_bank)):
                    pe.wait_ge(freed[name], at[name])
                    cols = slice(o * INNER, (o + 1) * INNER)
                    pe.matmul(bank, h_high[:, t], w_high[:, cols], start=True, stop=False)
                    pe.matmul(bank, h_high[:, t], w_low[:, cols], start=False, stop=False)
                    pe.matmul(bank, h_low[:, t], w_high[:, cols], start=False, stop=True).then_inc(filled[name], 1)

            def turn(l, b, slot, i, at):
                pe.wait_ge(scaled, seq(l, b) * TT + i + 1)
                for x, (o, fl) in enumerate(((w0_bank, w0_filled), (w1_bank, w1_filled))):
                    pe.wait_ge((w0_freed, w1_freed)[x], at[("w0", "w1")[x]])
                    for p in range(PAIRS):
                        last = pe.transpose(o[:, p * P:(p + 1) * P], qk[:, i, x, p * P:(p + 1) * P], ident[:])
                    last.then_inc(fl, 1)

            def scores(l, b, slot, s, at):
                h, c = divmod(s, 2)
                if s == 0:
                    pe.wait_ge(w0_freed, at["w0"])
                    pe.wait_ge(w1_freed, at["w1"])
                if not at_start(b) or s >= 2:
                    pe.wait_ge(probs_made, chunk(l, b, s) - 1)
                for k in range(2):
                    i = 2 * c + k
                    out = s_bank[:, c, k * SPAN:(k + 1) * SPAN]
                    pe.matmul(out, ident_bf[:], mask_q[:, int(i == 0), :], start=True, stop=False)
                    before = WIN if i else 0
                    last = pe.matmul(out[:, WIN - before:SPAN], qT[:, slot, h // 2, h % 2, i * P:(i + 1) * P],
                                     kT[:, slot, h // 2, i * P - before:(i + 1) * P], start=False, stop=True)
                last.then_inc(scores_filled, 1)

            def turn_probs(l, b, slot, s):
                h, c = divmod(s, 2)
                n = chunk(l, b, s)
                pe.wait_ge(probs_made, n + 1)
                if not at_start(b) or s >= 2:
                    pe.wait_ge(pt_copied, n - 1)
                for k in range(2):
                    last = pe.transpose(pt_bank[:, c, k * P:(k + 1) * P], probs[:, c, k, P:2 * P], ident[:])
                    if c or k:
                        last = pe.transpose(pt_bank[:, c, window(k)], probs[0:WIN, c, k, 0:P], ident[0:WIN, 0:WIN])
                last.then_inc(pt_filled, 1)

            def pv(l, b, slot, s):
                h, c = divmod(s, 2)
                pe.wait_ge(pt_copied, chunk(l, b, s) + 1)
                if s % 4 == 0 and not (at_start(b) and s == 0):
                    pe.wait_ge(o_copied, seq(l, b) * PAIRS + s // 4)
                rows = (LOW, UP)[h % 2]
                for k in range(2):
                    i = 2 * c + k
                    vh = lambda tile: v[:, slot, tile, h * DH:(h + 1) * DH]
                    last = pe.matmul(o_bank[rows, i * P:(i + 1) * P], vh(i), pT[:, c, k * P:(k + 1) * P], start=True,
                                     stop=(i == 0), skip_group_check=True)
                    if i:
                        last = pe.matmul(o_bank[rows, i * P:i * P + WIN], vh(i - 1), pT[:, c, window(k)], start=False,
                                         stop=True, skip_group_check=True)
                last.then_inc(pv_done, 1)

            def den(l, b, slot, at):
                pe.wait_ge(dve_step, at["dve"])
                pe.wait_ge(x_freed, at["x"])
                for i in range(TT):
                    last = pe.transpose(x_bank[:, i * P:(i + 1) * P], rpack[:, i, :], ident[:])
                last.then_inc(x_filled, 1)

            def spread_pair(p, at, bank, name):
                pe.wait_ge(freed[name], at[name])
                pe.matmul(bank, sel[:, p, :], rT[:], start=True, stop=True).then_inc(filled[name], 1)

            def spread(l, b, slot, at):
                pe.wait_ge(x_freed, at["x"])
                for p, (name, bank) in enumerate(work_banks):
                    spread_pair(p, at, bank, name)

            def spread_last(l, b, slot, at):
                spread_pair(PAIRS - 1, at, x_bank, "x")

            def out(l, b, slot, at):
                pe.wait_ge(x_freed, at["x"])
                for p in range(PAIRS):
                    last = pe.matmul(x_bank, wo[:, p, :], oT[:, p, :], start=(p == 0), stop=(p == PAIRS - 1))
                last.then_inc(x_filled, 1)

            def stat(l, b, slot, at):
                pe.wait_ge(h2_made, seq(l, b) + 1)
                pe.wait_ge(x_freed, at["x"])
                for i in range(TT):
                    last = pe.transpose(x_bank[:, i * P:(i + 1) * P], h2[:, i * P:(i + 1) * P], ident[:])
                last.then_inc(x_filled, 1)

            def rstd_(l, b, slot, at):
                pe.wait_ge(dve_step, at["dve"])
                pe.wait_ge(x_freed, at["x"])
                for i in range(TT):
                    last = pe.transpose(x_bank[:, i * P:(i + 1) * P], rstd[:, i:i + 1].to_broadcast([P, P]), ident[:])
                last.then_inc(x_filled, 1)

            def up(half, at):
                for c, (name, bank) in enumerate(work_banks):
                    pe.wait_ge(freed[name], at[name])
                    r = P if c < HC - 1 else HREST
                    pe.matmul(bank[0:r, :], w1c[:, half, c * P:c * P + r], h2[:], start=True, stop=True).then_inc(filled[name], 1)

            def gates(l, b, slot, at):
                pe.wait_ge(x_freed, at["x"])
                up(1, at)

            def values(l, b, slot, at):
                up(0, at)

            def down(l, b, slot, at):
                pe.wait_ge(x_freed, at["x"])
                for c in range(HC):
                    last = pe.matmul(x_bank, w2[:, c, :], hid[:, c, :], start=(c == 0), stop=(c == HC - 1))
                last.then_inc(x_filled, 1)

            Walk(pe, scores, turn_probs, pv, dict(weights=weights, project=project, turn=turn, den=den,
                 spread=spread, spread_last=spread_last, out=out, stat=stat, rstd=rstd_, gates=gates, values=values, down=down)).run()


CONSTS_MADE = 20


def last_norm(nc, sem, ident, u, x1_v, out_v):
    with ExitStack() as ctx:
        sb = lambda name, shape: ctx.enter_context(nc.sbuf_tensor("c_" + name, shape, F32))
        uf = sb("uf", [D, 2, T])
        x1 = sb("x1", [P, B, TT, D])
        y = sb("y", [P, 2, TT, D])
        stats = sb("stats", [P, TT, 6])
        mv = sb("mv", [P, TT, 2])
        var, rstd, tmp = (sb(n, [P, TT]) for n in ("var", "rstd", "tmp"))
        pause = sb("pause", [P, 1])
        bank = ctx.enter_context(nc.psum_tensor("c_bank", [P, 2, TT, D], F32))
        x1_loaded, copied, turned, dve_step, made = (sem("c_" + n) for n in "x1_loaded copied turned dve_step made".split())
        stored = [sem(f"c_stored_{slot}") for slot in range(2)]
        STEPS = 3 + 11 + 1
        block = ctx.enter_context(nc.Block())

        def twice(eng, one):
            one(0, 0)
            one(1, 1)
            with eng.Fori(2, B - 1, 2) as b:
                one(b, 0)
                one(b + 1, 1)

        @block.sync
        def _(sp):
            sp.dma_start(x1[:], x1_v).then_inc(x1_loaded, 16)

            def one(b, slot):
                sp.wait_ge(made, b + 1)
                sp.dma_start(out_v[:, bass.ds(b, 1)], y[:, slot:slot + 1]).then_inc(stored[slot], 16)
            twice(sp, one)
            for slot in range(2):
                sp.wait_ge(stored[slot], 16 * B // 2)

        @block.scalar
        def _(act):
            def one(b, slot):
                if not isinstance(b, int):
                    act.wait_ge(turned, b - 1)
                act.copy(uf[:, slot, :], u[:, bass.ds(b, 1), :].rearrange("p a t -> p (a t)")).then_inc(copied, 1)
            twice(act, one)

        @block.tensor
        def _(pe):
            def one(b, slot):
                pe.wait_ge(copied, b + 1)
                if not isinstance(b, int):
                    pe.wait_ge(made, b - 1)
                for i in range(TT):
                    last = pe.transpose(bank[:, slot, i, :], uf[:, slot, i * P:(i + 1) * P], ident[:])
                last.then_inc(turned, 1)
            twice(pe, one)

        @block.vector
        def _(dve):
            dve.wait_ge(x1_loaded, 16)

            def one(b, slot):
                count = [b * STEPS]

                def step(instruction, then_stats=False):
                    instruction.then_inc(dve_step, 1)
                    count[0] = count[0] + 1
                    dve.wait_ge(dve_step, count[0])
                    if then_stats:
                        dve.memset(pause[:], 0.0)

                dve.wait_ge(turned, b + 1)
                dve.memset(pause[:], 0.0)
                for i in range(TT):
                    last = dve.bn_stats(stats[:, i, :], bank[:, slot, i, :])
                step(last, then_stats=True)
                for i in range(TT):
                    last = dve.bn_aggr(mv[:, i, :], stats[:, i, :])
                step(last)
                step(dve.tensor_scalar(var[:], mv[:, :, 1], EPS, None, ALU.add))
                rsqrt(dve, step, rstd[:], var[:], tmp[:])
                if not isinstance(b, int):
                    dve.wait_ge(stored[slot], (b - slot) * 8)
                for i in range(TT):
                    last = dve.tensor_scalar(y[:, slot, i, :], bank[:, slot, i, :], mv[:, i, 0:1], rstd[:, i:i + 1],
                                             ALU.subtract, ALU.mult)
                step(last)
                dve.tensor_tensor(y[:, slot], y[:, slot], x1[:, bass.ds(b, 1)].rearrange("p a i d -> p (a i) d"),
                                  ALU.add).then_inc(made, 1)
            twice(dve, one)


NORM = 3 + 11


_INS = ['L0_attn_x', 'L0_attn_Wq', 'L0_attn_bq', 'L0_attn_Wk', 'L0_attn_bk', 'L0_attn_Wv', 'L0_attn_bv', 'L0_attn_Wo', 'L0_attn_bo',
        'L0_ffn_wqkv', 'L0_ffn_q_scale', 'L0_ffn_k_scale', 'L0_ffn_wo', 'L0_ffn_ln_g', 'L0_ffn_ln_b', 'L0_ffn_w1', 'L0_ffn_b1',
        'L0_ffn_w2', 'L0_ffn_b2']


def kernel(**inputs):
    import numpy as _np
    import concourse.bacc as _bacc
    from concourse import mybir as _mybir
    from concourse.bass_utils import run_bass_kernel_spmd as _run

    nc = _bacc.Bacc("TRN2", target_bir_lowering=False, num_devices=1)
    arrays = {f"in_{n}": _np.ascontiguousarray(inputs[n]) for n in _INS}
    arrays["cos1"], arrays["sin1"] = rope_tables()
    arrays["tab2"] = xpos_tables()
    args = [nc.dram_tensor(n, a.shape, _mybir.dt.from_np(a.dtype), kind="ExternalInput").ap() for n, a in arrays.items()]
    args.append(nc.dram_tensor("out_0", (B, T, D), _mybir.dt.float32, kind="ExternalOutput").ap())
    sandwich_kernel(nc, *args)
    r = _run(nc, [arrays], core_ids=[0])
    return r.results[0]["out_0"]
```

```python
from contextlib import ExitStack

import numpy as np
import concourse.bass as bass
from concourse import mybir

F32 = mybir.dt.float32
F32R = mybir.dt.float32r
BF16 = mybir.dt.bfloat16
I32 = mybir.dt.int32
ALU = mybir.AluOpType
ACT = mybir.ActivationFunctionType
AX = mybir.AxisListType.X

P = 128
B, T, D = 16, 512, 128
TT = T // P
EPS = 1e-5
MASKED = -1e30
RSQRT_SEED = 0x5F3759DF
NORM = 3 + 11

H1, G1, DH1 = 16, 4, 8
J1 = H1 // G1
QK1 = H1 * DH1 + G1 * DH1
QKV1 = QK1 + G1 * DH1
ROWS = P // G1
NEG_MAX = 3 * DH1
SCALE1 = 1.0 / float(np.sqrt(np.float32(DH1)))

CHUNKS = [(3, [g]) for g in range(G1)] + [(2, [g]) for g in range(G1)] + [(1, [0, 1]), (1, [2, 3]), (0, [0, 1, 2, 3])]
NCH = len(CHUNKS)
UNITS = []
for _gp in range(G1 // 2):
    for _g in (2 * _gp, 2 * _gp + 1):
        UNITS += [[(_g, 0, 0)], [(_g, 1, 0), (_g, 3, 384)]]
    UNITS += [[(2 * _gp, 2, 0), (2 * _gp + 1, 2, 256)]]
NU = len(UNITS)
PLACE = {(g, s): (n, c) for n, un in enumerate(UNITS) for g, s, c in un}
UNIT_BANK = [0, 1, 2, 0, 1, 2, 0, 1, 2, 1]
UNIT_BACK = [next(d for d in range(1, NU + 1) if UNIT_BANK[(n - d) % NU] == UNIT_BANK[n]) for n in range(NU)]


def rope_tables():
    d = np.arange(0, DH1, 2, dtype=np.float32) / np.float32(DH1)
    freq = np.exp(-d * np.log(np.float32(10000.0))).astype(np.float32)
    angle = (np.arange(T, dtype=np.float32)[:, None] * freq).astype(np.float32).astype(np.float64)
    cos = np.repeat(np.cos(angle), 2, axis=1)
    sin = np.repeat(np.sin(angle), 2, axis=1) * np.tile([-1.0, 1.0], DH1 // 2)
    lay = lambda a: np.tile(a, (1, QK1 // DH1)).reshape(TT, P, QK1).transpose(1, 0, 2).astype(np.float32)
    return np.ascontiguousarray(lay(cos)), np.ascontiguousarray(lay(sin))


class Tally:

    def __init__(self, parts):
        self.parts = parts
        self.base, self.k = 0, 0

    def body(self, b):
        p1, p2, p3 = self.parts
        self.base = p1 if isinstance(b, int) and b == 0 else b * (p1 + p2 + p3) + (p1 - p3)
        self.k = 0

    def epilogue(self):
        p1, p2, p3 = self.parts
        self.base, self.k = B * (p1 + p2 + p3) - p3, 0

    def check(self, want):
        assert self.k == want, (self.k, want, self.parts)

    def next(self):
        self.k += 1
        return self.base + (self.k - 1)


def skewed(eng, tallies, prologue, body, epilogue):
    prologue()
    for t in tallies:
        t.check(t.parts[0])

    def one(b, slot, first=False, last=False):
        for t in tallies:
            t.body(b)
        body(b, slot, first, last)
        for t in tallies:
            t.check(sum(t.parts) - (t.parts[2] if first else 0) - (t.parts[0] if last else 0))

    one(0, 0, first=True)
    with eng.Fori(1, B - 2, 2) as b:
        one(b, 1)
        one(b + 1, 0)
    one(B - 1, 1, last=True)
    for t in tallies:
        t.epilogue()
    epilogue()


def sandwich_kernel(nc, x, Wq, bq, Wk, bk, Wv, bv, Wo, bo, wqkv, q_scale, k_scale, wo, ln_g, ln_b, w1, b1, w2, b2,
                    cos1, sin1, tab2, out):
    x_v = x.rearrange("b (i p) d -> p b i d", p=P)
    out_v = out.rearrange("b (i p) d -> p b i d", p=P)

    with ExitStack() as whole:
        def sem(name):
            return whole.enter_context(nc.semaphore(name))

        def resident(name, shape, dt=F32):
            return whole.enter_context(nc.sbuf_tensor(name, shape, dt))

        ident = resident("ident", [P, P])
        ident_bf = resident("ident_bf", [P, P], BF16)
        u = resident("u", [P, B, T])

        x1_dram = nc.dram_tensor("x1_scratch", (B, T, D), F32, kind="Internal").ap()
        x1_v = x1_dram.rearrange("b (i p) d -> p b i d", p=P)

        causal_attention(nc, sem, ident, ident_bf, x1_v, u, x_v, Wq, bq, Wk, bk, Wv, bv, Wo, bo, cos1, sin1)
        local_layers(nc, sem, ident, ident_bf, u, wqkv, q_scale, k_scale, wo, ln_g, ln_b, w1, b1, w2, b2, tab2)
        last_norm(nc, sem, ident, u, x1_v, out_v)


def rsqrt_steps(dve, y, v, t):
    seed = [lambda: dve.tensor_scalar(y.bitcast(I32), v.bitcast(I32), 1, None, ALU.logical_shift_right),
            lambda: dve.tensor_scalar(y.bitcast(I32), y.bitcast(I32), -1.0, float(RSQRT_SEED), ALU.mult, ALU.add)]
    newton = [lambda: dve.tensor_tensor(t, y, y, ALU.mult),
              lambda: dve.scalar_tensor_tensor(t, t, -0.5, v, ALU.mult, ALU.mult),
              lambda: dve.scalar_tensor_tensor(y, t, 1.5, y, ALU.add, ALU.mult)]
    return seed + 3 * newton


def rsqrt(dve, step, y, v, t):
    for instruction in rsqrt_steps(dve, y, v, t):
        step(instruction())


def causal_attention(nc, sem, ident, ident_bf, x1_v, u, x_v, Wq, bq, Wk, bk, Wv, bv, Wo, bo, cos1, sin1):
    with ExitStack() as ctx:
        def sb(name, shape, dt=F32):
            return ctx.enter_context(nc.sbuf_tensor("a_" + name, shape, dt))

        def banks(name, n):
            return ctx.enter_context(nc.psum_tensor("a_" + name, [P, n, 512], F32))

        x1 = sb("x1", [P, B, TT, D])
        wqkv = sb("wqkv", [D, QKV1])
        wo = sb("wo", [D, D])
        bqkv = sb("bqkv", [P, QKV1])
        bo_b = sb("bo", [P, D])
        cos = sb("cos", [P, TT, QK1])
        sin = sb("sin", [P, TT, QK1])
        mask_ts = sb("mask_ts", [P, P], BF16)
        mask_st = sb("mask_st", [P, P], BF16)
        xn = sb("xn", [P, TT, D])
        xT = sb("xT", [D, T])
        qkv = sb("qkv", [P, TT, QKV1])
        turned = sb("turned", [P, TT, QK1])
        crossed = sb("crossed", [P, TT, QK1])
        qpack = sb("qpack", [P, 2, TT, J1, G1, ROWS])
        kpack = sb("kpack", [P, TT, G1, ROWS])
        qT = sb("qT", [P, 2, J1, T], F32R)
        qmT = sb("qmT", [P, 2, T], F32R)
        kT = sb("kT", [P, 2, G1, T], F32R)
        v = sb("v", [P, 2, TT, G1, ROWS])
        probs = sb("probs", [P, 2, NU, 512])
        oT = sb("oT", [P, 2, T])
        rden = sb("rden", [P, TT, G1])
        attn = sb("attn", [P, 2, TT, G1, J1, DH1])
        aT = sb("aT", [D, T])
        z = sb("z", [P, TT, D])
        stats_2 = sb("stats", [P, 2, TT, 6])
        mv_2 = sb("mv", [P, 2, TT, 2])
        var_2, rstd_2, tmp_2 = (sb(n, [P, 2, TT]) for n in ("var", "rstd", "tmp"))
        pause = sb("pause", [P, 1])

        s_bank = banks("s", 2)
        st_bank = banks("st", 3)
        o_bank = banks("o", 1)[:, 0]
        act_bank = banks("for_act", 1)[:, 0]
        dve_bank = banks("for_dve", 1)[:, 0]

        (consts_loaded, first_loaded, rest_loaded, consts_made, xn_made, act_bank_filled, act_bank_copied,
         dve_bank_filled, dve_bank_copied, rope_step, high_made, packed, scores_filled, maxed, units_filled,
         probs_made, pv_done, o_copied, dve_step, x1_made, x1_stored) = (
            sem("a_" + n) for n in """consts_loaded first_loaded rest_loaded consts_made xn_made act_bank_filled act_bank_copied
            dve_bank_filled dve_bank_copied rope_step high_made packed scores_filled maxed units_filled
            probs_made pv_done o_copied dve_step x1_made x1_stored""".split())

        LOADS, CONSTS_MADE = 10, 13
        def act_uses():
            return Tally((1 + 1 + 2 + 1, J1 - 1, 2))
        def dve_uses():
            return Tally((2 + 2, J1 - 1, 2))

        def quads(b, slot, first, last, scores, units, tasks):
            def task(name, *args):
                if name in tasks:
                    tasks[name](*args)

            for j in range(J1):
                after = (b, slot, j + 1) if j < J1 - 1 else (b + 1, 1 - slot, 0)
                before = (b, slot, j - 1) if j else (b - 1, 1 - slot, J1 - 1)
                for k in range(NCH):
                    if j < J1 - 1 or not last:
                        for c in CHUNKS_AT[k]:
                            scores(*after, c)
                    if k < NU:
                        units(b, slot, j, k)
                    if (j or not first) and 1 <= k <= TT:
                        task("pv", *before, k - 1)
                    if (j or not first) and k == 6:
                        task("o_copy", *before)
                    if (j or not first) and k == 8:
                        task("o_turn", *before)
                    if not last:
                        for at, name, *args in PART1:
                            if at == j * NCH + k:
                                task(name, b + 1, 1 - slot, *args)
                    if not first:
                        for at, name, *args in PART3:
                            if at == j * NCH + k:
                                task(name, b - 1, 1 - slot, *args)

                    if k == NCH - 1 and (j < J1 - 1 or not last):
                        task("max_turn", *after)

        CHUNKS_AT = [[0, 1], [2], [3, 4], [5], [6], [7], [8], [9], [10], [], []]
        pairs = lambda name, first, count, place: [(place + n // 2, name, first + n) for n in range(count)]
        PART1 = [*pairs("norm", 0, NORM + 1, 0), (9, "x_turn"), (9, "project", 0), (12, "project", 1), (15, "rope"),
                 (19, "high"), (25, "k_turn"), (26, "q_turn", 1), (27, "q_turn", 0), (28, "q_turn", 3), (29, "q_turn", 2)]
        PART3 = [(11, "attn_turn"), (13, "out_project"), (13, "last_norms", 0), (14, "last_norms", 1),
                 *pairs("last_norms", 2, 2 * NORM + 2, 17), (33, "u_turn")]

        def prologue(scores, tasks):
            for _, name, *args in PART1:
                if name in tasks:
                    tasks[name](0, 0, *args)
            for c in range(NCH):
                scores(0, 0, 0, c)
            if "max_turn" in tasks:
                tasks["max_turn"](0, 0, 0)

        def epilogue(tasks):
            for k in range(TT):
                if "pv" in tasks:
                    tasks["pv"](B - 1, 1, J1 - 1, k)
            for name in ("o_copy", "o_turn"):
                if name in tasks:
                    tasks[name](B - 1, 1, J1 - 1)
            for _, name, *args in PART3:
                if name in tasks:
                    tasks[name](B - 1, 1, *args)

        def program(eng, tallies, scores, units, tasks):
            skewed(eng, tallies, lambda: prologue(scores, tasks),
                   lambda b, slot, first, last: quads(b, slot, first, last, scores, units, tasks),
                   lambda: epilogue(tasks))

        nothing = lambda *a: None
        block = ctx.enter_context(nc.Block())

        @block.sync
        def _(sp):
            row = lambda a: a.rearrange("(a n) -> a n", a=1)
            sp.dma_start(x1[:, 0], x_v[:, 0]).then_inc(first_loaded, 16)
            for dst, src in [
                    (wqkv[:, 0:128], Wq), (wqkv[:, 128:160], Wk), (wqkv[:, 160:192], Wv), (wo[:], Wo),
                    (bqkv[:, 0:128], row(bq).to_broadcast([P, 128])), (bqkv[:, 128:160], row(bk).to_broadcast([P, 32])),
                    (bqkv[:, 160:192], row(bv).to_broadcast([P, 32])), (bo_b[:], row(bo).to_broadcast([P, D])),
                    (cos[:], cos1), (sin[:], sin1)]:
                sp.dma_start(dst, src).then_inc(consts_loaded, 16)
            sp.dma_start(x1[:, 1:B], x_v[:, 1:B]).then_inc(rest_loaded, 16)
            with sp.Fori(0, B) as b:
                sp.wait_ge(x1_made, b + 1)
                sp.dma_start(x1_v[:, bass.ds(b, 1)], x1[:, bass.ds(b, 1)]).then_inc(x1_stored, 16)
            sp.wait_ge(x1_stored, 16 * B)

        @block.gpsimd
        def _(pool):
            for t, val in [(ident, 0.0), (ident_bf, 0.0), (mask_ts, 0.0), (mask_st, 0.0), (qpack, 0.0), (kpack, 0.0), (v, 1.0)]:
                pool.memset(t[:], val).then_inc(consts_made, 1)
            pool.memset(kT[:].bitcast(F32), 0.0).then_inc(consts_made, 1)
            pool.wait_ge(consts_made, 8)
            for t in (ident, ident_bf):
                pool.affine_select(out=t[:], in_=t[:], compare_op=ALU.not_equal, fill=1.0, base=0,
                                   pattern=[[-1, P]], channel_multiplier=1).then_inc(consts_made, 1)
            pool.affine_select(out=mask_ts[:], in_=mask_ts[:], compare_op=ALU.is_ge, fill=MASKED, base=0,
                               pattern=[[-1, P]], channel_multiplier=1).then_inc(consts_made, 1)
            pool.affine_select(out=mask_st[:], in_=mask_st[:], compare_op=ALU.is_ge, fill=MASKED, base=0,
                               pattern=[[1, P]], channel_multiplier=-1).then_inc(consts_made, 1)
            pool.memset(kpack[:, :, :, NEG_MAX:NEG_MAX + 1], 1.0).then_inc(consts_made, 1)
            pool.wait_ge(consts_loaded, 16 * LOADS)
            dve = dve_uses()

            def project(b, slot, half):
                dve.next()

            def rope(b, slot):
                pool.wait_ge(dve_bank_copied, dve.base + dve.k)
                pool.tensor_tensor(turned[:], qkv[:, :, 0:QK1], cos[:], ALU.mult).then_inc(rope_step, 1)
                pick = lambda a, e: a.rearrange("p i (n e) -> p i n e", e=2)[:, :, :, e]
                for e in range(2):
                    pool.tensor_tensor(pick(crossed[:], e), pick(qkv[:, :, 0:QK1], 1 - e), pick(sin[:], e),
                                       ALU.mult).then_inc(rope_step, 1)
                pool.wait_ge(rope_step, b * 4 + 3)
                pool.tensor_tensor(turned[:], turned[:], crossed[:], ALU.add).then_inc(rope_step, 1)
                for t in range(TT):
                    last = pool.tensor_copy(v[:, slot, t, :, 0:DH1], qkv[:, t, QK1:QKV1].rearrange("p (g d) -> p g d", g=G1))

            def high(b, slot):
                pool.wait_ge(high_made, (b + 1) * 5)
                for t in range(TT):
                    q = turned[:, t, 0:128].rearrange("p (g j d) -> p j g d", g=G1, j=J1)
                    pool.tensor_tensor(qpack[:, slot, t, :, :, 8:16], q, qpack[:, slot, t, :, :, 0:8], ALU.subtract)
                    pool.memset(qpack[:, slot, t, :, :, NEG_MAX:NEG_MAX + 1], 0.0)
                    pool.tensor_copy(qpack[:, slot, t, :, :, 16:24], qpack[:, slot, t, :, :, 0:8])
                k = turned[:, :, 128:160].rearrange("p i (g d) -> p i g d", g=G1)
                pool.tensor_copy(kpack[:, :, :, 8:16], kpack[:, :, :, 0:8])
                pool.tensor_tensor(kpack[:, :, :, 16:24], k, kpack[:, :, :, 0:8], ALU.subtract).then_inc(packed, 1)

            program(pool, [dve], nothing, nothing, dict(
                project=project, rope=rope, high=high, q_turn=lambda b, s, j: j % 2 and dve.next(),
                o_turn=lambda *a: dve.next(), last_norms=lambda b, s, n: n or dve.next()))

        @block.scalar
        def _(act):
            uses = act_uses()

            def copy_out(dst, src):
                n = uses.next()
                act.wait_ge(act_bank_filled, n + 1)
                act.copy(dst, src).then_inc(act_bank_copied, 1)

            def k_turn(b, slot):
                n = uses.next()
                act.wait_ge(act_bank_filled, n + 1)
                for g in range(G1):
                    r = slice(ROWS * g, ROWS * g + ROWS)
                    last = act.copy(kT[r, slot, g, :], act_bank[r, :])
                last.then_inc(act_bank_copied, 1)

            def units(b, slot, j, k):
                n = (b * J1 + j) * NU + k
                act.wait_ge(units_filled, n + 1)
                act.activation(probs[:, j % 2, k, :], st_bank[:, UNIT_BANK[k], :], ACT.Exp, scale=SCALE1).then_inc(probs_made, 1)

            def o_copy(b, slot, j):
                act.wait_ge(pv_done, b * J1 + j + 1)
                act.copy(oT[:, j % 2, :], o_bank).then_inc(o_copied, 1)

            def u_turn(b, slot):
                n = uses.next()
                act.wait_ge(act_bank_filled, n + 1)
                act.copy(u[:, bass.ds(b, 1), :].rearrange("p a t -> p (a t)"), act_bank).then_inc(act_bank_copied, 1)

            act.wait_ge(consts_made, CONSTS_MADE)
            program(act, [uses], nothing, units, dict(
                max_turn=lambda b, slot, j: copy_out(qmT[:, j % 2, :], act_bank),
                x_turn=lambda b, slot: copy_out(xT[:], act_bank), k_turn=k_turn,
                q_turn=lambda b, slot, j: j % 2 or copy_out(qT[:, slot, j, :], act_bank),
                o_copy=o_copy, attn_turn=lambda b, slot: copy_out(aT[:], act_bank), u_turn=u_turn))

        @block.vector
        def _(dve):
            uses, steps = dve_uses(), Tally((NORM, J1 - 1, 2 * NORM + 4))

            def step(instruction, stats=False):
                n = steps.next()
                if not isinstance(n, int) or n > 0:
                    dve.wait_ge(dve_step, n)
                    if stats:
                        dve.memset(pause[:], 0.0)
                instruction().then_inc(dve_step, 1)

            def each(instruction):
                for t in range(TT):
                    last = instruction(t)
                return last

            def norm_steps(src, which):
                stats, mv, var, rstd, tmp = (a[:, which] for a in (stats_2, mv_2, var_2, rstd_2, tmp_2))
                return [lambda: step(lambda: each(lambda t: dve.bn_stats(stats[:, t, :], src(t))), stats=True),
                        lambda: step(lambda: each(lambda t: dve.bn_aggr(mv[:, t, :], stats[:, t, :])), stats=True),
                        lambda: step(lambda: dve.tensor_scalar(var, mv[:, :, 1], EPS, None, ALU.add)),
                        *[lambda one=one: step(one) for one in rsqrt_steps(dve, rstd, var, tmp)]]

            def normed(dst, src, which, whole=None):
                for t in range(TT):
                    last = dve.tensor_scalar(dst(t), src(t), mv_2[:, which, t, 0:1], rstd_2[:, which, t:t + 1], ALU.subtract, ALU.mult)
                    if whole and not t:
                        last.then_inc(whole, 1)
                return last

            def tokens(b):
                return lambda t: x1[:, bass.ds(b, 1), t, :].rearrange("p a d -> p (a d)")

            def norm(b, slot, n):
                if isinstance(b, int) and n == 0:
                    dve.wait_ge(first_loaded if b == 0 else rest_loaded, 16)
                if n < NORM:
                    norm_steps(tokens(b), 0)[n]()
                    return
                steps_before = steps.base + steps.k
                dve.wait_ge(dve_step, steps_before)
                normed(lambda t: xn[:, t, :], tokens(b), 0).then_inc(xn_made, 1)

            def project(b, slot, half):
                n = uses.next()
                dve.wait_ge(dve_bank_filled, n + 1)
                for t in range(2):
                    last = dve.tensor_tensor(qkv[:, 2 * half + t, :], dve_bank[:, t * QKV1:(t + 1) * QKV1], bqkv[:], ALU.add)
                last.then_inc(dve_bank_copied, 1)

            def high(b, slot):
                dve.wait_ge(rope_step, b * 4 + 4)
                for t in range(TT):
                    dve.tensor_copy(qpack[:, slot, t, :, :, 0:8].bitcast(F32R),
                                    turned[:, t, 0:128].rearrange("p (g j d) -> p j g d", g=G1, j=J1)).then_inc(high_made, 1)
                dve.tensor_copy(kpack[:, :, :, 0:8].bitcast(F32R),
                                turned[:, :, 128:160].rearrange("p i (g d) -> p i g d", g=G1)).then_inc(high_made, 1)

            def q_turn(b, slot, j):
                if j % 2:
                    n = uses.next()
                    dve.wait_ge(dve_bank_filled, n + 1)
                    dve.tensor_copy(qT[:, slot, j, :], dve_bank).then_inc(dve_bank_copied, 1)

            def scores(b, slot, j, c):
                i, gs = CHUNKS[c]
                n = (b * J1 + j) * NCH + c
                dve.wait_ge(scores_filled, n + 1)
                w = (i + 1) * P
                dve.tensor_reduce(qpack[:, slot, i, j, gs[0]:gs[-1] + 1, NEG_MAX],
                                  s_bank[:, (j * NCH + c) % 2, 0:w * len(gs)].rearrange("p (g s) -> p g s", g=len(gs)),
                                  AX, ALU.max, negate=True).then_inc(maxed, 1)

            def o_turn(b, slot, j):
                n = uses.next()
                dve.wait_ge(dve_bank_filled, n + 1)
                o = dve_bank.rearrange("p (i g d) -> p i g d", i=TT, g=G1)
                step(lambda: dve.reciprocal(rden[:], o[:, :, :, DH1]))
                dve.wait_ge(dve_step, steps.base + steps.k)
                for t in range(TT):
                    last = dve.tensor_tensor(attn[:, slot, t, :, j, :], o[:, t, :, 0:DH1],
                                             rden[:, t, :].rearrange("p (g a) -> p g a", a=1).to_broadcast([P, G1, DH1]), ALU.mult)
                last.then_inc(dve_bank_copied, 1)

            def last_norms(b, slot, n):
                if n == 0:
                    m = uses.next()
                    dve.wait_ge(dve_bank_filled, m + 1)
                    dve.tensor_tensor(z[:], dve_bank.rearrange("p (i d) -> p i d", i=TT),
                                      bo_b[:].rearrange("p (a d) -> p a d", a=1).to_broadcast([P, TT, D]), ALU.add).then_inc(dve_bank_copied, 1)
                    return
                if n == 1:
                    dve.wait_ge(dve_bank_copied, uses.base + uses.k)
                zs = lambda t: z[:, t, :]
                row = x1[:, bass.ds(b, 1), :, :].rearrange("p a i d -> p (a i) d")
                chain = [*norm_steps(zs, 1),
                         lambda: step(lambda: normed(zs, zs, 1)),
                         lambda: step(lambda: dve.tensor_tensor(row, row, z[:], ALU.add)),
                         *norm_steps(tokens(b), 1),
                         lambda: step(lambda: normed(zs, tokens(b), 1, x1_made))]
                chain[n - 1]()

            dve.wait_ge(consts_loaded, 16 * LOADS)
            dve.wait_ge(consts_made, CONSTS_MADE)
            program(dve, [uses, steps], scores, nothing, dict(
                norm=norm, project=project, high=high, q_turn=q_turn, o_turn=o_turn, last_norms=last_norms))

        @block.tensor
        def _(pe):
            for_act, for_dve, steps = act_uses(), dve_uses(), Tally((NORM, J1 - 1, 2 * NORM + 4))
            pe.wait_ge(consts_made, CONSTS_MADE)
            pe.wait_ge(consts_loaded, 16 * LOADS)

            def act_turn(src):
                n = for_act.next()
                pe.wait_ge(act_bank_copied, n)
                for t in range(TT):
                    last = pe.transpose(act_bank[:, t * P:(t + 1) * P], src(t), ident[:])
                last.then_inc(act_bank_filled, 1)
                return last

            def x_turn(b, slot):
                pe.wait_ge(xn_made, b + 1)
                act_turn(lambda t: xn[:, t, :])

            def project(b, slot, half):
                pe.wait_ge(act_bank_copied, for_act.base + for_act.k)
                n = for_dve.next()
                pe.wait_ge(dve_bank_copied, n)
                for t in range(2):
                    i = 2 * half + t
                    last = pe.matmul(dve_bank[:, t * QKV1:(t + 1) * QKV1], xT[:, i * P:(i + 1) * P], wqkv[:], start=True, stop=True)
                last.then_inc(dve_bank_filled, 1)

            def k_turn(b, slot):
                pe.wait_ge(packed, b + 1)
                act_turn(lambda t: kpack[:, t, :, :].rearrange("p g r -> p (g r)"))

            def q_turn(b, slot, j):
                src = lambda t: qpack[:, slot, t, j, :, :].rearrange("p g r -> p (g r)")
                if j % 2 == 0:
                    act_turn(src)
                    return
                n = for_dve.next()
                pe.wait_ge(dve_bank_copied, n)
                for t in range(TT):
                    last = pe.transpose(dve_bank[:, t * P:(t + 1) * P], src(t), ident[:])
                last.then_inc(dve_bank_filled, 1)

            def max_turn(b, slot, j):
                pe.wait_ge(maxed, (b * J1 + j + 1) * NCH)
                act_turn(lambda t: qpack[:, slot, t, j, :, :].rearrange("p g r -> p (g r)"))

            def scores(b, slot, j, c):
                i, gs = CHUNKS[c]
                n = (b * J1 + j) * NCH + c
                if j == 0 and c == 0:
                    pe.wait_ge(act_bank_copied, for_act.base + for_act.k)
                    pe.wait_ge(dve_bank_copied, for_dve.base + for_dve.k)
                if not isinstance(n, int) or n >= 2:
                    pe.wait_ge(maxed, n - 1)
                w = (i + 1) * P
                bank = s_bank[:, (j * NCH + c) % 2, :]
                for k, g in enumerate(gs):
                    pe.matmul(bank[:, k * w:(k + 1) * w], qT[:, slot, j, i * P:(i + 1) * P], kT[:, slot, g, 0:w], start=True, stop=False)
                    last = pe.matmul(bank[:, k * w + i * P:(k + 1) * w], ident_bf[:], mask_ts[:], start=False, stop=True)
                last.then_inc(scores_filled, 1)

            def units(b, slot, j, k):
                n = (b * J1 + j) * NU + k
                if k == 0:
                    pe.wait_ge(act_bank_copied, for_act.base + for_act.k)
                if not isinstance(n, int) or n >= UNIT_BACK[k]:
                    pe.wait_ge(probs_made, n - UNIT_BACK[k] + 1)
                for g, s, col in UNITS[k]:
                    bank = st_bank[:, UNIT_BANK[k], col:col + T - s * P]
                    pe.matmul(bank, kT[:, slot, g, s * P:(s + 1) * P], qmT[:, j % 2, s * P:T], start=True, stop=False)
                    last = pe.matmul(bank[:, 0:P], ident_bf[:], mask_st[:], start=False, stop=True)
                last.then_inc(units_filled, 1)

            def pv(b, slot, j, s):
                n = b * J1 + j
                if s == 0:
                    pe.wait_ge(probs_made, (n + 1) * NU)
                    if not isinstance(n, int) or n >= 1:
                        pe.wait_ge(o_copied, n)
                for g in range(G1):
                    k, col = PLACE[g, s]
                    r = slice(ROWS * g, ROWS * g + ROWS)
                    last = pe.matmul(o_bank[r, s * P:T], v[:, slot, s, g, :], probs[:, j % 2, k, col:col + T - s * P],
                                     start=(s == 0), stop=(s == TT - 1))
                if s == TT - 1:
                    last.then_inc(pv_done, 1)

            def o_turn(b, slot, j):
                pe.wait_ge(o_copied, b * J1 + j + 1)
                n = for_dve.next()
                pe.wait_ge(dve_bank_copied, n)
                for t in range(TT):
                    last = pe.transpose(dve_bank[:, t * P:(t + 1) * P], oT[:, j % 2, t * P:(t + 1) * P], ident[:])
                last.then_inc(dve_bank_filled, 1)
                steps.next()

            def attn_turn(b, slot):
                pe.wait_ge(dve_bank_copied, for_dve.base + for_dve.k)
                act_turn(lambda t: attn[:, slot, t].rearrange("p g j d -> p (g j d)"))

            def out_project(b, slot):
                pe.wait_ge(act_bank_copied, for_act.base + for_act.k)
                n = for_dve.next()
                pe.wait_ge(dve_bank_copied, n)
                for t in range(TT):
                    last = pe.matmul(dve_bank[:, t * P:(t + 1) * P], aT[:, t * P:(t + 1) * P], wo[:], start=True, stop=True)
                last.then_inc(dve_bank_filled, 1)

            def last_norms(b, slot, n):
                if n:
                    steps.next()

            def u_turn(b, slot):
                pe.wait_ge(dve_step, steps.base + steps.k)
                act_turn(lambda t: z[:, t, :])

            def norm(b, slot, n):
                if n < NORM:
                    steps.next()

            program(pe, [for_act, for_dve, steps], scores, units, dict(
                norm=norm, x_turn=x_turn, project=project, k_turn=k_turn, q_turn=q_turn, max_turn=max_turn, pv=pv,
                o_turn=o_turn, attn_turn=attn_turn, out_project=out_project, last_norms=last_norms, u_turn=u_turn))


DEPTH, HEADS, DH, WIN = 2, 8, 64, 64
INNER = HEADS * DH
PAIRS = HEADS // 2
HID = int(D * 4 * 2 / 3)
HC = -(-HID // P)
HREST = HID - (HC - 1) * P
SPAN = P + WIN
QK_SCALE = 8.0


def xpos_tables():
    half = np.arange(0, DH, 2, dtype=np.float32)
    inv = (np.float32(1.0) / np.power(np.float32(10000.0), half / np.float32(DH))).astype(np.float32)
    t = np.arange(T, dtype=np.float32)
    angle = (t[:, None] * inv[None, :]).astype(np.float32).astype(np.float64)
    base = ((half + 0.4 * DH) / (1.4 * DH)).astype(np.float64)
    scale = base[None, :] ** (((t - T // 2) / float(WIN // 2)).astype(np.float64)[:, None])
    two = lambda a, sign=1.0: np.concatenate([sign * a, a], axis=1)
    q_by, k_by = scale * QK_SCALE, 1.0 / scale
    rows = np.stack([np.stack([two(wave(angle) * q_by, sign), two(wave(angle) * k_by, sign)], axis=1)
                     for wave, sign in ((np.cos, 1.0), (np.sin, -1.0))], axis=1)
    return np.ascontiguousarray(rows.reshape(TT, P, 2, 2, DH).transpose(1, 0, 2, 3, 4).astype(np.float32))


STEPS2 = 2 * HEADS
NORM2 = 2 + 11
USES = {
    "weights_ffn": dict(w0=1, w1=1, x=1, dve=1),
    "project": dict(w0=1, w1=1, x=1), "rs": dict(dve=1 + 11), "turn": dict(w0=1, w1=1),
    "recip": dict(dve=3), "den": dict(x=1), "spread": dict(w0=1, w1=1, x=1), "spread_last": dict(x=1), "out": dict(x=1),
    "stat": dict(x=1, dve=NORM2), "rstd": dict(x=1), "gates": dict(w0=1, w1=1, x=1), "values": dict(w0=1, w1=1, x=1),
    "down": dict(x=1),
}
PART1B = [(1, "h"), (2, "low"), (3, "project", 0), (4, "sums", 0), (4, "project", 1), (5, "sums", 1),
          (5, "project", 2), (7, "sums", 2), (7, "project", 3), (9, "sums", 3), (9, "rs"), (9, "scale", 0),
          (11, "scale", 1), (11, "scale", 2), (11, "turn", 0), (12, "turn", 1), (12, "scale", 3), (13, "turn", 2),
          (14, "turn", 3)]
PART3B = [(0, "recip"), (1, "den"), (2, "spread"), (3, "spread_last"), (4, "out"), (4, "shift"), (7, "stat"),
          (9, "rstd"), (10, "gates"), (11, "values"), (12, "down")]
COUNTED = ("w0", "w1", "x", "dve")
TOTALS = {c: tuple(sum(USES.get(t[1], {}).get(c, 0) for t in part) for part in (PART1B, PART3B)) for c in COUNTED}


class Walk:

    def __init__(self, eng, scores, turn_probs, pv, tasks, copies_first=False, sequences=True):
        self.eng, self.scores, self.turn_probs, self.pv, self.tasks = eng, scores, turn_probs, pv, tasks
        self.copies_first = copies_first
        self.sequences = sequences
        self.projected = {}
        self.base = dict.fromkeys(COUNTED, 0)
        self.k = dict.fromkeys(COUNTED, 0)

    @property
    def at(self):
        return {c: self.base[c] + self.k[c] for c in COUNTED}

    def task(self, name, l, b, slot, *args):
        if name == "project":
            self.projected[args] = self.at
        if name in self.tasks:
            self.tasks[name](l, b, slot, *args, at=self.projected[args] if name == "sums" else self.at)
        for c, n in USES.get(name, {}).items():
            self.k[c] += n

    def enter(self, l, b, after_last=False):
        for c, (p1, p3) in TOTALS.items():
            w = USES["weights_ffn"].get(c, 0)
            whole = p1 + p3
            early = isinstance(b, int) and b == 0 and not (isinstance(l, int) and l == 0)
            self.base[c] = l * (B * whole + w)
            self.k[c] = 0 if early else w
            if isinstance(b, int):
                self.k[c] += b * whole
            else:
                self.base[c] = self.base[c] + b * whole
            first = isinstance(l, int) and isinstance(b, int) and l == b == 0
            self.k[c] += (0 if after_last else p1) - (0 if first else p3)

    def lagging(self, here, before, slot, s, lag, do):
        if s >= lag:
            do(*here, slot, s - lag)
        elif before:
            do(*before, 1 - slot, s - lag + STEPS2)

    def body(self, here, slot, before, after):
        self.enter(*here)
        ends = before and isinstance(here[1], int) and here[1] == B - 1 and after
        begins = before and isinstance(here[1], int) and here[1] == 0
        for s in range(STEPS2):
            if ends and s == 0:
                self.task("load_attn", *after, slot)
            if ends and s == 2:
                self.task("weights_attn", *after, slot)
            for at, name, *args in PART3B:
                if at == s and before:
                    self.task(name, *before, 1 - slot, *args)
                    if begins and name == "out":
                        self.task("load_ffn", *here, slot)
                    if begins and name == "down":
                        self.task("load_products", *here, slot)
            self.lagging(here, before, slot, s, 2, self.turn_probs)
            if self.copies_first:
                self.lagging(here, before, slot, s, 3, self.pv)
            self.scores(*here, slot, s, at=self.at)
            if not self.copies_first:
                self.lagging(here, before, slot, s, 3, self.pv)
            for at, name, *args in PART1B:
                if at == s and after:
                    self.task(name, *after, 1 - slot, *args)
        if begins:
            self.task("weights_ffn", *here, slot)

    def layer(self, l):
        if self.sequences:
            with self.eng.Fori(1, B - 2, 2) as b:
                self.body((l, b), 1, (l, b - 1), (l, b + 1))
                self.body((l, b + 1), 0, (l, b), (l, b + 2))

    def run(self):
        for name in ("load_attn", "load_ffn", "load_products", "weights_attn", "weights_ffn"):
            self.task(name, 0, 0, 0)
        for _, name, *args in PART1B:
            self.task(name, 0, 0, 0, *args)
        self.body((0, 0), 0, None, (0, 1))
        with self.eng.Fori(0, DEPTH - 1) as l:
            self.layer(l)
            self.body((l, B - 1), 1, (l, B - 2), (l + 1, 0))
            self.body((l + 1, 0), 0, (l, B - 1), (l + 1, 1))
        l = DEPTH - 1
        self.layer(l)
        self.body((l, B - 1), 1, (l, B - 2), None)
        self.enter(l, B, after_last=True)
        for s in range(STEPS2, STEPS2 + 3):
            if s < STEPS2 + 2:
                self.turn_probs(l, B - 1, 1, s - 2)
            self.pv(l, B - 1, 1, s - 3)
        for _, name, *args in PART3B:
            self.task(name, l, B - 1, 1, *args)


def local_layers(nc, sem, ident, ident_bf, u, Wqkv, q_scale, k_scale, Wo, ln_g, ln_b, W1, B1, W2, B2, tab2):
    with ExitStack() as ctx:
        def sb(name, shape, dt=F32):
            return ctx.enter_context(nc.sbuf_tensor("b_" + name, shape, dt))

        def banks(name, n):
            return ctx.enter_context(nc.psum_tensor("b_" + name, [P, n, 512], F32))

        w_high = sb("w_high", [D, 3 * INNER], F32R)
        w_low = sb("w_low", [D, 3 * INNER], F32R)
        wo = sb("wo", [P, PAIRS, D])
        w1c = sb("w1c", [D, 2, HC * P])
        w2 = sb("w2", [P, HC, D])
        g_col, b_col = sb("g_col", [D, 1]), sb("b_col", [D, 1])
        bias = sb("bias", [P, 8])
        scales = sb("scales", [P, 2, DH])
        tabs = sb("tabs", [P, TT, 2, 2, DH])
        center = sb("center", [D, D])
        ones = sb("ones", [P, ROWS])
        sel_f = sb("sel_f", [P, 2 * HEADS, DH])
        sel = sb("sel", [P, PAIRS, P], F32R)
        mask_q = sb("mask_q", [P, 2, SPAN], BF16)
        h_high, h_low = sb("h_high", [D, T], F32R), sb("h_low", [D, T], F32R)
        raw = sb("raw", [P, 2, 2, INNER])
        sq = sb("sq", [P, 2, INNER])
        part_b = sb("part_b", [P, 2, INNER])
        qk = sb("qk", [P, TT, 2, INNER])
        ss, rs, tmp = (sb(n, [P, TT * 2 * HEADS]) for n in ("ss", "rs", "tmp"))
        qT = sb("qT", [P, 2, PAIRS, 2, T])
        kT = sb("kT", [P, 2, PAIRS, T])
        v = sb("v", [P, 2, TT, INNER])
        neg_max = sb("neg_max", [P, 2, HEADS, TT])
        dens = sb("dens", [P, 2, HEADS, TT])
        probs = sb("probs", [P, 2, 2, WIN + SPAN])
        pT = sb("pT", [P, 2, 2 * P + 2 * WIN])
        o_raw = sb("o_raw", [P, PAIRS, T])
        rden = sb("rden", [P, HEADS, TT])
        rpack = sb("rpack", [P, TT, P])
        rT = sb("rT", [P, T], F32R)
        oT = sb("oT", [P, PAIRS, T])
        x2 = sb("x2", [D, T])
        h2 = sb("h2", [D, T])
        stats, mv, pause = sb("stats", [P, TT, 6]), sb("mv", [P, TT, 2]), sb("pause", [P, 1])
        var, rstd, tmp4 = (sb(n, [P, TT]) for n in ("var", "rstd", "tmp4"))
        hid = sb("hid", [P, HC, T])
        idle = qk[:].rearrange("p i x n -> p (i x n)")
        tab = idle[:, 0:TT * 4 * DH].rearrange("p (i s x d) -> p i s x d", i=TT, s=2, x=2)
        w_raw = idle[:, TT * 4 * DH:TT * 4 * DH + 3 * INNER]
        idle = oT[:].rearrange("p c t -> p (c t)")
        w1 = idle[:, 0:2 * HC * P].rearrange("p (h n) -> p h n", h=2)
        b1r = idle[0:1, 2 * HC * P:4 * HC * P].rearrange("p (h n) -> p h n", h=2)
        b2r = idle[0:1, 4 * HC * P:4 * HC * P + D]

        w_banks = banks("w", 2)
        x_bank = banks("x", 1)[:, 0]
        s_bank = banks("s", 2)
        pt_bank = banks("pt", 2)
        o_bank = banks("o", 1)[:, 0]
        w0_bank, w1_bank = w_banks[:, 0], w_banks[:, 1]

        (consts_made, qT_zeroed, w2_zeroed, attn_loaded, ffn_loaded, products_loaded, w0_filled, w0_freed, w1_filled, w1_freed, x_filled, x_freed, dve_step, high_made,
         low_made, split_made, tabs_made, squared, ss_made, a_made, pool_step, c_made, scaled, scores_filled, maxed,
         probs_made, pt_filled, pt_copied, pv_done, o_copied, h2_made) = (sem("b_" + n) for n in
         """consts_made qT_zeroed w2_zeroed attn_loaded ffn_loaded products_loaded w0_filled w0_freed w1_filled w1_freed x_filled x_freed dve_step high_made
         low_made split_made tabs_made squared ss_made a_made pool_step c_made scaled scores_filled maxed
         probs_made pt_filled pt_copied pv_done o_copied h2_made""".split())
        work_banks = (("w0", w0_bank), ("w1", w1_bank), ("x", x_bank))
        filled = dict(w0=w0_filled, w1=w1_filled, x=x_filled)
        freed = dict(w0=w0_freed, w1=w1_freed, x=x_freed)
        nothing = lambda *a, **k: None
        seq = lambda l, b: l * B + b
        chunk = lambda l, b, s: seq(l, b) * STEPS2 + s
        at_start = lambda l, b: isinstance(l, int) and isinstance(b, int) and l == b == 0
        ATTN_LOADS, FFN_LOADS, PRODUCT_LOADS = 4, 7, 3
        CONSTS_MADE = 18
        block = ctx.enter_context(nc.Block())

        def ds_u(b, rows, cols):
            return u[rows, bass.ds(b, 1), cols].rearrange("p a t -> p (a t)")

        LOW, UP = slice(0, DH), slice(DH, P)

        def window(k):
            return slice(2 * P + (1 - k) * WIN, 2 * P + (2 - k) * WIN)

        @block.sync
        def _(sp):
            one = lambda a, l: a[bass.ds(l, 1)]

            def load(sem, count, loads):
                assert len(loads) == count
                for dst, src in loads:
                    sp.dma_start(dst, src).then_inc(sem, 16)

            def load_attn(l, b, slot, at):
                if not at_start(l, b):
                    sp.wait_ge(w0_freed, at["w0"])
                    sp.wait_ge(w1_freed, at["w1"])
                load(attn_loaded, ATTN_LOADS, [
                    (tab, tab2), (w_raw, one(Wqkv, l).rearrange("a p n -> (a p) n")),
                    (scales[:, 0, :], one(q_scale, l).to_broadcast([P, DH])),
                    (scales[:, 1, :], one(k_scale, l).to_broadcast([P, DH]))])

            def load_ffn(l, b, slot, at):
                if not at_start(l, b):
                    sp.wait_ge(x_freed, at["x"])
                loads = [(b2r, one(B2, l)),
                         (g_col[:], one(ln_g, l).rearrange("a (p n) -> (a p) n", n=1)),
                         (b_col[:], one(ln_b, l).rearrange("a (p n) -> (a p) n", n=1))]
                for half in range(2):
                    loads += [(w1[:, half, 0:HID], one(W1, l)[:, :, half * HID:(half + 1) * HID].rearrange("a p n -> (a p) n")),
                              (b1r[:, half, 0:HID], one(B1, l)[:, half * HID:(half + 1) * HID])]
                load(ffn_loaded, FFN_LOADS, loads)

            def load_products(l, b, slot, at):
                if at_start(l, b):
                    sp.wait_ge(w2_zeroed, 1)
                else:
                    sp.wait_ge(x_freed, at["x"])
                load(products_loaded, PRODUCT_LOADS, [
                    (wo[:], one(Wo, l).rearrange("a (c p) n -> p (a c) n", p=P)),
                    (w2[0:HREST, HC - 1, :], one(W2, l)[:, (HC - 1) * P:HID, :].rearrange("a p n -> (a p) n")),
                    (w2[:, 0:HC - 1, :], one(W2, l)[:, 0:(HC - 1) * P, :].rearrange("a (c p) n -> p (a c) n", p=P))])

            Walk(sp, nothing, nothing, nothing, dict(load_attn=load_attn, load_ffn=load_ffn, load_products=load_products),
                 sequences=False).run()

        @block.gpsimd
        def _(pool):
            pool.memset(w2[:], 0.0).then_inc(w2_zeroed, 1)
            zero = [center[:], mask_q[:], sel_f[:], probs[:], rpack[:], h_high[:].bitcast(F32),
                    h_low[:].bitcast(F32), h2[:], hid[:]]
            for a in zero:
                pool.memset(a, 0.0).then_inc(consts_made, 1)
            pool.memset(ones[:], 1.0).then_inc(consts_made, 1)
            n = len(zero) + 1
            pool.wait_ge(consts_made, n)
            select = lambda a, op, fill, base, pattern, mult: pool.affine_select(
                out=a, in_=a, compare_op=op, fill=fill, base=base, pattern=pattern, channel_multiplier=mult).then_inc(consts_made, 1)
            select(center[:], ALU.not_equal, 1.0, 0, [[-1, D]], 1)
            for half in range(2):
                select(sel_f[:, half * HEADS:(half + 1) * HEADS, :], ALU.not_equal, 1.0, -half * HEADS, [[-1, HEADS], [0, DH]], 1)
            select(mask_q[:], ALU.is_ge, MASKED, 0, [[0, 2], [1, SPAN]], -1)
            pool.wait_ge(consts_made, n + 4)
            select(mask_q[:], ALU.is_ge, MASKED, WIN, [[0, 2], [-1, SPAN]], 1)
            pool.tensor_tensor(sel[:].rearrange("p c n -> p (c n)"), sel_f[:, 0:HEADS, :].rearrange("p h d -> p (h d)"),
                               sel_f[:, HEADS:2 * HEADS, :].rearrange("p h d -> p (h d)"), ALU.add).then_inc(consts_made, 1)
            pool.tensor_scalar(center[:], center[:], -1.0 / D, None, ALU.add).then_inc(consts_made, 1)
            pool.wait_ge(consts_made, n + 7)
            select(mask_q[:, 1, :], ALU.is_ge, MASKED, -WIN, [[1, SPAN]], 0)
            assert n + 8 == CONSTS_MADE, n + 8

            def project(l, b, slot, i, at):
                n = seq(l, b) * TT + i
                pool.wait_ge(w0_freed, at["w0"] + 1)
                pool.wait_ge(w1_freed, at["w1"] + 1)
                if not at_start(l, b) or i > 0:
                    pool.wait_ge(c_made, n)
                if i == 0 and isinstance(b, int) and b == 0:
                    pool.wait_ge(tabs_made, (l + 1) * 3)
                hd = lambda a, lo: a.rearrange("p x (h d) -> p x h d", d=DH)[:, :, :, lo:lo + DH // 2]
                table = lambda x, lo: tabs[:, i, 1, x, lo:lo + DH // 2].rearrange("p (a d) -> p a d", a=1).to_broadcast([P, HEADS, DH // 2])
                for x in range(2):
                    for lo in (0, DH // 2):
                        last = pool.tensor_tensor(part_b[:, x, :].rearrange("p (h d) -> p h d", d=DH)[:, :, lo:lo + DH // 2],
                                                  raw[:, i % 2, x, :].rearrange("p (h d) -> p h d", d=DH)[:, :, DH // 2 - lo:DH - lo],
                                                  table(x, lo), ALU.mult)
                last.then_inc(pool_step, 1)
                pool.wait_ge(pool_step, n + 1)
                pool.wait_ge(a_made, n + 1)
                pool.tensor_tensor(qk[:, i], qk[:, i], part_b[:], ALU.add).then_inc(c_made, 1)

            Walk(pool, nothing, nothing, nothing, dict(project=project)).run()

        @block.scalar
        def _(act):
            act.wait_ge(consts_made, CONSTS_MADE)

            def weights_attn(l, b, slot, at):
                act.wait_ge(attn_loaded, (l + 1) * ATTN_LOADS * 16)
                act.copy(w_high[:], w_raw).then_inc(split_made, 1)

            def weights_ffn(l, b, slot, at):
                act.wait_ge(w0_filled, at["w0"] + 1)
                act.copy(w1c[:, 0, 0:HID], w0_bank[:, 0:HID]).then_inc(w0_freed, 1)
                act.wait_ge(w1_filled, at["w1"] + 1)
                act.copy(w1c[:, 1, 0:HID], w1_bank[:, 0:HID]).then_inc(w1_freed, 1)

            def h(l, b, slot, at):
                act.copy(h_high[LOW, :], ds_u(b, LOW, slice(0, T))).then_inc(high_made, 1)
                act.copy(h_high[UP, 1:T], ds_u(b, UP, slice(0, T - 1))).then_inc(high_made, 1)

            def project(l, b, slot, i, at):
                n = seq(l, b) * TT + i
                act.wait_ge(x_filled, at["x"] + 1)
                act.copy(v[:, slot, i, :], x_bank).then_inc(x_freed, 1)
                act.wait_ge(w0_filled, at["w0"] + 1)
                act.wait_ge(w1_filled, at["w1"] + 1)
                if not at_start(l, b) or i >= 1:
                    act.wait_ge(ss_made, n)
                if not at_start(l, b) or i >= 2:
                    act.wait_ge(a_made, n - 1)
                    act.wait_ge(c_made, n - 1)
                act.activation(sq[:], w_banks[:], ACT.Square).then_inc(squared, 1)
                act.copy(raw[:, i % 2, 0, :], w0_bank).then_inc(w0_freed, 1)
                act.copy(raw[:, i % 2, 1, :], w1_bank).then_inc(w1_freed, 1)

            def turn(l, b, slot, i, at):
                act.wait_ge(w1_filled, at["w1"] + 1)
                act.copy(kT[:, slot, :, i * P:(i + 1) * P],
                         w1_bank.rearrange("p (c t) -> p c t", c=PAIRS)).then_inc(w1_freed, 1)

            def scores(l, b, slot, s, at):
                h, c = divmod(s, 2)
                act.wait_ge(maxed, chunk(l, b, s) + 1)
                for k in range(2):
                    last = act.activation(probs[:, c, k, WIN:WIN + SPAN], s_bank[:, c, k * SPAN:(k + 1) * SPAN], ACT.Exp,
                                          bias=neg_max[:, slot, h, 2 * c + k:2 * c + k + 1],
                                          accum_out=dens[:, slot, h, 2 * c + k:2 * c + k + 1])
                last.then_inc(probs_made, 1)

            def turn_probs(l, b, slot, s):
                c, n = s % 2, chunk(l, b, s)
                act.wait_ge(pt_filled, n + 1)
                if not at_start(l, b) or s >= 2:
                    act.wait_ge(pv_done, n - 1)
                w = 2 * P + (1 + c) * WIN
                act.copy(pT[:, c, 0:w], pt_bank[:, c, 0:w]).then_inc(pt_copied, 1)

            def pv(l, b, slot, s):
                if s % 4 == 3:
                    act.wait_ge(pv_done, chunk(l, b, s) + 1)
                    act.copy(o_raw[:, s // 4, :], o_bank).then_inc(o_copied, 1)

            def den(l, b, slot, at):
                act.wait_ge(x_filled, at["x"] + 1)
                act.copy(rT[:], x_bank).then_inc(x_freed, 1)

            def shift(l, b, slot, at):
                act.wait_ge(x_freed, at["x"])
                act.copy(h2[LOW, :], x2[LOW, :])
                act.copy(h2[UP, 1:T], x2[UP, 0:T - 1]).then_inc(h2_made, 1)

            def gates(l, b, slot, at):
                for c, (name, bank) in enumerate(work_banks):
                    act.wait_ge(filled[name], at[name] + 1)
                    r = slice(0, P if c < HC - 1 else HREST)
                    act.activation(hid[r, c, :], bank[r, :], ACT.Gelu, bias=bias[r, HC + c:HC + c + 1]).then_inc(freed[name], 1)

            Walk(act, scores, turn_probs, pv, dict(weights_attn=weights_attn, weights_ffn=weights_ffn, h=h, project=project, turn=turn, den=den,
                                                   shift=shift, gates=gates), copies_first=True).run()

        @block.vector
        def _(dve):
            dve.memset(qT[:], 0.0).then_inc(qT_zeroed, 1)
            dve.wait_ge(qT_zeroed, 1)
            dve.wait_ge(consts_made, CONSTS_MADE)

            class Steps:
                def __init__(self, at):
                    self.n = at["dve"]

                def __call__(self, instruction):
                    instruction.then_inc(dve_step, 1)
                    self.n = self.n + 1
                    dve.wait_ge(dve_step, self.n)

            def weights_attn(l, b, slot, at):
                dve.wait_ge(attn_loaded, (l + 1) * ATTN_LOADS * 16)
                dve.wait_ge(split_made, l * 2 + 1)
                dve.tensor_tensor(w_low[:], w_raw, w_high[:].bitcast(F32), ALU.subtract).then_inc(split_made, 1)
                for i in range(TT):
                    last = dve.tensor_tensor(tabs[:, i, 0], tab[:, i, 0], scales[:], ALU.mult)
                last.then_inc(tabs_made, 1)
                for lo in (0, DH // 2):
                    for i in range(TT):
                        last = dve.tensor_tensor(tabs[:, i, 1, :, lo:lo + DH // 2], tab[:, i, 1, :, lo:lo + DH // 2],
                                                 scales[:, :, DH // 2 - lo:DH - lo], ALU.mult)
                    last.then_inc(tabs_made, 1)
                dve.wait_ge(tabs_made, (l + 1) * 3)

            def weights_ffn(l, b, slot, at):
                step = Steps(at)
                dve.wait_ge(x_filled, at["x"] + 1)
                for first in (0, HC):
                    dve.tensor_copy(bias[:, first:first + HC - 1], x_bank[:, first:first + HC - 1])
                    dve.tensor_copy(bias[0:HREST, first + HC - 1:first + HC], x_bank[0:HREST, first + HC - 1:first + HC])
                dve.tensor_copy(bias[:, 6:7], x_bank[:, 6:7]).then_inc(x_freed, 1)
                step(dve.tensor_scalar(w1[:, :, 0:HID], w1[:, :, 0:HID], g_col[:], None, ALU.mult))

            def low(l, b, slot, at):
                dve.wait_ge(high_made, seq(l, b) * 2 + 2)
                dve.tensor_tensor(h_low[LOW, :], ds_u(b, LOW, slice(0, T)), h_high[LOW, :].bitcast(F32), ALU.subtract)
                dve.tensor_tensor(h_low[UP, 1:T], ds_u(b, UP, slice(0, T - 1)), h_high[UP, 1:T].bitcast(F32),
                                  ALU.subtract).then_inc(low_made, 1)

            def sums(l, b, slot, i, at):
                n = seq(l, b) * TT + i
                dve.wait_ge(squared, n + 1)
                dve.tensor_reduce(ss[:, i * 16:(i + 1) * 16], sq[:].rearrange("p x (h d) -> p (x h) d", d=DH),
                                  AX, ALU.add).then_inc(ss_made, 1)
                dve.wait_ge(w0_freed, at["w0"] + 1)
                dve.wait_ge(w1_freed, at["w1"] + 1)
                for x in range(2):
                    last = dve.tensor_tensor(qk[:, i, x, :].rearrange("p (h d) -> p h d", d=DH),
                                             raw[:, i % 2, x, :].rearrange("p (h d) -> p h d", d=DH),
                                             tabs[:, i, 0, x, :].rearrange("p (a d) -> p a d", a=1).to_broadcast([P, HEADS, DH]), ALU.mult)
                last.then_inc(a_made, 1)

            def rs_(l, b, slot, at):
                step = Steps(at)
                dve.wait_ge(ss_made, seq(l, b) * TT + TT)
                step(dve.tensor_scalar(ss[:], ss[:], 1e-24, None, ALU.max))
                rsqrt(dve, step, rs[:], ss[:], tmp[:])

            def scale(l, b, slot, i, at):
                n = seq(l, b) * TT + i
                dve.wait_ge(c_made, n + 1)
                a = qk[:, i].rearrange("p x (h d) -> p (x h) d", d=DH)
                dve.tensor_tensor(a, a, rs[:, i * 16:(i + 1) * 16].rearrange("p (h a) -> p h a", a=1).to_broadcast([P, 16, DH]),
                                  ALU.mult).then_inc(scaled, 1)

            def turn(l, b, slot, i, at):
                dve.wait_ge(w0_filled, at["w0"] + 1)
                for a, r in enumerate((LOW, UP)):
                    last = dve.tensor_copy(qT[r, slot, :, a, i * P:(i + 1) * P], w0_bank[r, :].rearrange("p (c t) -> p c t", c=PAIRS))
                last.then_inc(w0_freed, 1)

            def scores(l, b, slot, s, at):
                h, c = divmod(s, 2)
                dve.wait_ge(scores_filled, chunk(l, b, s) + 1)
                dve.tensor_reduce(neg_max[:, slot, h, 2 * c:2 * c + 2], s_bank[:, c, 0:2 * SPAN].rearrange("p (i k) -> p i k", i=2),
                                  AX, ALU.max, negate=True).then_inc(maxed, 1)

            def recip(l, b, slot, at):
                step = Steps(at)
                dve.wait_ge(probs_made, chunk(l, b, STEPS2))
                step(dve.reciprocal(rden[:], dens[:, slot]))
                high = rpack[:, :, 0:HEADS].rearrange("p i h -> p h i")
                step(dve.tensor_copy(high.bitcast(F32R), rden[:]))
                step(dve.tensor_tensor(rpack[:, :, HEADS:2 * HEADS].rearrange("p i h -> p h i"), rden[:], high, ALU.subtract))

            def normed(p, l, b, at, bank, name):
                dve.wait_ge(o_copied, seq(l, b) * PAIRS + p + 1)
                dve.wait_ge(filled[name], at[name] + 1)
                dve.tensor_tensor(oT[:, p, :], o_raw[:, p, :], bank, ALU.mult).then_inc(freed[name], 1)

            def spread(l, b, slot, at):
                for p, (name, bank) in enumerate(work_banks):
                    normed(p, l, b, at, bank, name)

            def spread_last(l, b, slot, at):
                normed(PAIRS - 1, l, b, at, x_bank, "x")

            def out(l, b, slot, at):
                dve.wait_ge(x_filled, at["x"] + 1)
                dve.tensor_tensor(x2[:], ds_u(b, slice(0, P), slice(0, T)), x_bank, ALU.add).then_inc(x_freed, 1)

            def stat(l, b, slot, at):
                step = Steps(at)
                dve.wait_ge(x_filled, at["x"] + 1)
                for i in range(TT):
                    last = dve.bn_stats(stats[:, i, :], x_bank[:, i * P:(i + 1) * P])
                last.then_inc(x_freed, 1)
                dve.wait_ge(x_freed, at["x"] + 1)
                dve.memset(pause[:], 0.0)
                for i in range(TT):
                    last = dve.bn_aggr(mv[:, i, :], stats[:, i, :])
                step(last)
                step(dve.tensor_scalar(var[:], mv[:, :, 1], EPS, None, ALU.add))
                rsqrt(dve, step, rstd[:], var[:], tmp4[:])

            def rstd_(l, b, slot, at):
                dve.wait_ge(x_filled, at["x"] + 1)
                dve.wait_ge(h2_made, seq(l, b) + 1)
                dve.tensor_tensor(h2[:], h2[:], x_bank, ALU.mult).then_inc(x_freed, 1)

            def values(l, b, slot, at):
                for c, (name, bank) in enumerate(work_banks):
                    dve.wait_ge(filled[name], at[name] + 1)
                    r = slice(0, P if c < HC - 1 else HREST)
                    dve.scalar_tensor_tensor(hid[r, c, :], bank[r, :], bias[r, c:c + 1], hid[r, c, :], ALU.add,
                                             ALU.mult).then_inc(freed[name], 1)

            def down(l, b, slot, at):
                dve.wait_ge(x_filled, at["x"] + 1)
                dve.scalar_tensor_tensor(ds_u(b, slice(0, P), slice(0, T)), x_bank, bias[:, 6:7], x2[:], ALU.add,
                                         ALU.add).then_inc(x_freed, 1)

            Walk(dve, scores, nothing, nothing, dict(weights_attn=weights_attn, weights_ffn=weights_ffn, low=low, sums=sums, rs=rs_, scale=scale, turn=turn,
                 recip=recip, spread=spread, spread_last=spread_last, out=out, stat=stat, rstd=rstd_, values=values, down=down)).run()

        @block.tensor
        def _(pe):
            pe.wait_ge(consts_made, CONSTS_MADE)
            pe.wait_ge(qT_zeroed, 1)

            def weights_ffn(l, b, slot, at):
                pe.wait_ge(ffn_loaded, (l + 1) * FFN_LOADS * 16)
                pe.wait_ge(products_loaded, (l + 1) * PRODUCT_LOADS * 16)
                if not at_start(l, b):
                    for name in freed:
                        pe.wait_ge(freed[name], at[name])
                for half in range(2):
                    for c in range(HC):
                        r = P if c < HC - 1 else HREST
                        col = x_bank[0:r, half * HC + c:half * HC + c + 1]
                        pe.matmul(col, w1[:, half, c * P:c * P + r], b_col[:], start=True, stop=False)
                        pe.matmul(col, b1r[:, half, c * P:c * P + r], ones[0:1, 0:1], start=False, stop=True)
                pe.matmul(x_bank[:, 6:7], b2r, ones[0:1, 0:1], start=True, stop=True).then_inc(x_filled, 1)
                pe.wait_ge(dve_step, at["dve"] + 1)
                pe.matmul(w0_bank[:, 0:HID], center[:], w1[:, 0, 0:HID], start=True, stop=True).then_inc(w0_filled, 1)
                pe.matmul(w1_bank[:, 0:HID], center[:], w1[:, 1, 0:HID], start=True, stop=True).then_inc(w1_filled, 1)

            def project(l, b, slot, i, at):
                if i == 0:
                    pe.wait_ge(low_made, seq(l, b) + 1)
                if i == 0 and isinstance(b, int) and b == 0:
                    pe.wait_ge(split_made, l * 2 + 2)
                t = slice(i * P, (i + 1) * P)
                for o, name, bank in ((2, "x", x_bank), (0, "w0", w0_bank), (1, "w1", w1_bank)):
                    pe.wait_ge(freed[name], at[name])
                    cols = slice(o * INNER, (o + 1) * INNER)
                    pe.matmul(bank, h_high[:, t], w_high[:, cols], start=True, stop=False)
                    pe.matmul(bank, h_high[:, t], w_low[:, cols], start=False, stop=False)
                    pe.matmul(bank, h_low[:, t], w_high[:, cols], start=False, stop=True).then_inc(filled[name], 1)

            def turn(l, b, slot, i, at):
                pe.wait_ge(scaled, seq(l, b) * TT + i + 1)
                for x, (o, fl) in enumerate(((w0_bank, w0_filled), (w1_bank, w1_filled))):
                    pe.wait_ge((w0_freed, w1_freed)[x], at[("w0", "w1")[x]])
                    for p in range(PAIRS):
                        last = pe.transpose(o[:, p * P:(p + 1) * P], qk[:, i, x, p * P:(p + 1) * P], ident[:])
                    last.then_inc(fl, 1)

            def scores(l, b, slot, s, at):
                h, c = divmod(s, 2)
                if s == 0:
                    pe.wait_ge(w0_freed, at["w0"])
                    pe.wait_ge(w1_freed, at["w1"])
                if not at_start(l, b) or s >= 2:
                    pe.wait_ge(probs_made, chunk(l, b, s) - 1)
                for k in range(2):
                    i = 2 * c + k
                    out = s_bank[:, c, k * SPAN:(k + 1) * SPAN]
                    pe.matmul(out, ident_bf[:], mask_q[:, int(i == 0), :], start=True, stop=False)
                    before = WIN if i else 0
                    last = pe.matmul(out[:, WIN - before:SPAN], qT[:, slot, h // 2, h % 2, i * P:(i + 1) * P],
                                     kT[:, slot, h // 2, i * P - before:(i + 1) * P], start=False, stop=True)
                last.then_inc(scores_filled, 1)

            def turn_probs(l, b, slot, s):
                h, c = divmod(s, 2)
                n = chunk(l, b, s)
                pe.wait_ge(probs_made, n + 1)
                if not at_start(l, b) or s >= 2:
                    pe.wait_ge(pt_copied, n - 1)
                for k in range(2):
                    last = pe.transpose(pt_bank[:, c, k * P:(k + 1) * P], probs[:, c, k, P:2 * P], ident[:])
                    if c or k:
                        last = pe.transpose(pt_bank[:, c, window(k)], probs[0:WIN, c, k, 0:P], ident[0:WIN, 0:WIN])
                last.then_inc(pt_filled, 1)

            def pv(l, b, slot, s):
                h, c = divmod(s, 2)
                pe.wait_ge(pt_copied, chunk(l, b, s) + 1)
                if s % 4 == 0 and not (at_start(l, b) and s == 0):
                    pe.wait_ge(o_copied, seq(l, b) * PAIRS + s // 4)
                rows = (LOW, UP)[h % 2]
                for k in range(2):
                    i = 2 * c + k
                    vh = lambda tile: v[:, slot, tile, h * DH:(h + 1) * DH]
                    last = pe.matmul(o_bank[rows, i * P:(i + 1) * P], vh(i), pT[:, c, k * P:(k + 1) * P], start=True,
                                     stop=(i == 0), skip_group_check=True)
                    if i:
                        last = pe.matmul(o_bank[rows, i * P:i * P + WIN], vh(i - 1), pT[:, c, window(k)], start=False,
                                         stop=True, skip_group_check=True)
                last.then_inc(pv_done, 1)

            def den(l, b, slot, at):
                pe.wait_ge(dve_step, at["dve"])
                pe.wait_ge(x_freed, at["x"])
                for i in range(TT):
                    last = pe.transpose(x_bank[:, i * P:(i + 1) * P], rpack[:, i, :], ident[:])
                last.then_inc(x_filled, 1)

            def spread_pair(p, at, bank, name):
                pe.wait_ge(freed[name], at[name])
                pe.matmul(bank, sel[:, p, :], rT[:], start=True, stop=True).then_inc(filled[name], 1)

            def spread(l, b, slot, at):
                pe.wait_ge(x_freed, at["x"])
                for p, (name, bank) in enumerate(work_banks):
                    spread_pair(p, at, bank, name)

            def spread_last(l, b, slot, at):
                spread_pair(PAIRS - 1, at, x_bank, "x")

            def out(l, b, slot, at):
                pe.wait_ge(x_freed, at["x"])
                for p in range(PAIRS):
                    last = pe.matmul(x_bank, wo[:, p, :], oT[:, p, :], start=(p == 0), stop=(p == PAIRS - 1))
                last.then_inc(x_filled, 1)

            def stat(l, b, slot, at):
                pe.wait_ge(h2_made, seq(l, b) + 1)
                pe.wait_ge(x_freed, at["x"])
                for i in range(TT):
                    last = pe.transpose(x_bank[:, i * P:(i + 1) * P], h2[:, i * P:(i + 1) * P], ident[:])
                last.then_inc(x_filled, 1)

            def rstd_(l, b, slot, at):
                pe.wait_ge(dve_step, at["dve"])
                pe.wait_ge(x_freed, at["x"])
                for i in range(TT):
                    last = pe.transpose(x_bank[:, i * P:(i + 1) * P], rstd[:, i:i + 1].to_broadcast([P, P]), ident[:])
                last.then_inc(x_filled, 1)

            def up(half, at):
                for c, (name, bank) in enumerate(work_banks):
                    pe.wait_ge(freed[name], at[name])
                    r = P if c < HC - 1 else HREST
                    pe.matmul(bank[0:r, :], w1c[:, half, c * P:c * P + r], h2[:], start=True, stop=True).then_inc(filled[name], 1)

            def gates(l, b, slot, at):
                pe.wait_ge(x_freed, at["x"])
                up(1, at)

            def values(l, b, slot, at):
                up(0, at)

            def down(l, b, slot, at):
                pe.wait_ge(x_freed, at["x"])
                for c in range(HC):
                    last = pe.matmul(x_bank, w2[:, c, :], hid[:, c, :], start=(c == 0), stop=(c == HC - 1))
                last.then_inc(x_filled, 1)

            Walk(pe, scores, turn_probs, pv, dict(weights_ffn=weights_ffn, project=project, turn=turn, den=den,
                 spread=spread, spread_last=spread_last, out=out, stat=stat, rstd=rstd_, gates=gates, values=values, down=down)).run()


GROUP = 4


def last_norm(nc, sem, ident, u, x1_v, out_v):
    with ExitStack() as ctx:
        sb = lambda name, shape: ctx.enter_context(nc.sbuf_tensor("c_" + name, shape, F32))
        groups, tiles = B // GROUP, GROUP * TT
        uf = sb("uf", [D, 2, GROUP, T])
        x1 = sb("x1", [P, 2, GROUP, TT * D])
        y = sb("y", [P, 2, GROUP, TT * D])
        stats = sb("stats", [P, tiles, 6])
        mv = sb("mv", [P, tiles, 2])
        var, tmp = (sb(n, [P, tiles]) for n in ("var", "tmp"))
        rstd, shift = (sb(n, [P, 2, tiles]) for n in ("rstd", "shift"))
        pause = sb("pause", [P, 1])
        bank = ctx.enter_context(nc.psum_tensor("c_bank", [P, 2, GROUP, TT * D], F32))
        copied, turned, dve_step, normed, made = (sem("c_" + n) for n in "copied turned dve_step normed made".split())
        loaded, stored = ([sem(f"c_{n}_{slot}") for slot in range(2)] for n in ("loaded", "stored"))
        steps = 3 + 11 + 1
        block = ctx.enter_context(nc.Block())

        def in_turn(eng, one):
            one(0, 0, True, False)
            with eng.Fori(1, groups - 2, 2) as g:
                one(g, 1, False, False)
                one(g + 1, 0, False, False)
            one(groups - 1, 1, False, True)

        early = lambda g: isinstance(g, int) and g < 2
        of_group = lambda a, g: a[:, bass.ds(g * GROUP, GROUP)]

        @block.sync
        def _(sp):
            def load(g, slot):
                if not early(g):
                    sp.wait_ge(made, g - 1)
                sp.dma_start(x1[:, slot].rearrange("p s (i d) -> p s i d", i=TT), of_group(x1_v, g)).then_inc(loaded[slot], 16)

            def one(g, slot, first, last):
                if not last:
                    load(g + 1, 1 - slot)
                sp.wait_ge(made, g + 1)
                sp.dma_start(of_group(out_v, g), y[:, slot].rearrange("p s (i d) -> p s i d", i=TT)).then_inc(stored[slot], 16)
            load(0, 0)
            in_turn(sp, one)
            for slot in range(2):
                sp.wait_ge(stored[slot], 16 * groups // 2)

        @block.scalar
        def _(act):
            def copy(g, slot):
                if not early(g):
                    act.wait_ge(turned, g - 1)
                act.copy(uf[:, slot], of_group(u, g)).then_inc(copied, 1)

            def one(g, slot, first, last):
                if not last:
                    copy(g + 1, 1 - slot)
                act.wait_ge(dve_step, (g + 1) * steps)
                if not early(g):
                    act.wait_ge(stored[slot], (g - slot) * 8)
                for n in range(tiles):
                    at = slice(n % TT * D, (n % TT + 1) * D)
                    last_one = act.activation(y[:, slot, n // TT, at], bank[:, slot, n // TT, at], ACT.Identity,
                                              scale=rstd[:, slot, n:n + 1], bias=shift[:, slot, n:n + 1])
                last_one.then_inc(normed, 1)
            copy(0, 0)
            in_turn(act, one)

        @block.gpsimd
        def _(pool):
            def one(g, slot, first, last):
                pool.wait_ge(loaded[slot], (g - slot) * 8 + 16)
                pool.wait_ge(normed, g + 1)
                pool.tensor_tensor(y[:, slot], y[:, slot], x1[:, slot], ALU.add).then_inc(made, 1)
            in_turn(pool, one)

        @block.tensor
        def _(pe):
            def one(g, slot, first, last):
                pe.wait_ge(copied, g + 1)
                if not early(g):
                    pe.wait_ge(normed, g - 1)
                for n in range(tiles):
                    t = slice(n % TT * P, (n % TT + 1) * P)
                    last_one = pe.transpose(bank[:, slot, n // TT, t], uf[:, slot, n // TT, t], ident[:])
                last_one.then_inc(turned, 1)
            in_turn(pe, one)

        @block.vector
        def _(dve):
            def one(g, slot, first, last):
                count = [g * steps]

                def step(instruction):
                    instruction.then_inc(dve_step, 1)
                    count[0] = count[0] + 1
                    dve.wait_ge(dve_step, count[0])

                dve.wait_ge(turned, g + 1)
                for n in range(tiles):
                    last_one = dve.bn_stats(stats[:, n, :], bank[:, slot, n // TT, n % TT * D:(n % TT + 1) * D])
                step(last_one)
                dve.memset(pause[:], 0.0)
                for n in range(tiles):
                    last_one = dve.bn_aggr(mv[:, n, :], stats[:, n, :])
                step(last_one)
                step(dve.tensor_scalar(var[:], mv[:, :, 1], EPS, None, ALU.add))
                rsqrt(dve, step, rstd[:, slot], var[:], tmp[:])
                step(dve.scalar_tensor_tensor(shift[:, slot], mv[:, :, 0], -1.0, rstd[:, slot], ALU.mult, ALU.mult))
            in_turn(dve, one)




_INS = ['L0_attn_x', 'L0_attn_Wq', 'L0_attn_bq', 'L0_attn_Wk', 'L0_attn_bk', 'L0_attn_Wv', 'L0_attn_bv', 'L0_attn_Wo', 'L0_attn_bo',
        'L0_ffn_wqkv', 'L0_ffn_q_scale', 'L0_ffn_k_scale', 'L0_ffn_wo', 'L0_ffn_ln_g', 'L0_ffn_ln_b', 'L0_ffn_w1', 'L0_ffn_b1',
        'L0_ffn_w2', 'L0_ffn_b2']


def kernel(**inputs):
    import numpy as _np
    import concourse.bacc as _bacc
    from concourse import mybir as _mybir
    from concourse.bass_utils import run_bass_kernel_spmd as _run

    nc = _bacc.Bacc("TRN2", target_bir_lowering=False, num_devices=1)
    arrays = {f"in_{n}": _np.ascontiguousarray(inputs[n]) for n in _INS}
    arrays["cos1"], arrays["sin1"] = rope_tables()
    arrays["tab2"] = xpos_tables()
    args = [nc.dram_tensor(n, a.shape, _mybir.dt.from_np(a.dtype), kind="ExternalInput").ap() for n, a in arrays.items()]
    args.append(nc.dram_tensor("out_0", (B, T, D), _mybir.dt.float32, kind="ExternalOutput").ap())
    sandwich_kernel(nc, *args)
    r = _run(nc, [arrays], core_ids=[0])
    return r.results[0]["out_0"]
```
